# Optimizing a Trainium2 kernel written in Bass

```python
import numpy as np
import jax
import jax.numpy as jnp

def _softmax(x, axis=-1):
    return jax.nn.softmax(x, axis=axis)

def _gelu(x):
    return jax.nn.gelu(x, approximate=True)

def _silu(x):
    return jax.nn.silu(x)

def _sigmoid(x):
    return jax.nn.sigmoid(x)

def _layernorm(x, axis=-1, eps=1e-05):
    m = jnp.mean(x, axis=axis, keepdims=True)
    v = jnp.var(x, axis=axis, keepdims=True)
    return (x - m) / jnp.sqrt(v + eps)

def _scatter_add(tgt, idx, src, axis=0):
    return tgt.at[idx].add(src)

def _segment_sum(src, seg, n):
    return jax.ops.segment_sum(src, seg, n)
kernel_name = 'mk_decoder_preln_d1_seqx_r4_f0cea7'

def setup_inputs(seed: int=0):
    np.random.seed(seed)
    _w = jnp.asarray

    def _rec_inputs():
        import jax
        import jax.numpy as jnp
        _rk = jax.random.key(seed)
        x = -0.000125 + 0.9999 * jax.random.normal(jax.random.fold_in(_rk, 1), (4, 1024, 256), jnp.float32)
        _lenS = 1024 - jax.random.randint(jax.random.fold_in(_rk, 7), (4,), 0, max(1, 1024 // 4) + 1, jnp.int32)
        _lenS2 = 77 - jax.random.randint(jax.random.fold_in(_rk, 8), (4,), 0, max(1, 77 // 4) + 1, jnp.int32)
        _ctx_768P = jax.random.normal(jax.random.fold_in(_rk, 11), (4, 16, 192), jnp.float32)
        _ctx_768c = jax.random.dirichlet(jax.random.fold_in(_rk, 511), 0.3 * jnp.ones((16,), jnp.float32), (4, 77))
        _ctx_768t = jnp.einsum('bsk,bkd->bsd', _ctx_768c, _ctx_768P)
        _ctx_768t = _ctx_768t * jax.lax.rsqrt(jnp.mean(jnp.square(_ctx_768t)) + 1e-12) * 0.953939
        ctx_768 = 0.00272024 + 0.999456 * (_ctx_768t + 0.3 * jax.random.normal(jax.random.fold_in(_rk, 611), (4, 77, 192), jnp.float32))
        return (x, ctx_768)
    x, ctx_768 = _rec_inputs()

    def _L0_attn_setup():
        import jax, jax.numpy as jnp
        import numpy as np
        B, T, D_MODEL = (2, 128, 256)
        D_INNER, D_HEAD, D_CONV = (512, 64, 4)
        N_HEADS, D_STATE = (32, 32)
        DT_MIN, DT_MAX, K_MAX, EPS = (0.0001, 0.1, 0.5, 1e-08)

        def _forward(x, W_in, dw_weight, dw_bias, W_bc, W_out, skip, A_log, dt_bias):
            Bsz, Tlen, D = x.shape
            DI, K = dw_weight.shape
            H, N = A_log.shape
            DH = DI // H
            proj = jnp.einsum('btd,od->bto', x, W_in)
            gate = proj[..., :DI]
            value_raw = proj[..., DI:2 * DI]
            params = proj[..., 2 * DI:].reshape(Bsz, Tlen, H, 2)
            xp = jnp.pad(value_raw, ((0, 0), (K - 1, 0), (0, 0)))
            conv = dw_bias + sum((xp[:, k:k + Tlen, :] * dw_weight[:, k] for k in range(K)))
            value = jax.nn.silu(conv)
            dt = jnp.clip(jax.nn.softplus(params[..., 0] + dt_bias), DT_MIN, DT_MAX)
            kd = K_MAX * jax.nn.sigmoid(params[..., 1])
            A = jnp.exp(A_log)
            bc = jnp.einsum('bti,oi->bto', value, W_bc).reshape(Bsz, Tlen, H, 4, N)
            bc = bc / (jnp.sqrt(jnp.sum(bc * bc, axis=-1, keepdims=True)) + EPS)
            Bz, Bx, Cz, Cx = (bc[..., 0, :], bc[..., 1, :], bc[..., 2, :], bc[..., 3, :])
            u = value.reshape(Bsz, Tlen, H, DH)

            def step(carry, inp):
                z, s = carry
                u_t, dt_t, k_t, Bz_t, Bx_t, Cz_t, Cx_t = inp
                dtE = dt_t[:, :, None, None]
                S = 1.0 / (1.0 + dt_t[..., None] * k_t[..., None] + (dt_t * dt_t)[..., None] * A)
                z = S[..., None] * (z - dtE * A[None, :, :, None] * s + dtE * (Bz_t[..., None] * u_t[:, :, None, :]))
                s = s + dtE * z + dtE * (Bx_t[..., None] * u_t[:, :, None, :])
                y = jnp.einsum('bhn,bhnd->bhd', Cz_t, z) + jnp.einsum('bhn,bhnd->bhd', Cx_t, s)
                return ((z, s), y)
            tm = lambda a: jnp.moveaxis(a, 1, 0)
            init = (jnp.zeros((Bsz, H, N, DH), x.dtype), jnp.zeros((Bsz, H, N, DH), x.dtype))
            _, ys = jax.lax.scan(step, init, (tm(u), tm(dt), tm(kd), tm(Bz), tm(Bx), tm(Cz), tm(Cx)))
            y = jnp.moveaxis(ys, 0, 1).reshape(Bsz, Tlen, DI)
            y = (y + skip * value) * jax.nn.silu(gate)
            return jnp.einsum('bti,oi->bto', y, W_out)
        key = jax.random.key(seed)
        ks = jax.random.split(key, 8)
        n = lambda k, sh, s=1.0: jax.random.normal(k, sh, jnp.float32) * s
        return {'x': n(ks[0], (B, T, D_MODEL)), 'W_in': n(ks[1], (2 * D_INNER + N_HEADS * 2, D_MODEL), D_MODEL ** (-0.5)), 'dw_weight': n(ks[2], (D_INNER, D_CONV), D_CONV ** (-0.5)), 'dw_bias': n(ks[3], (D_INNER,), 0.1), 'W_bc': n(ks[4], (N_HEADS * 4 * D_STATE, D_INNER), D_INNER ** (-0.5)), 'W_out': n(ks[5], (D_MODEL, D_INNER), D_INNER ** (-0.5)), 'skip': jnp.ones((D_INNER,), jnp.float32), 'A_log': n(ks[6], (N_HEADS, D_STATE), 0.5), 'dt_bias': n(ks[7], (N_HEADS,), 0.5)}
    _L0_attn_all = _L0_attn_setup()
    _L0_attn_in = {k: v for k, v in _L0_attn_all.items() if k in ('W_in', 'dw_weight', 'dw_bias', 'W_bc', 'W_out', 'skip', 'A_log', 'dt_bias')}
    del _L0_attn_all

    def _L0_xattn_setup():
        import jax, jax.numpy as jnp
        import numpy as np
        N_HEADS = 16
        DIM_EMBED = 256
        DIM_CROSS = 192
        DIM_HEAD = DIM_EMBED // N_HEADS
        key = jax.random.key(seed)
        ks = jax.random.split(key, 10)
        B, Sq, Sk = (8, 1024, 77)
        s_e = 1.0 / np.sqrt(DIM_EMBED)
        s_c = 1.0 / np.sqrt(DIM_CROSS)
        return {'x': jax.random.normal(ks[0], (B, Sq, DIM_EMBED), jnp.float32), 'y': jax.random.normal(ks[1], (B, Sk, DIM_CROSS), jnp.float32), 'wq': jax.random.normal(ks[2], (DIM_EMBED, DIM_EMBED), jnp.float32) * s_e, 'bq': jax.random.normal(ks[3], (DIM_EMBED,), jnp.float32) * 0.01, 'wk': jax.random.normal(ks[4], (DIM_CROSS, DIM_EMBED), jnp.float32) * s_c, 'bk': jax.random.normal(ks[5], (DIM_EMBED,), jnp.float32) * 0.01, 'wv': jax.random.normal(ks[6], (DIM_CROSS, DIM_EMBED), jnp.float32) * s_c, 'bv': jax.random.normal(ks[7], (DIM_EMBED,), jnp.float32) * 0.01, 'wo': jax.random.normal(ks[8], (DIM_EMBED, DIM_EMBED), jnp.float32) * s_e, 'bo': jax.random.normal(ks[9], (DIM_EMBED,), jnp.float32) * 0.01}
    _L0_xattn_all = _L0_xattn_setup()
    _L0_xattn_in = {k: v for k, v in _L0_xattn_all.items() if k in ('wq', 'bq', 'wk', 'bk', 'wv', 'bv', 'wo', 'bo')}
    del _L0_xattn_all

    def _L0_ffn_setup():
        import jax, jax.numpy as jnp
        import numpy as np
        D_MODEL = 256
        D_FF = 1024
        NUM_M = 2
        E_ROUTER = 8 * NUM_M - 1
        D_FF_R = D_FF // NUM_M
        TOP_K = NUM_M * 2 - 1
        B, T = (2, 512)

        def _expert_stack(x, W1, b1, W2, b2):
            h = jax.nn.gelu(jnp.einsum('btd,edf->ebtf', x, W1) + b1[:, None, None, :], approximate=False)
            return jnp.einsum('ebtf,efd->ebtd', h, W2) + b2[:, None, None, :]
        key = jax.random.key(seed)
        ks = jax.random.split(key, 12)
        s = lambda fan_in: 1.0 / np.sqrt(fan_in)
        x = jax.random.normal(ks[0], (B, T, D_MODEL), dtype=jnp.float32)
        sW1 = jax.random.uniform(ks[1], (1, D_MODEL, D_FF), jnp.float32, -s(D_MODEL), s(D_MODEL))
        sb1 = jax.random.uniform(ks[2], (1, D_FF), jnp.float32, -s(D_MODEL), s(D_MODEL))
        sW2 = jax.random.uniform(ks[3], (1, D_FF, D_MODEL), jnp.float32, -s(D_FF), s(D_FF))
        sb2 = jax.random.uniform(ks[4], (1, D_MODEL), jnp.float32, -s(D_FF), s(D_FF))
        rW1 = jax.random.uniform(ks[5], (E_ROUTER, D_MODEL, D_FF_R), jnp.float32, -s(D_MODEL), s(D_MODEL))
        rb1 = jax.random.uniform(ks[6], (E_ROUTER, D_FF_R), jnp.float32, -s(D_MODEL), s(D_MODEL))
        rW2 = jax.random.uniform(ks[7], (E_ROUTER, D_FF_R, D_MODEL), jnp.float32, -s(D_FF_R), s(D_FF_R))
        rb2 = jax.random.uniform(ks[8], (E_ROUTER, D_MODEL), jnp.float32, -s(D_FF_R), s(D_FF_R))
        gW = jax.random.uniform(ks[9], (D_MODEL, E_ROUTER), jnp.float32, -s(D_MODEL), s(D_MODEL))
        gb = jax.random.uniform(ks[10], (E_ROUTER,), jnp.float32, -s(D_MODEL), s(D_MODEL))
        return {'x': x, 'sW1': sW1, 'sb1': sb1, 'sW2': sW2, 'sb2': sb2, 'rW1': rW1, 'rb1': rb1, 'rW2': rW2, 'rb2': rb2, 'gW': gW, 'gb': gb}
    _L0_ffn_all = _L0_ffn_setup()
    _L0_ffn_in = {k: v for k, v in _L0_ffn_all.items() if k in ('sW1', 'sb1', 'sW2', 'sb2', 'rW1', 'rb1', 'rW2', 'rb2', 'gW', 'gb')}
    del _L0_ffn_all
    return {'x': x, 'ctx_768': ctx_768, 'L0_attn_W_in': _L0_attn_in['W_in'], 'L0_attn_dw_weight': _L0_attn_in['dw_weight'], 'L0_attn_dw_bias': _L0_attn_in['dw_bias'], 'L0_attn_W_bc': _L0_attn_in['W_bc'], 'L0_attn_W_out': _L0_attn_in['W_out'], 'L0_attn_skip': _L0_attn_in['skip'], 'L0_attn_A_log': _L0_attn_in['A_log'], 'L0_attn_dt_bias': _L0_attn_in['dt_bias'], 'L0_xattn_wq': _L0_xattn_in['wq'], 'L0_xattn_bq': _L0_xattn_in['bq'], 'L0_xattn_wk': _L0_xattn_in['wk'], 'L0_xattn_bk': _L0_xattn_in['bk'], 'L0_xattn_wv': _L0_xattn_in['wv'], 'L0_xattn_bv': _L0_xattn_in['bv'], 'L0_xattn_wo': _L0_xattn_in['wo'], 'L0_xattn_bo': _L0_xattn_in['bo'], 'L0_ffn_sW1': _L0_ffn_in['sW1'], 'L0_ffn_sb1': _L0_ffn_in['sb1'], 'L0_ffn_sW2': _L0_ffn_in['sW2'], 'L0_ffn_sb2': _L0_ffn_in['sb2'], 'L0_ffn_rW1': _L0_ffn_in['rW1'], 'L0_ffn_rb1': _L0_ffn_in['rb1'], 'L0_ffn_rW2': _L0_ffn_in['rW2'], 'L0_ffn_rb2': _L0_ffn_in['rb2'], 'L0_ffn_gW': _L0_ffn_in['gW'], 'L0_ffn_gb': _L0_ffn_in['gb']}

def reference(x, ctx_768, L0_attn_W_in, L0_attn_dw_weight, L0_attn_dw_bias, L0_attn_W_bc, L0_attn_W_out, L0_attn_skip, L0_attn_A_log, L0_attn_dt_bias, L0_xattn_wq, L0_xattn_bq, L0_xattn_wk, L0_xattn_bk, L0_xattn_wv, L0_xattn_bv, L0_xattn_wo, L0_xattn_bo, L0_ffn_sW1, L0_ffn_sb1, L0_ffn_sW2, L0_ffn_sb2, L0_ffn_rW1, L0_ffn_rb1, L0_ffn_rW2, L0_ffn_rb2, L0_ffn_gW, L0_ffn_gb):
    import jax
    import jax.numpy as jnp

    def _L0_attn_ref(x, W_in, dw_weight, dw_bias, W_bc, W_out, skip, A_log, dt_bias):
        import jax, jax.numpy as jnp
        import numpy as np
        B, T, D_MODEL = (2, 128, 256)
        D_INNER, D_HEAD, D_CONV = (512, 64, 4)
        N_HEADS, D_STATE = (32, 32)
        DT_MIN, DT_MAX, K_MAX, EPS = (0.0001, 0.1, 0.5, 1e-08)

        def _forward(x, W_in, dw_weight, dw_bias, W_bc, W_out, skip, A_log, dt_bias):
            Bsz, Tlen, D = x.shape
            DI, K = dw_weight.shape
            H, N = A_log.shape
            DH = DI // H
            proj = jnp.einsum('btd,od->bto', x, W_in)
            gate = proj[..., :DI]
            value_raw = proj[..., DI:2 * DI]
            params = proj[..., 2 * DI:].reshape(Bsz, Tlen, H, 2)
            xp = jnp.pad(value_raw, ((0, 0), (K - 1, 0), (0, 0)))
            conv = dw_bias + sum((xp[:, k:k + Tlen, :] * dw_weight[:, k] for k in range(K)))
            value = jax.nn.silu(conv)
            dt = jnp.clip(jax.nn.softplus(params[..., 0] + dt_bias), DT_MIN, DT_MAX)
            kd = K_MAX * jax.nn.sigmoid(params[..., 1])
            A = jnp.exp(A_log)
            bc = jnp.einsum('bti,oi->bto', value, W_bc).reshape(Bsz, Tlen, H, 4, N)
            bc = bc / (jnp.sqrt(jnp.sum(bc * bc, axis=-1, keepdims=True)) + EPS)
            Bz, Bx, Cz, Cx = (bc[..., 0, :], bc[..., 1, :], bc[..., 2, :], bc[..., 3, :])
            u = value.reshape(Bsz, Tlen, H, DH)

            def step(carry, inp):
                z, s = carry
                u_t, dt_t, k_t, Bz_t, Bx_t, Cz_t, Cx_t = inp
                dtE = dt_t[:, :, None, None]
                S = 1.0 / (1.0 + dt_t[..., None] * k_t[..., None] + (dt_t * dt_t)[..., None] * A)
                z = S[..., None] * (z - dtE * A[None, :, :, None] * s + dtE * (Bz_t[..., None] * u_t[:, :, None, :]))
                s = s + dtE * z + dtE * (Bx_t[..., None] * u_t[:, :, None, :])
                y = jnp.einsum('bhn,bhnd->bhd', Cz_t, z) + jnp.einsum('bhn,bhnd->bhd', Cx_t, s)
                return ((z, s), y)
            tm = lambda a: jnp.moveaxis(a, 1, 0)
            init = (jnp.zeros((Bsz, H, N, DH), x.dtype), jnp.zeros((Bsz, H, N, DH), x.dtype))
            _, ys = jax.lax.scan(step, init, (tm(u), tm(dt), tm(kd), tm(Bz), tm(Bx), tm(Cz), tm(Cx)))
            y = jnp.moveaxis(ys, 0, 1).reshape(Bsz, Tlen, DI)
            y = (y + skip * value) * jax.nn.silu(gate)
            return jnp.einsum('bti,oi->bto', y, W_out)
        return _forward(x, W_in, dw_weight, dw_bias, W_bc, W_out, skip, A_log, dt_bias)

    def _L0_xattn_ref(x, y, wq, bq, wk, bk, wv, bv, wo, bo):
        import jax, jax.numpy as jnp
        import numpy as np
        N_HEADS = 16
        DIM_EMBED = 256
        DIM_CROSS = 192
        DIM_HEAD = DIM_EMBED // N_HEADS
        B, Sq, E = x.shape
        H, D = (N_HEADS, DIM_HEAD)
        q = (x @ wq + bq).reshape(B, Sq, H, D).transpose(0, 2, 1, 3)
        k = (y @ wk + bk).reshape(B, -1, H, D).transpose(0, 2, 1, 3)
        v = (y @ wv + bv).reshape(B, -1, H, D).transpose(0, 2, 1, 3)
        scores = jnp.einsum('bhqd,bhkd->bhqk', q, k) / jnp.sqrt(jnp.asarray(D, x.dtype))
        attn = jax.nn.softmax(scores, axis=-1)
        out = jnp.einsum('bhqk,bhkd->bhqd', attn, v)
        out = out.transpose(0, 2, 1, 3).reshape(B, Sq, E)
        return out @ wo + bo

    def _L0_ffn_ref(x, sW1, sb1, sW2, sb2, rW1, rb1, rW2, rb2, gW, gb):
        import jax, jax.numpy as jnp
        import numpy as np
        D_MODEL = 256
        D_FF = 1024
        NUM_M = 2
        E_ROUTER = 8 * NUM_M - 1
        D_FF_R = D_FF // NUM_M
        TOP_K = NUM_M * 2 - 1
        B, T = (2, 512)

        def _expert_stack(x, W1, b1, W2, b2):
            h = jax.nn.gelu(jnp.einsum('btd,edf->ebtf', x, W1) + b1[:, None, None, :], approximate=False)
            return jnp.einsum('ebtf,efd->ebtd', h, W2) + b2[:, None, None, :]
        shared_enc = _expert_stack(x, sW1, sb1, sW2, sb2).sum(0)
        weights = jax.nn.softmax(x @ gW + gb, axis=-1)
        topv, topi = jax.lax.top_k(weights, TOP_K)
        gated = (jax.nn.one_hot(topi, E_ROUTER, dtype=weights.dtype) * topv[..., None]).sum(axis=-2)
        router_out = _expert_stack(x, rW1, rb1, rW2, rb2)
        router_enc = jnp.einsum('ebtd,bte->btd', router_out, gated)
        return shared_enc + router_enc + x
    x = x + _L0_attn_ref(_layernorm(x, axis=-1), L0_attn_W_in, L0_attn_dw_weight, L0_attn_dw_bias, L0_attn_W_bc, L0_attn_W_out, L0_attn_skip, L0_attn_A_log, L0_attn_dt_bias)
    x = x + _L0_xattn_ref(_layernorm(x, axis=-1), ctx_768, L0_xattn_wq, L0_xattn_bq, L0_xattn_wk, L0_xattn_bk, L0_xattn_wv, L0_xattn_bv, L0_xattn_wo, L0_xattn_bo)
    x = x + _L0_ffn_ref(_layernorm(x, axis=-1), L0_ffn_sW1, L0_ffn_sb1, L0_ffn_sW2, L0_ffn_sb2, L0_ffn_rW1, L0_ffn_rb1, L0_ffn_rW2, L0_ffn_rb2, L0_ffn_gW, L0_ffn_gb)
    return x

_drawn_inputs = setup_inputs


def setup_inputs(seed=0):
    import zlib

    import numpy as np

    out = dict(_drawn_inputs(seed))
    spreads = {'L0_attn_skip': (1.0, 0.2)}
    factors = {'L0_attn_dt_bias': 8.0,
     'L0_xattn_bq': 8.0,
     'L0_xattn_bk': 8.0,
     'L0_xattn_bv': 7.001,
     'L0_xattn_bo': 6.605,
     'L0_ffn_sb1': 8.0,
     'L0_ffn_sb2': 7.063,
     'L0_ffn_rW1': 2.923,
     'L0_ffn_rb1': 8.0,
     'L0_ffn_rW2': 2.766,
     'L0_ffn_rb2': 8.0,
     'L0_ffn_gW': 3.006,
     'L0_ffn_gb': 8.0}
    for name, (base, spread) in spreads.items():
        noise = np.random.default_rng([zlib.crc32(name.encode()), seed]).standard_normal(out[name].shape)
        drawn = base * np.exp(spread * noise) if base else spread * noise
        out[name] = jnp.asarray(drawn.astype(out[name].dtype))
    for name, factor in factors.items():
        out[name] = (out[name] * factor).astype(out[name].dtype)
    return out
```

```python
from contextlib import ExitStack

import numpy as np

import concourse.bass as bass
from concourse import mybir

F32 = mybir.dt.float32
ALU = mybir.AluOpType
ACT = mybir.ActivationFunctionType
AX = mybir.AxisListType

P = 128
B, T, DM = 4, 1024, 256
NTOK = B * T
DI, H, N, DH = 512, 32, 32, 16
KCONV = 4
L = 64
CH = 4
UT = CH * L
NU = NTOK // UT
TT = UT // P
UPB = T // UT
G, J = 8, 4
LANES = G * CH
EPS_LN, EPS_BC = 1e-5, 1e-8
DT_MIN, DT_MAX, Y_MAX = 1e-4, 0.1, 0.106


class Signal:

    def __init__(self, sem, per):
        self.sem, self.per = sem, per

    def wait(self, eng, u, k):
        eng.wait_ge(self.sem, k if u is None else u * self.per + k)


def constants():
    c = {}
    c["ident"] = np.eye(P, dtype=np.float32)
    jn = np.arange(P) // N
    c["sel4"] = (jn[:, None] == np.arange(J)[None]).astype(np.float32)
    c["blockd"] = (jn[:, None] == (np.arange(J * DH) // DH)[None]).astype(np.float32)
    h = np.arange(64) % H
    c["selh"] = (h[:, None, None] == (np.arange(G)[:, None] * J + jn[None])[None]).astype(np.float32)
    c["causal"] = (np.arange(L)[None] >= (np.arange(P) % L)[:, None]).astype(np.float32)
    r = np.ones((P, 2 * CH * L), np.float32)
    r[:, ::L] = 0
    c["resetm"] = r
    c["contm"] = np.tile((np.arange(NU) % UPB != 0).astype(np.float32)[None], (P, 1))
    par = (np.arange(P) // 16) % 2
    c["parity"] = np.stack([par == 0, par == 1], 1).astype(np.float32)
    c["onesrow"] = np.ones((1, P), np.float32)
    return c


def ring_tiles():
    tiles = [("xT",), ("val", 0), ("val", 1), ("gate", 0), ("gate", 1), ("par",), ("vt", 0), ("vt", 1), ("pt",)]
    tiles += [("w", g) for g in range(G)] + [("D", i) for i in range(G // 2)] + [("Qe",)]
    for s in range(G + 2):
        if s < G:
            tiles.append(("bcB", s))
        if 1 <= s <= G:
            tiles.append(("FB", s - 1))
        if s >= 2:
            tiles += [("BT", s - 2), ("G", s - 2, 0), ("G", s - 2, 1)]
    for s in range(G + 1):
        if s < G:
            tiles.append(("bcC", s))
        if s >= 1:
            tiles.append(("FC", s - 1))
    tiles += [("yT", 0), ("yT", 1)]
    return tiles


RING = ring_tiles()
RIDX = {k: i for i, k in enumerate(RING)}
assert len(RING) % 2 == 0


def attention(nc, d, x, x1):
    with ExitStack() as ctx:
        def sb(name, shape):
            return ctx.enter_context(nc.sbuf_tensor(name, shape, F32))

        def ps(name, shape):
            return ctx.enter_context(nc.psum_tensor(name, shape, F32))

        def sem(name):
            return ctx.enter_context(nc.semaphore(name))

        ident = sb("ident", [P, P])
        sel4 = sb("sel4", [P, J])
        blockd = sb("blockd", [P, J * DH])
        seld = sb("seld", [64, G, P])
        causal = sb("causal", [P, L])
        resetm = sb("resetm", [P, 2 * CH * L])
        contm = sb("contm", [P, NU])
        win = sb("win", [P, 2, 2 * DI + 2 * H])
        wbc = sb("wbc", [P, 4, G, 4, P])
        wout = sb("wout", [P, 4, DM])
        convw = sb("convw", [P, 4, KCONV])
        convb = sb("convb", [P, 4])
        dtb = sb("dtb", [H, 1])
        arow = sb("arow", [2 * H, N])
        nega = sb("nega", [P, G])
        skipb = sb("skipb", [P, DI])
        hist = sb("hist", [P, 4, KCONV - 1])
        hst = sb("hst", [P, CH + 1, 2, G, DH])
        cmask = sb("cmask", [P, 1])
        xt = sb("xt", [P, TT, DM])
        mv = sb("mv", [P, TT, 2])
        bst = sb("bst", [P, TT, 6])
        std = sb("std", [P, TT])
        rstd = sb("rstd", [P, TT])
        valt = sb("valt", [P, 4, UT])
        vtok = sb("vtok", [P, TT, DI])
        sg = sb("sg", [P, TT, DI])
        ptok = sb("ptok", [P, 3, TT, H])
        phi = sb("phi", [P, L + 1, 2, 2, LANES])
        pinv = sb("pinv", [P, G, UT])
        qe = sb("qe", [P, LANES])
        em = sb("em", [P, 2, 2, LANES])
        pend = sb("pend", [P, 2, LANES])
        du = sb("du", [P, TT, DI])
        share = sb("share", [P, 11776])
        phi_flat = phi[:].rearrange("p t r k l -> p (t r k l)")

        def carve(mem, at, parts):
            out = []
            for rows, shape in parts:
                n = int(np.prod(shape))
                v = mem[0:rows, at:at + n]
                if len(shape) > 1:
                    names = "abcde"[:len(shape)]
                    v = v.rearrange(f"p ({' '.join(names)}) -> p {' '.join(names)}",
                                    **{k: s for k, s in zip(names, shape)})
                out.append(v)
                at += n
            assert at <= mem.shape[1], at
            return out

        (coef,) = carve(share[:], 0, [(P, (L, 2, LANES))])
        (xn, xnt, vraw, cv, lnd, lnr, p5, qb, dr, ey, th, yv, iq) = carve(phi_flat, 4 * LANES, [
            (P, (TT, DM)), (P, (2, UT)), (P, (4, UT + 3)), (P, (4, UT)), (P, (2, 2 * UT)),
            (P, (2, 2 * UT)), (H, (5, UT)), (H, (CH, L + 1)), (64, (UT,)), (H, (UT,)), (H, (UT,)), (H, (UT,)),
            (H, (UT,))])
        (bt, bcs, sq, fbs, m1, m2, ct, km, btt, hbd) = carve(share[:], 0, [
            (P, (G, 2, UT)), (P, (2, 2, UT)), (P, (2, 2, UT)), (P, (2, UT)), (P, (2, UT)), (P, (2, UT)),
            (P, (3, 2, UT)), (P, (2, J, TT, L)), (P, (2, TT, P)), (P, (2, CH, 2, J * DH))])
        at_bcs, at_m1, at_km = G * 2 * UT, G * 2 * UT + 10 * UT, G * 2 * UT + 20 * UT
        (ygt,) = carve(share[:], at_bcs, [(P, (TT, 4, P))])
        (x1s,) = carve(share[:], at_m1, [(P, (TT, DM))])
        (gs,) = carve(share[:], at_km, [(P, (CH, 2, G, DH))])
        (hu,) = carve(share[:], at_km + 4 * UT, [(P, (2, 2, G, DH))])
        tz = sb("tz", [P, 2, UT])
        nr = sb("nr", [P, 2, TT, 2, J])
        nre = sb("nre", [P, TT, 2, J])
        rn = sb("rn", [P, TT, 2, J])
        fc4 = sb("fc4", [P, TT, J])
        fct = sb("fct", [P, 2, TT, J, N])
        dus = sb("dus", [P, TT, J])
        rcz = sb("rcz", [P, G, TT, J])
        uu = sb("uu", [P, 2, 2, LANES])
        ht = sb("ht", [P, 2, G, DH])
        ysc = sb("ysc", [P, 2, TT, J * DH])
        ysk = sb("ysk", [P, TT, J * DH])
        epsln = sb("epsln", [P, 1])

        ring = ps("ring", [P, 2, 512])
        ssp_bank = ps("ssp", [P, 512])
        yp_bank = ps("yp", [P, 512])
        ssp = ssp_bank[:, 0:TT * 2 * J].rearrange("p (a v j) -> p a v j", a=TT, v=2)
        yp = yp_bank[:, 0:TT * J * DH].rearrange("p (a e) -> p a e", a=TT)
        kp = ps("kp", [P, 4, 512])

        w_loaded = sem("w_loaded")
        NW = 16
        exps_ready = sem("exps_ready")
        init_ready = sem("init_ready")
        x_in = Signal(sem("x_in"), 16)
        x_out = Signal(sem("x_out"), 16)
        ring_full = Signal(sem("ring_full"), len(RING))
        mv_ready = Signal(sem("mv_ready"), 1)
        std_ready = Signal(sem("std_ready"), 1)
        xn_ready = Signal(sem("xn_ready"), 1)
        xnt_ready = Signal(sem("xnt_ready"), 1)
        vraw_ready = Signal(sem("vraw_ready"), 2)
        gate_ready = Signal(sem("gate_ready"), 2)
        conv_ready = Signal(sem("conv_ready"), 1)
        valt_ready = Signal(sem("valt_ready"), 1)
        par_ready = Signal(sem("par_ready"), 1)
        vtok_ready = Signal(sem("vtok_ready"), 2)
        p5_ready = Signal(sem("p5_ready"), 1)
        ptok_ready = Signal(sem("ptok_ready"), 1)
        coef_ready = Signal(sem("coef_ready"), G)
        lnd_ready = Signal(sem("lnd_ready"), G // 2)
        lnr_ready = Signal(sem("lnr_ready"), G // 2)
        pinv_ready = Signal(sem("pinv_ready"), G // 2)
        qe_ready = Signal(sem("qe_ready"), 1)
        evolved = Signal(sem("evolved"), 1)
        em_ready = Signal(sem("em_ready"), 1)
        bcs_ready = Signal(sem("bcs_ready"), 2 * G)
        sq_ready = Signal(sem("sq_ready"), 2 * G)
        ss_ready = Signal(sem("ss_ready"), 2 * G)
        nr_ready = Signal(sem("nr_ready"), 2 * G)
        fct_ready = Signal(sem("fct_ready"), 2 * G)
        fbs_ready = Signal(sem("fbs_ready"), 2 * G)
        bt_ready = Signal(sem("bt_ready"), G)
        du_ready = Signal(sem("du_ready"), G)
        btt_ready = Signal(sem("btt_ready"), G)
        gs_ready = Signal(sem("gs_ready"), 2 * G)
        h_ready = Signal(sem("h_ready"), 4 * CH)
        hbd_ready = Signal(sem("hbd_ready"), G)
        ct_ready = Signal(sem("ct_ready"), G)
        k_ready = Signal(sem("k_ready"), G)
        km_ready = Signal(sem("km_ready"), G)
        y_ready = Signal(sem("y_ready"), G)
        ysc_ready = Signal(sem("ysc_ready"), G)
        yg_ready = Signal(sem("yg_ready"), 3 * G)
        ygt_ready = Signal(sem("ygt_ready"), TT)
        o_ready = Signal(sem("o_ready"), TT)
        x1_ready = Signal(sem("x1_ready"), 1)
        step = sem("dve_step")

        emptied = {("xT",): (xnt_ready, 1), ("par",): (par_ready, 1), ("pt",): (ptok_ready, 1), ("Qe",): (qe_ready, 1)}
        for i in range(2):
            emptied |= {("val", i): (vraw_ready, i + 1), ("gate", i): (gate_ready, i + 1),
                        ("vt", i): (vtok_ready, i + 1), ("yT", i): (ygt_ready, i + 1)}
        for g in range(G):
            emptied |= {("w", g): (coef_ready, g + 1), ("D", g): (lnd_ready, g + 1),
                        ("bcB", g): (sq_ready, g + 1), ("bcC", g): (sq_ready, G + g + 1),
                        ("FB", g): (fbs_ready, g + 1), ("FC", g): (fbs_ready, G + g + 1),
                        ("BT", g): (btt_ready, g + 1), ("G", g, 0): (gs_ready, 2 * g + 1),
                        ("G", g, 1): (gs_ready, 2 * g + 2)}

        xv = x.rearrange("(u a p) m -> u p a m", a=TT, p=P)
        x1v = x1.rearrange("(u a p) m -> u p a m", a=TT, p=P)

        def lead(v, k):
            return v.unsqueeze(1).broadcast_to([v.shape[0], k, *v.shape[1:]])

        def spread(v, k):
            n = len(v.shape)
            return v.unsqueeze(n).broadcast_to([*v.shape, k])

        block = ctx.enter_context(nc.Block())

        @block.sync
        def _(sp):
            for dst, src in (
                    (ident[:], d["ident"]), (sel4[:], d["sel4"]), (blockd[:], d["blockd"]),
                    (seld[:], d["selh"]), (causal[:], d["causal"]), (resetm[:], d["resetm"]),
                    (contm[:], d["contm"]), (win[:], d["W_in"].rearrange("(k p) o -> p k o", p=P)),
                    (wbc[:], d["W_bc"].rearrange("(k p) (g c o) -> p k g c o", p=P, g=G, c=4)),
                    (wout[:], d["W_out"].rearrange("(k p) o -> p k o", p=P)),
                    (convw[:], d["dw_weight"].rearrange("(k p) c -> p k c", p=P)),
                    (convb[:], d["conv_bias"]),
                    (dtb[:], d["dt_bias"].rearrange("(h a) -> h a", a=1)),
                    (nega[:], d["A_states"]),
                    (skipb[:], d["skip"].partition_broadcast(P)),
                    (arow[H:2 * H, :], d["A_log"])):
                sp.dma_start(dst, src).then_inc(w_loaded, 16)
            sp.sem_inc(x_out.sem, 16)
            sp.sem_inc(x1_ready.sem, 1)
            with sp.Fori(0, NU) as u:
                x1_ready.wait(sp, u, 1)
                sp.dma_start(xt[:], xv[u]).then_inc(x_in.sem, 16)
                x1_ready.wait(sp, u, 2)
                sp.dma_start(x1v[u], x1s[:]).then_inc(x_out.sem, 16)
            sp.wait_ge(x_out.sem, 16 * NU + 16)

        @block.tensor
        def _(pe):
            pe.wait_ge(w_loaded, 16 * NW)
            pe.wait_ge(init_ready, 3)
            with pe.Fori(0, NU) as u:
                def put(key):
                    i = RIDX[key]
                    if i >= 2:
                        sig, k = emptied[RING[i - 2]]
                        sig.wait(pe, u, k)
                    return ring[:, i % 2, :]

                def full(ins):
                    ins.then_inc(ring_full.sem, 1)

                xn_ready.wait(pe, u, 1)
                o = put(("xT",))
                for k in range(2):
                    for a in range(TT):
                        mm = pe.transpose(o[:, k * UT + a * P:k * UT + (a + 1) * P], xn[:, a, k * P:(k + 1) * P],
                                          ident[:])
                full(mm)
                xnt_ready.wait(pe, u, 1)
                for i in range(2):
                    o = put(("val", i))
                    for v in range(2):
                        for k in range(2):
                            c0 = DI + (2 * i + v) * P
                            mm = pe.matmul(o[:, v * UT:(v + 1) * UT], win[:, k, c0:c0 + P], xnt[:, k, :],
                                           start=(k == 0), stop=(k == 1))
                    full(mm)
                for a in range(TT):
                    o = put(("gate", a))
                    for k in range(2):
                        mm = pe.matmul(o, xnt[:, k, a * P:(a + 1) * P], win[:, k, 0:DI], start=(k == 0), stop=(k == 1))
                    full(mm)
                o = put(("par",))
                for v in range(2):
                    for k in range(2):
                        c0 = 2 * DI + v * H
                        mm = pe.matmul(o[0:H, v * UT:(v + 1) * UT], win[:, k, c0:c0 + H], xnt[:, k, :],
                                       start=(k == 0), stop=(k == 1))
                full(mm)
                valt_ready.wait(pe, u, 1)
                for a in range(TT):
                    o = put(("vt", a))
                    for k in range(4):
                        mm = pe.transpose(o[:, k * P:(k + 1) * P], valt[:, k, a * P:(a + 1) * P], ident[:])
                    full(mm)
                p5_ready.wait(pe, u, 1)
                o = put(("pt",))
                for q in range(3):
                    for a in range(TT):
                        c0 = (q * TT + a) * H
                        mm = pe.matmul(o[:, c0:c0 + H], p5[:, 2 + q, a * P:(a + 1) * P], ident[0:H, 0:H],
                                       start=True, stop=True)
                full(mm)
                ptok_ready.wait(pe, u, 1)
                for g in range(G):
                    o = put(("w", g))
                    for q in range(2):
                        mm = pe.matmul(o[:, q * UT:(q + 1) * UT], seld[0:H, g, :], p5[:, q, :], start=True, stop=True)
                    full(mm)
                for i in range(G // 2):
                    o = put(("D", i))
                    for v in range(2):
                        mm = pe.matmul(o[:, v * UT:(v + 1) * UT], seld[:, 2 * i + v, :], dr[:, :],
                                       start=True, stop=True)
                    full(mm)
                o = put(("Qe",))
                for g in range(G):
                    mm = pe.matmul(o[:, g * CH:(g + 1) * CH], seld[0:H, g, :], qb[:, :, L], start=True, stop=True)
                full(mm)

                def bc(name, g, first):
                    if name == "bcB" and g == 0:
                        evolved.wait(pe, u, 1)
                    o = put((name, g))
                    for v in range(2):
                        for k in range(4):
                            mm = pe.matmul(o[:, v * UT:(v + 1) * UT], wbc[:, k, g, first + v, :], valt[:, k, :],
                                           start=(k == 0), stop=(k == 3))
                    full(mm)

                def sums(n, g):
                    sq_ready.wait(pe, u, n + 1)
                    if n > 0:
                        nr_ready.wait(pe, u, n)
                    for a in range(TT):
                        for v in range(2):
                            mm = pe.matmul(ssp[:, a, v, :], sq[:, g % 2, v, a * P:(a + 1) * P], sel4[:],
                                           start=True, stop=True)
                    mm.then_inc(ss_ready.sem, 1)

                def factors(name, n, g):
                    fct_ready.wait(pe, u, n + 1)
                    o = put((name, g))
                    for a in range(TT):
                        mm = pe.transpose(o[:, a * P:(a + 1) * P], fct[:, g % 2, a].rearrange("p j n -> p (j n)"), ident[:])
                    full(mm)

                for s in range(G + 2):
                    if s < G:
                        bc("bcB", s, 0)
                    if 1 <= s <= G:
                        factors("FB", s - 1, s - 1)
                    if s >= 2:
                        g = s - 2
                        bt_ready.wait(pe, u, g + 1)
                        o = put(("BT", g))
                        for v in range(2):
                            for a in range(TT):
                                c0 = (v * TT + a) * P
                                mm = pe.transpose(o[:, c0:c0 + P], bt[:, g, v, a * P:(a + 1) * P], ident[:])
                        full(mm)
                        btt_ready.wait(pe, u, g + 1)
                        du_ready.wait(pe, u, g + 1)
                        for odd in range(2):
                            o = put(("G", g, odd))
                            r = slice(L * odd, L * odd + L)
                            for a in range(TT):
                                for v in range(2):
                                    c0 = (a * 2 + v) * J * DH
                                    mm = pe.matmul(o[:, c0:c0 + J * DH], btt[r, v, a, :],
                                                   du[r, a, g * J * DH:(g + 1) * J * DH], start=True, stop=True)
                            full(mm)
                    if s < G:
                        sums(s, s)
                for s in range(G + 3):
                    if s < G:
                        bc("bcC", s, 2)
                    if 1 <= s <= G:
                        factors("FC", G + s - 1, s - 1)
                    if 2 <= s <= G + 1:
                        g = s - 2
                        ct_ready.wait(pe, u, g + 1)
                        if g > 0:
                            km_ready.wait(pe, u, g)
                        for c in range(CH):
                            r0 = L * (c % 2)
                            for v in range(2):
                                for j in range(J):
                                    mm = pe.matmul(kp[r0:r0 + L, j, (c // 2) * L:(c // 2 + 1) * L],
                                                   bt[N * j:N * j + N, g, v, c * L:(c + 1) * L],
                                                   ct[N * j:N * j + N, g % 3, v, c * L:(c + 1) * L],
                                                   start=(v == 0), stop=(v == 1), skip_group_check=True)
                        mm.then_inc(k_ready.sem, 1)
                    if s < G:
                        sums(G + s, s)
                    if s >= 3:
                        g = s - 3
                        km_ready.wait(pe, u, g + 1)
                        hbd_ready.wait(pe, u, g + 1)
                        if g > 0:
                            ysc_ready.wait(pe, u, g)
                        for c in range(CH):
                            r0 = L * (c % 2)
                            o = yp[r0:r0 + L, c // 2, :]
                            for v in range(2):
                                pe.matmul(o, ct[:, g % 3, v, c * L:(c + 1) * L], hbd[:, g % 2, c, v, :],
                                          start=(v == 0), stop=False, skip_group_check=True)
                            for j in range(J):
                                q0 = (g * J + j) * DH
                                mm = pe.matmul(o[:, j * DH:(j + 1) * DH], km[r0:r0 + L, g % 2, j, c // 2, :],
                                               du[r0:r0 + L, c // 2, q0:q0 + DH],
                                               start=False, stop=(j == J - 1), skip_group_check=True)
                        mm.then_inc(y_ready.sem, 1)
                yg_ready.wait(pe, u, 3 * G)
                for a in range(TT):
                    o = put(("yT", a))
                    for k in range(4):
                        mm = pe.transpose(o[:, k * P:(k + 1) * P], sg[:, a, k * P:(k + 1) * P], ident[:])
                    full(mm)
                for a in range(TT):
                    ygt_ready.wait(pe, u, a + 1)
                    for k in range(4):
                        mm = pe.matmul(kp[:, a, 0:DM], ygt[:, a, k, :], wout[:, k, :], start=(k == 0), stop=(k == 3))
                    mm.then_inc(o_ready.sem, 1)

        @block.scalar
        def _(act):
            act.wait_ge(w_loaded, 16 * NW)
            nc.scalar.activation(nega[:], nega[:], ACT.Exp).then_inc(exps_ready, 1)
            nc.scalar.activation(arow[H:2 * H, :], arow[H:2 * H, :], ACT.Exp).then_inc(exps_ready, 1)
            act.wait_ge(init_ready, 3)
            with act.Fori(0, NU) as u:
                def take(key):
                    i = RIDX[key]
                    ring_full.wait(act, u, i + 1)
                    return ring[:, i % 2, :]

                mv_ready.wait(act, u, 1)
                nc.scalar.activation(std[:], mv[:, :, 1], ACT.Sqrt, bias=epsln[:, 0:1]).then_inc(std_ready.sem, 1)

                o = take(("xT",))
                nc.scalar.copy(xnt[:], o.rearrange("p (k t) -> p k t", k=2)).then_inc(xnt_ready.sem, 1)
                for i in range(2):
                    o = take(("val", i))
                    nc.scalar.copy(vraw[:, 2 * i:2 * i + 2, 3:], o.rearrange("p (k t) -> p k t", k=2)) \
                        .then_inc(vraw_ready.sem, 1)
                for a in range(TT):
                    o = take(("gate", a))
                    nc.scalar.activation(sg[:, a, :], o, ACT.Silu).then_inc(gate_ready.sem, 1)
                conv_ready.wait(act, u, 1)
                nc.scalar.activation(valt[:], cv[:], ACT.Silu).then_inc(valt_ready.sem, 1)
                o = take(("par",))
                nc.scalar.activation(ey[:], o[0:H, 0:UT], ACT.Exp, bias=dtb[:, 0:1])
                nc.scalar.activation(th[:], o[0:H, UT:2 * UT], ACT.Tanh, scale=0.5).then_inc(par_ready.sem, 1)
                for a in range(TT):
                    o = take(("vt", a))
                    nc.scalar.copy(vtok[:, a, :], o).then_inc(vtok_ready.sem, 1)
                o = take(("pt",))
                nc.scalar.copy(ptok[:], o[:, 0:3 * TT * H].rearrange("p (q a h) -> p q a h", q=3, a=TT)) \
                    .then_inc(ptok_ready.sem, 1)
                for g in range(G):
                    o = take(("w", g))
                    for q in range(2):
                        src = o[:, q * UT:(q + 1) * UT].rearrange("p (c t) -> p c t", c=CH)
                        dst = coef[:, :, q, g * CH:(g + 1) * CH].rearrange("p t c -> p c t")
                        if q == 0:
                            nc.scalar.activation(dst, src, ACT.Copy, scale=nega[:, g:g + 1])
                        else:
                            nc.scalar.copy(dst, src).then_inc(coef_ready.sem, 1)
                for i in range(G // 2 + 1):
                    if i < G // 2:
                        o = take(("D", i))
                        if i >= 2:
                            lnr_ready.wait(act, u, i - 1)
                        nc.scalar.activation(lnd[:, i % 2, :], o, ACT.Ln).then_inc(lnd_ready.sem, 1)
                    if i >= 1:
                        lnr_ready.wait(act, u, i)
                        nc.scalar.activation(pinv[:, 2 * i - 2:2 * i, :],
                                             lnr[:, (i - 1) % 2, :].rearrange("p (g t) -> p g t", g=2),
                                             ACT.Exp, scale=-1.0).then_inc(pinv_ready.sem, 1)
                o = take(("Qe",))
                nc.scalar.copy(qe[:], o[:, 0:LANES]).then_inc(qe_ready.sem, 1)

                def bc(name, n, g):
                    o = take((name, g)).rearrange("p (v t) -> p v t", v=2)
                    if n >= 2:
                        (bt_ready if n - 2 < G else ct_ready).wait(act, u, (n - 2) % G + 1)
                        ss_ready.wait(act, u, n - 1)
                    nc.scalar.copy(bcs[:, g % 2, :, :], o).then_inc(bcs_ready.sem, 1)
                    nc.scalar.activation(sq[:, g % 2, :, :], o, ACT.Square).then_inc(sq_ready.sem, 1)

                def factors(name, n, g):
                    o = take((name, g))
                    if n >= 2:
                        (bt_ready if n - 2 < G else ct_ready).wait(act, u, (n - 2) % G + 1)
                    nc.scalar.copy(fbs[:, g % 2, :], o[:, 0:UT]).then_inc(fbs_ready.sem, 1)

                def norms(n, g):
                    ss_ready.wait(act, u, n + 1)
                    if n >= 2:
                        fct_ready.wait(act, u, n - 1)
                    nc.scalar.activation(nr[:, g % 2], ssp[:], ACT.Sqrt).then_inc(nr_ready.sem, 1)

                for s in range(G + 2):
                    if s < G:
                        bc("bcB", s, s)
                    if 1 <= s <= G:
                        factors("FB", s - 1, s - 1)
                    if s >= 2:
                        g = s - 2
                        o = take(("BT", g))
                        nc.scalar.copy(btt[:], o.rearrange("p (v a m) -> p v a m", v=2, a=TT)) \
                            .then_inc(btt_ready.sem, 1)
                        for odd in range(2):
                            o = take(("G", g, odd))
                            for j in range(J):
                                r = slice(N * j, N * j + N)
                                src = o[r, 0:TT * 2 * J * DH].rearrange("p (a v e) -> p a v e", a=TT, v=2)
                                ins = nc.scalar.copy(gs[r, odd::2, :, g, :], src[:, :, :, DH * j:DH * (j + 1)])
                            ins.then_inc(gs_ready.sem, 1)
                    if s < G:
                        norms(s, s)
                for s in range(G + 1):
                    if s < G:
                        bc("bcC", G + s, s)
                    if s >= 1:
                        factors("FC", G + s - 1, s - 1)
                    if s < G:
                        norms(G + s, s)
                for a in range(TT):
                    o = take(("yT", a))
                    nc.scalar.copy(ygt[:, a], o.rearrange("p (k t) -> p k t", k=4)).then_inc(ygt_ready.sem, 1)

        @block.gpsimd
        def _(pool):
            nc.gpsimd.memset(hst[:, CH], 0.0).then_inc(init_ready, 1)
            with pool.Fori(0, NU) as u:
                em_ready.wait(pool, u, 1)
                gs_ready.wait(pool, u, 2 * G)
                n = 0
                for c in range(CH):
                    nc.gpsimd.tensor_tensor(ht[:], hst[:, c], gs[:, c], ALU.add).then_inc(h_ready.sem, 1)
                    n += 1
                    h_ready.wait(pool, u, n)
                    for r in range(2):
                        nc.gpsimd.tensor_tensor(
                            hu[:, r], ht[:], spread(em[:, r].rearrange("p k (g c) -> p k g c", g=G)[:, :, :, c], DH),
                            ALU.mult).then_inc(h_ready.sem, 1)
                        n += 1
                    h_ready.wait(pool, u, n)
                    nc.gpsimd.tensor_tensor(hst[:, c + 1], hu[:, :, 0], hu[:, :, 1], ALU.add).then_inc(h_ready.sem, 1)
                    n += 1
                    h_ready.wait(pool, u, n)
                assert n == h_ready.per
                vtok_ready.wait(pool, u, TT)
                gate_ready.wait(pool, u, TT)

                def expand(g):
                    if g >= 2:
                        y_ready.wait(pool, u, g - 1)
                    hv = hst[:, 0:CH, :, g, :].rearrange("p c v e -> p (c v) e")
                    nc.gpsimd.tensor_tensor(
                        hbd[:, g % 2].rearrange("p c v (j e) -> p (c v) j e", j=J),
                        hv.unsqueeze(2).broadcast_to([P, CH * 2, J, DH]),
                        blockd[:].rearrange("p (j e) -> p j e", j=J).unsqueeze(1).broadcast_to([P, CH * 2, J, DH]),
                        ALU.mult).then_inc(hbd_ready.sem, 1)

                def gated(g):
                    cs = slice(g * J * DH, (g + 1) * J * DH)
                    nc.gpsimd.tensor_tensor(ysk[:], vtok[:, :, cs], lead(skipb[:, cs], TT), ALU.mult) \
                        .then_inc(yg_ready.sem, 1)
                    ysc_ready.wait(pool, u, g + 1)
                    yg_ready.wait(pool, u, 3 * g + 1)
                    nc.gpsimd.tensor_tensor(ysk[:], ysk[:], ysc[:, g % 2], ALU.add).then_inc(yg_ready.sem, 1)
                    yg_ready.wait(pool, u, 3 * g + 2)
                    nc.gpsimd.tensor_tensor(sg[:, :, cs], ysk[:], sg[:, :, cs], ALU.mult).then_inc(yg_ready.sem, 1)
                    yg_ready.wait(pool, u, 3 * g + 3)

                expand(0)
                expand(1)
                for g in range(G):
                    gated(g)
                    if g + 2 < G:
                        expand(g + 2)

        @block.vector
        def _(dve):
            chain = [0]

            def link(ins):
                chain[0] += 1
                ins.then_inc(step, 1)
                dve.wait_ge(step, chain[0])

            V = nc.vector
            V.memset(hist[:], 0.0)
            for row in range(2):
                for col in range(2):
                    V.memset(phi[:, 0, row, col, :], 1.0 if row == col else 0.0)
            V.memset(epsln[:], EPS_LN).then_inc(init_ready, 1)
            dve.wait_ge(w_loaded, 16 * NW)
            dve.wait_ge(exps_ready, 2)
            for g in range(G):
                link(V.tensor_tensor(seld[32:64, g, :].rearrange("p (j n) -> p j n", j=J),
                                     seld[32:64, g, :].rearrange("p (j n) -> p j n", j=J), lead(arow[H:2 * H, :], J), ALU.mult))
            V.tensor_scalar(nega[:], nega[:], -1.0, None, ALU.mult).then_inc(init_ready, 1)
            dve.wait_ge(init_ready, 3)
            with dve.Fori(0, NU) as u:
                dve.sem_clear(step)
                chain[0] = 0
                x_in.wait(dve, u, 16)
                link(V.tensor_copy(cmask[:], contm[:, bass.ds(u, 1)]))
                for a in range(TT):
                    link(V.bn_stats(bst[:, a, :], xt[:, a, :]))
                V.bn_aggr(mv[:, 0, :], bst[:, 0, :])
                V.bn_aggr(mv[:, 1, :], bst[:, 1, :]).then_inc(mv_ready.sem, 1)
                link(V.tensor_scalar(vraw[:, :, 0:3], hist[:], cmask[:, 0:1], None, ALU.mult))
                link(V.tensor_scalar(hst[:, 0], hst[:, CH], cmask[:, 0:1], None, ALU.mult))
                std_ready.wait(dve, u, 1)
                link(V.reciprocal(rstd[:], std[:]))
                V.tensor_scalar(xn[:, 0, :], xt[:, 0, :], mv[:, 0, 0:1], rstd[:, 0:1], ALU.subtract, ALU.mult)
                V.tensor_scalar(xn[:, 1, :], xt[:, 1, :], mv[:, 1, 0:1], rstd[:, 1:2], ALU.subtract, ALU.mult) \
                    .then_inc(xn_ready.sem, 1)
                for k in range(4):
                    if k % 2 == 0:
                        vraw_ready.wait(dve, u, k // 2 + 1)
                    link(V.tensor_scalar(cv[:, k, :], vraw[:, k, 3:], convw[:, k, 3:4], convb[:, k:k + 1],
                                         ALU.mult, ALU.add))
                    for q in range(3):
                        ins = V.scalar_tensor_tensor(cv[:, k, :], vraw[:, k, q:q + UT], convw[:, k, q:q + 1],
                                                     cv[:, k, :], ALU.mult, ALU.add)
                        if (k, q) == (3, 2):
                            ins.then_inc(conv_ready.sem, 1)
                        else:
                            link(ins)
                link(V.tensor_copy(hist[:], vraw[:, :, UT:]))
                par_ready.wait(dve, u, 1)
                link(V.tensor_scalar(ey[:], ey[:], Y_MAX, None, ALU.min))
                link(V.tensor_scalar(yv[:], ey[:], 1.0 / 7, None, ALU.mult))
                for cst in (-1.0 / 6, 1.0 / 5, -1.0 / 4, 1.0 / 3, -1.0 / 2, 1.0):
                    link(V.scalar_tensor_tensor(yv[:], yv[:], cst, ey[:], ALU.add, ALU.mult))
                dt = p5[:, 4, :]
                link(V.tensor_scalar(dt, yv[:], DT_MIN, DT_MAX, ALU.max, ALU.min))
                link(V.tensor_scalar(th[:], th[:], 0.25, 0.25, ALU.mult, ALU.add))
                link(V.tensor_tensor(yv[:], dt, th[:], ALU.mult))
                link(V.tensor_scalar(dr[0:H, :], yv[:], 1.0, None, ALU.add))
                link(V.tensor_tensor(dr[H:2 * H, :], dt, dt, ALU.mult))
                link(V.memset(qb[:, :, 0], 1.0))
                link(V.memset(iq[:], 1.0))
                for c in range(CH):
                    link(V.tensor_tensor_scan(qb[:, c, 1:], dr[0:H, c * L:(c + 1) * L], iq[:, 0:L], 1.0,
                                              ALU.mult, ALU.mult))
                cview = "p (c t) -> p c t"
                link(V.tensor_copy(p5[:, 2, :].rearrange(cview, c=CH), qb[:, :, 0:L]))
                link(V.tensor_copy(p5[:, 3, :].rearrange(cview, c=CH), qb[:, :, 1:]))
                link(V.reciprocal(iq[:], p5[:, 3, :]))
                link(V.tensor_tensor(p5[:, 0, :], dt, p5[:, 2, :], ALU.mult))
                V.tensor_tensor(p5[:, 1, :], dt, iq[:], ALU.mult).then_inc(p5_ready.sem, 1)
                for i in range(G // 2):
                    lnd_ready.wait(dve, u, i + 1)
                    if i >= 2:
                        pinv_ready.wait(dve, u, i - 1)
                    V.tensor_tensor_scan(lnr[:, i % 2, :], resetm[:], lnd[:, i % 2, :], 0.0, ALU.mult, ALU.add) \
                        .then_inc(lnr_ready.sem, 1)
                coef_ready.wait(dve, u, G)
                pinv_ready.wait(dve, u, G // 2)
                qe_ready.wait(dve, u, 1)
                for t in range(L):
                    cf = coef[:, t].unsqueeze(2).broadcast_to([P, 2, 2, LANES])
                    link(V.tensor_tensor(uu[:], phi[:, t, ::-1], cf, ALU.mult))
                    ins = V.tensor_tensor(phi[:, t + 1], phi[:, t], uu[:], ALU.add)
                    if t < L - 1:
                        link(ins)
                ins.then_inc(evolved.sem, 1)
                evolved.wait(dve, u, 1)
                pe_ = pinv[:].rearrange("p g (c t) -> p (g c) t", c=CH)[:, :, L - 1]
                link(V.tensor_copy(pend[:, 0], pe_))
                link(V.tensor_tensor(pend[:, 1], pend[:, 0], qe[:], ALU.mult))
                link(V.tensor_tensor(em[:, 0], phi[:, L, 0], lead(pend[:, 0], 2), ALU.mult))
                V.tensor_tensor(em[:, 1], phi[:, L, 1], lead(pend[:, 1], 2), ALU.mult).then_inc(em_ready.sem, 1)

                def rows(row, t0, g):
                    return phi[:, t0:t0 + L, row, :, g * CH:(g + 1) * CH].rearrange("p t k c -> p k c t")

                def cols(v):
                    return lead(v.rearrange("p (c t) -> p c t", c=CH), 2)

                def both(v):
                    return v.rearrange("p k (c t) -> p k c t", c=CH)

                def norm_parts(n, g):
                    nr_ready.wait(dve, u, n + 1)
                    link(V.tensor_scalar(nre[:], nr[:, g % 2], EPS_BC, None, ALU.add))
                    link(V.reciprocal(rn[:], nre[:]))

                def input_factors(g):
                    norm_parts(g, g)
                    hs = slice(J * g, J * g + J)
                    link(V.tensor_tensor(fc4[:], nre[:, :, 1], rn[:, :, 0], ALU.mult))
                    V.tensor_tensor(fct[:, g % 2], spread(fc4[:], N), spread(ptok[:, 0, :, hs], N), ALU.mult) \
                        .then_inc(fct_ready.sem, 1)
                    link(V.tensor_tensor(dus[:], ptok[:, 2, :, hs], rn[:, :, 1], ALU.mult))
                    cs = slice(g * J * DH, (g + 1) * J * DH)
                    if g == 0:
                        vtok_ready.wait(dve, u, TT)
                    V.tensor_tensor(du[:, :, cs].rearrange("p a (j e) -> p a j e", j=J),
                                    vtok[:, :, cs].rearrange("p a (j e) -> p a j e", j=J),
                                    spread(dus[:], DH), ALU.mult).then_inc(du_ready.sem, 1)

                def input_side(g):
                    bcs_ready.wait(dve, u, g + 1)
                    fbs_ready.wait(dve, u, g + 1)
                    link(V.tensor_tensor(tz[:, 0, :], bcs[:, g % 2, 0, :], fbs[:, g % 2, :], ALU.mult))
                    link(V.tensor_tensor(both(m1), rows(1, 0, g), cols(tz[:, 0, :]), ALU.mult))
                    link(V.tensor_tensor(both(m2), rows(0, 1, g), cols(bcs[:, g % 2, 1, :]), ALU.mult))
                    link(V.tensor_tensor(bt[:, g, 0, :], m1[:, 1, :], m2[:, 1, :], ALU.subtract))
                    V.tensor_tensor(bt[:, g, 1, :], m2[:, 0, :], m1[:, 0, :], ALU.subtract).then_inc(bt_ready.sem, 1)
                    bt_ready.wait(dve, u, g + 1)

                dve.wait_ge(x_out.sem, u * 16 + 16)
                for s in range(G + 1):
                    if s >= 1:
                        input_side(s - 1)
                    if s < G:
                        input_factors(s)

                def output_factors(g):
                    norm_parts(G + g, g)
                    hs = slice(J * g, J * g + J)
                    link(V.tensor_tensor(fc4[:], nre[:, :, 0], rn[:, :, 1], ALU.mult))
                    V.tensor_tensor(fct[:, g % 2], spread(fc4[:], N), spread(ptok[:, 1, :, hs], N), ALU.mult) \
                        .then_inc(fct_ready.sem, 1)
                    link(V.tensor_copy(rcz[:, g], rn[:, :, 0]))

                def output_side(g):
                    bcs_ready.wait(dve, u, G + g + 1)
                    fbs_ready.wait(dve, u, G + g + 1)
                    link(V.tensor_tensor(tz[:, 0, :], bcs[:, g % 2, 0, :], pinv[:, g, :], ALU.mult))
                    link(V.tensor_tensor(tz[:, 1, :], pinv[:, g, :], fbs[:, g % 2, :], ALU.mult))
                    link(V.tensor_tensor(tz[:, 1, :], bcs[:, g % 2, 1, :], tz[:, 1, :], ALU.mult))
                    link(V.tensor_tensor(both(m1), rows(0, 1, g), cols(tz[:, 0, :]), ALU.mult))
                    link(V.tensor_tensor(both(m2), rows(1, 1, g), cols(tz[:, 1, :]), ALU.mult))
                    if g >= 3:
                        y_ready.wait(dve, u, g - 2)
                    V.tensor_tensor(ct[:, g % 3], m1[:], m2[:], ALU.add).then_inc(ct_ready.sem, 1)
                    ct_ready.wait(dve, u, g + 1)

                def mask(g):
                    k_ready.wait(dve, u, g + 1)
                    if g == 0:
                        h_ready.wait(dve, u, 4 * CH)
                    if g >= 2:
                        y_ready.wait(dve, u, g - 1)
                    V.tensor_tensor(km[:, g % 2], kp[:, :, 0:TT * L].rearrange("p j (a t) -> p j a t", a=TT),
                                    lead(causal[:], TT).unsqueeze(1).broadcast_to([P, J, TT, L]), ALU.mult) \
                        .then_inc(km_ready.sem, 1)

                def scale_out(g):
                    y_ready.wait(dve, u, g + 1)
                    if g >= 2:
                        yg_ready.wait(dve, u, 3 * (g - 1))
                    V.tensor_tensor(ysc[:, g % 2].rearrange("p a (j e) -> p a j e", j=J),
                                    yp[:].rearrange("p a (j e) -> p a j e", j=J), spread(rcz[:, g], DH), ALU.mult) \
                        .then_inc(ysc_ready.sem, 1)

                for s in range(G + 3):
                    if 1 <= s <= G:
                        output_side(s - 1)
                    if s < G:
                        output_factors(s)
                    if 2 <= s <= G + 1:
                        mask(s - 2)
                    if s >= 3:
                        scale_out(s - 3)
                o_ready.wait(dve, u, TT)
                V.tensor_tensor(x1s[:], kp[:, 0:TT, 0:DM], xt[:], ALU.add).then_inc(x1_ready.sem, 1)
                x1_ready.wait(dve, u, 2)


SK, DC = 77, 192
DQ = DM // 16
XT = T // P
NT = NTOK // P
NE, NX, FF = 15, 17, 512


def cross_ring():
    tiles = [("kT",), ("v",)] + [("xT", i) for i in range(XT // 2)]
    tiles += [("qT", m, i) for m in range(2) for i in range(T // 512)]
    for s in range(XT + 3):
        if 1 <= s <= XT:
            tiles.append(("O", s - 1))
        if 2 <= s <= XT + 1:
            tiles.append(("oT", s - 2))
        if s >= 3:
            tiles.append(("out", s - 3))
    return tiles


XRING = cross_ring()
XIDX = {k: i for i, k in enumerate(XRING)}
assert len(XRING) % 2 == 0


def cross_attention(nc, d, x1, xres):
    with ExitStack() as ctx:
        def sb(name, shape):
            return ctx.enter_context(nc.sbuf_tensor("x_" + name, shape, F32))

        def ps(name, shape):
            return ctx.enter_context(nc.psum_tensor("xp_" + name, shape, F32))

        def sem(name):
            return ctx.enter_context(nc.semaphore("x_" + name))

        ident = sb("ident", [P, P])
        parity = sb("parity", [P, 2])
        ones = sb("ones", [1, P])
        wq = sb("wq", [P, 2, DM])
        wo = sb("wo", [P, 2, DM])
        wka = sb("wka", [P, DM])
        wkb = sb("wkb", [DC - P, DM])
        wva = sb("wva", [P, DM])
        wvb = sb("wvb", [DC - P, DM])
        bq = sb("bq", [P, 2])
        bk = sb("bk", [P, 2])
        bv = sb("bv", [1, DM])
        bo = sb("bo", [1, DM])
        ca = sb("ca", [P, SK])
        cb = sb("cb", [DC - P, SK])
        kraw = sb("kraw", [P, 2, SK])
        kz = sb("kz", [P, 2, 2, SK])
        va = sb("va", [SK, 16, DQ + 1])
        epsln = sb("epsln", [P, 1])
        bst = sb("bst", [P, XT, 6])
        mv = sb("mv", [P, XT, 2])
        std = sb("std", [P, XT])
        rstd = sb("rstd", [P, XT])
        xn = sb("xn", [P, XT, DM])
        xnt = sb("xnt", [P, 2, T])
        qt = sb("qt", [P, 2, T])
        mx = sb("mx", [P, 2, 4, 4])
        s_sb = sb("s", [P, 2, 16, SK])
        pt = sb("pt", [SK, 2, 16, P])
        rec = sb("rec", [P, 16])
        osb = sb("o", [P, 2, DM])
        ot = sb("ot", [P, 2, 2, P])

        ring = ps("ring", [P, 2, 512])
        sp_ = ps("scores", [P, 4, 512])
        ptp = ps("pt", [P, 2, 512])

        w_loaded = sem("w_loaded")
        NW = 13
        eps_ready = sem("eps_ready")
        x_in = Signal(sem("x_in"), 16)
        c_in = Signal(sem("c_in"), 32)
        ring_full = Signal(sem("ring_full"), len(XRING))
        mv_ready = Signal(sem("mv_ready"), 1)
        std_ready = Signal(sem("std_ready"), 1)
        bst_ready = sem("bst_ready")
        rstd_ready = Signal(sem("rstd_ready"), 1)
        xn_ready = Signal(sem("xn_ready"), XT)
        xnt_ready = Signal(sem("xnt_ready"), XT // 2)
        kraw_ready = Signal(sem("kraw_ready"), 2)
        kz_ready = Signal(sem("kz_ready"), 2)
        va_ready = Signal(sem("va_ready"), 1)
        qt_ready = Signal(sem("qt_ready"), 4)
        s_full = Signal(sem("s_full"), XT)
        mx_ready = Signal(sem("mx_ready"), XT)
        s_ready = Signal(sem("s_ready"), XT)
        pt_full = Signal(sem("pt_full"), 4 * XT)
        pt_ready = Signal(sem("pt_ready"), 4 * XT)
        rec_ready = Signal(sem("rec_ready"), XT)
        o_ready = Signal(sem("o_ready"), XT)
        ot_ready = Signal(sem("ot_ready"), XT)
        x2_ready = Signal(sem("x2_ready"), XT)
        kv_taken = Signal(sem("kv_taken"), 1)

        emptied = {("kT",): (kraw_ready, 2), ("v",): (va_ready, 1)}
        emptied |= {("xT", i): (xnt_ready, i + 1) for i in range(XT // 2)}
        emptied |= {("qT", m, i): (qt_ready, 2 * m + i + 1) for m in range(2) for i in range(2)}
        for i in range(XT):
            emptied |= {("O", i): (o_ready, i + 1), ("oT", i): (ot_ready, i + 1), ("out", i): (x2_ready, i + 1)}

        x1v = x1.rearrange("(n p) m -> p n m", p=P)
        block = ctx.enter_context(nc.Block())

        @block.sync
        def _(sp):
            for dst, src in (
                    (ident[:], d["ident"]), (parity[:], d["parity"]), (ones[:], d["onesrow"]),
                    (wq[:], d["wq"].rearrange("(k p) o -> p k o", p=P)),
                    (wo[:], d["wo"].rearrange("(k p) o -> p k o", p=P)),
                    (wka[:], d["wk"][0:P]), (wkb[:], d["wk"][P:DC]), (wva[:], d["wv"][0:P]), (wvb[:], d["wv"][P:DC]),
                    (bq[:], d["bq"]), (bk[:], d["bk"]), (bv[:], d["bv"]), (bo[:], d["bo"])):
                sp.dma_start(dst, src).then_inc(w_loaded, 16)
            sp.sem_inc(kv_taken.sem, 1)
            with sp.Fori(0, B) as b:
                kv_taken.wait(sp, b, 1)
                sp.dma_start(xres[:, bass.ds(b * XT, XT), :], x1v[:, bass.ds(b * XT, XT), :]).then_inc(x_in.sem, 16)
                sp.dma_start(ca[:], d["ctxT"][bass.ds(b, 1), 0:P].rearrange("a p s -> p (a s)")).then_inc(c_in.sem, 16)
                sp.dma_start(cb[:], d["ctxT"][bass.ds(b, 1), P:DC].rearrange("a p s -> p (a s)")) \
                    .then_inc(c_in.sem, 16)

        @block.tensor
        def _(pe):
            pe.wait_ge(w_loaded, 16 * NW)
            pe.wait_ge(eps_ready, 2)
            with pe.Fori(0, B) as b:
                def put(key):
                    i = XIDX[key]
                    if i >= 2:
                        sig, k = emptied[XRING[i - 2]]
                        sig.wait(pe, b, k)
                    return ring[:, i % 2, :]

                c_in.wait(pe, b, 32)
                o = put(("kT",))
                for m in range(2):
                    for k, (w, c) in enumerate(((wka, ca), (wkb, cb))):
                        mm = pe.matmul(o[:, m * SK:(m + 1) * SK], w[:, m * P:(m + 1) * P], c[:],
                                       start=(k == 0), stop=(k == 1))
                mm.then_inc(ring_full.sem, 1)
                o = put(("v",))
                pe.matmul(o[0:SK, 0:DM], ca[:], wva[:], start=True, stop=False)
                pe.matmul(o[0:SK, 0:DM], cb[:], wvb[:], start=False, stop=False)
                pe.matmul(o[0:SK, 0:DM], ones[:, 0:SK], bv[:], start=False, stop=True).then_inc(ring_full.sem, 1)
                for i in range(XT // 2):
                    xn_ready.wait(pe, b, 2 * i + 2)
                    o = put(("xT", i))
                    for k in range(2):
                        for a in range(2):
                            mm = pe.transpose(o[:, (2 * k + a) * P:(2 * k + a + 1) * P],
                                              xn[:, 2 * i + a, k * P:(k + 1) * P], ident[:])
                    mm.then_inc(ring_full.sem, 1)
                for m in range(2):
                    for i in range(2):
                        xnt_ready.wait(pe, b, 2 * i + 2)
                        o = put(("qT", m, i))
                        for k in range(2):
                            mm = pe.matmul(o, wq[:, k, m * P:(m + 1) * P], xnt[:, k, 512 * i:512 * (i + 1)],
                                           start=(k == 0), stop=(k == 1))
                        mm.then_inc(ring_full.sem, 1)
                qt_ready.wait(pe, b, 4)
                kz_ready.wait(pe, b, 2)
                va_ready.wait(pe, b, 1)
                for s in range(XT + 3):
                    if s < XT:
                        if s > 0:
                            s_ready.wait(pe, b, s)
                        for q in range(4):
                            for r in range(4):
                                m, par = q // 2, q % 2
                                rr = slice(32 * r, 32 * r + 32)
                                mm = pe.matmul(sp_[:, r, q * SK:(q + 1) * SK], qt[rr, m, s * P:(s + 1) * P],
                                               kz[rr, m, par, :], start=True, stop=True)
                        mm.then_inc(s_full.sem, 1)
                    if 1 <= s <= XT:
                        i = s - 1
                        s_ready.wait(pe, b, i + 1)
                        for q in range(4):
                            n = 4 * i + q
                            if q >= 2:
                                pt_ready.wait(pe, b, n - 1)
                            for h in range(4):
                                mm = pe.transpose(ptp[0:SK, q % 2, h * P:(h + 1) * P], s_sb[:, i % 2, 4 * q + h, :],
                                                  ident[:])
                            mm.then_inc(pt_full.sem, 1)
                        o = put(("O", i))
                        for q in range(4):
                            pt_ready.wait(pe, b, 4 * i + q + 1)
                            for h in range(4 * q, 4 * q + 4):
                                mm = pe.matmul(o[:, h * (DQ + 1):(h + 1) * (DQ + 1)], pt[:, i % 2, h, :], va[:, h, :],
                                               start=True, stop=True)
                        mm.then_inc(ring_full.sem, 1)
                    if 2 <= s <= XT + 1:
                        i = s - 2
                        o_ready.wait(pe, b, i + 1)
                        o = put(("oT", i))
                        for k in range(2):
                            mm = pe.transpose(o[:, k * P:(k + 1) * P], osb[:, i % 2, k * P:(k + 1) * P], ident[:])
                        mm.then_inc(ring_full.sem, 1)
                    if s >= 3:
                        i = s - 3
                        ot_ready.wait(pe, b, i + 1)
                        o = put(("out", i))
                        for k in range(2):
                            pe.matmul(o[:, 0:DM], ot[:, i % 2, k, :], wo[:, k, :], start=(k == 0), stop=False)
                        pe.matmul(o[:, 0:DM], ones[:], bo[:], start=False, stop=True).then_inc(ring_full.sem, 1)
                x2_ready.wait(pe, b, XT)

        @block.scalar
        def _(act):
            act.wait_ge(w_loaded, 16 * NW)
            act.wait_ge(eps_ready, 2)
            with act.Fori(0, B) as b:
                def take(key):
                    i = XIDX[key]
                    ring_full.wait(act, b, i + 1)
                    return ring[:, i % 2, :]

                o = take(("kT",))
                for m in range(2):
                    nc.scalar.activation(kraw[:, m, :], o[:, m * SK:(m + 1) * SK], ACT.Identity,
                                         bias=bk[:, m:m + 1]).then_inc(kraw_ready.sem, 1)
                o = take(("v",))
                nc.scalar.copy(va[:, :, 0:DQ], o[0:SK, 0:DM].rearrange("p (h e) -> p h e", h=16)) \
                    .then_inc(va_ready.sem, 1)
                mv_ready.wait(act, b, 1)
                nc.scalar.activation(std[:], mv[:, :, 1], ACT.Sqrt, bias=epsln[:, 0:1]).then_inc(std_ready.sem, 1)
                for i in range(XT // 2):
                    o = take(("xT", i))
                    nc.scalar.copy(xnt[:, :, 256 * i:256 * (i + 1)], o.rearrange("p (k t) -> p k t", k=2)) \
                        .then_inc(xnt_ready.sem, 1)
                for m in range(2):
                    for i in range(2):
                        o = take(("qT", m, i))
                        nc.scalar.activation(qt[:, m, 512 * i:512 * (i + 1)], o, ACT.Identity, bias=bq[:, m:m + 1]) \
                            .then_inc(qt_ready.sem, 1)
                for s in range(XT + 2):
                    if 1 <= s <= XT:
                        i = s - 1
                        for q in range(4):
                            pt_full.wait(act, b, 4 * i + q + 1)
                            if q == 0 and i >= 2:
                                ring_full.wait(act, b, XIDX[("O", i - 2)] + 1)
                            nc.scalar.activation(pt[:, i % 2, 4 * q:4 * q + 4, :],
                                                 ptp[0:SK, q % 2, :].rearrange("p (h t) -> p h t", h=4),
                                                 ACT.Exp, scale=DQ ** -0.5).then_inc(pt_ready.sem, 1)
                    if s >= 2:
                        i = s - 2
                        o = take(("oT", i))
                        nc.scalar.copy(ot[:, i % 2], o[:, 0:2 * P].rearrange("p (k t) -> p k t", k=2)) \
                            .then_inc(ot_ready.sem, 1)

        @block.vector
        def _(dve):
            V = nc.vector
            V.memset(epsln[:], EPS_LN).then_inc(eps_ready, 1)
            V.memset(va[:], 1.0).then_inc(eps_ready, 1)
            dve.wait_ge(w_loaded, 16 * NW)
            with dve.Fori(0, B) as b:
                dve.sem_clear(bst_ready)
                x_in.wait(dve, b, 16)
                for i in range(XT):
                    ins = V.bn_stats(bst[:, i, :], xres[:, bass.ds(b * XT + i, 1), :].rearrange("p a m -> p (a m)"))
                ins.then_inc(bst_ready, 1)
                dve.wait_ge(bst_ready, 1)
                for i in range(XT):
                    ins = V.bn_aggr(mv[:, i, :], bst[:, i, :])
                ins.then_inc(mv_ready.sem, 1)
                std_ready.wait(dve, b, 1)
                V.reciprocal(rstd[:], std[:]).then_inc(rstd_ready.sem, 1)
                rstd_ready.wait(dve, b, 1)
                for i in range(XT):
                    V.tensor_scalar(xn[:, i, :], xres[:, bass.ds(b * XT + i, 1), :].rearrange("p a m -> p (a m)"),
                                    mv[:, i, 0:1], rstd[:, i:i + 1], ALU.subtract, ALU.mult).then_inc(xn_ready.sem, 1)
                kraw_ready.wait(dve, b, 2)
                for par in range(2):
                    V.tensor_scalar(kz[:, :, par, :], kraw[:], parity[:, par:par + 1], None, ALU.mult) \
                        .then_inc(kz_ready.sem, 1)
                for s in range(XT + 3):
                    if s < XT:
                        s_full.wait(dve, b, s + 1)
                        sc = sp_[:, :, 0:4 * SK].rearrange("p r (q k) -> p r q k", q=4)
                        V.tensor_reduce(mx[:, s % 2], sc, AX.X, ALU.max).then_inc(mx_ready.sem, 1)
                        mx_ready.wait(dve, b, s + 1)
                        V.tensor_tensor(s_sb[:, s % 2].rearrange("p (r q) k -> p r q k", r=4), sc,
                                        mx[:, s % 2].unsqueeze(3).broadcast_to([P, 4, 4, SK]), ALU.subtract) \
                            .then_inc(s_ready.sem, 1)
                    if 1 <= s <= XT:
                        i = s - 1
                        ring_full.wait(dve, b, XIDX[("O", i)] + 1)
                        o = ring[:, XIDX[("O", i)] % 2, 0:16 * (DQ + 1)].rearrange("p (h e) -> p h e", h=16)
                        V.reciprocal(rec[:], o[:, :, DQ]).then_inc(rec_ready.sem, 1)
                        rec_ready.wait(dve, b, i + 1)
                        V.tensor_tensor(osb[:, i % 2].rearrange("p (h e) -> p h e", h=16), o[:, :, 0:DQ],
                                        rec[:].unsqueeze(2).broadcast_to([P, 16, DQ]), ALU.mult) \
                            .then_inc(o_ready.sem, 1)
                    if s >= 3:
                        i = s - 3
                        ring_full.wait(dve, b, XIDX[("out", i)] + 1)
                        xr = xres[:, bass.ds(b * XT + i, 1), :].rearrange("p a m -> p (a m)")
                        V.tensor_tensor(xr, ring[:, XIDX[("out", i)] % 2, 0:DM], xr, ALU.add).then_inc(x2_ready.sem, 1)

        @block.gpsimd
        def _(pool):
            with pool.Fori(0, B) as b:
                ring_full.wait(pool, b, 2)
                pool.sem_inc(kv_taken.sem, 1)


def experts(nc, d, xres, out):
    with ExitStack() as ctx:
        def sb(name, shape):
            return ctx.enter_context(nc.sbuf_tensor("f_" + name, shape, F32))

        def ps(name, shape):
            return ctx.enter_context(nc.psum_tensor("fp_" + name, shape, F32))

        def sem(name):
            return ctx.enter_context(nc.semaphore("f_" + name))

        NB = NTOK // 512
        ident = sb("ident", [P, P])
        ones = sb("ones", [1, P])
        gw = sb("gw", [P, 2, NE])
        gb = sb("gb", [1, NE])
        b1 = sb("b1", [P, 2, 4])
        b2 = sb("b2", [NX, DM])
        w1 = sb("w1", [P, 2, 2, FF])
        w2 = sb("w2", [P, 2, 4, DM])
        epsln = sb("epsln", [P, 1])
        bst = sb("bst", [P, NT, 6])
        mv = sb("mv", [P, NT, 2])
        std = sb("std", [P, NT])
        rstd = sb("rstd", [P, NT])
        xn = sb("xn", [P, 2, DM])
        xnt = sb("xnt", [P, 2, NTOK])
        lg = sb("lg", [P, NT, NE])
        nmx = sb("nmx", [P, NT])
        sm = sb("sm", [P, NT])
        pr = sb("pr", [P, 2, 24])
        top = sb("top", [P, 8])
        rest = sb("rest", [P, 24])
        gate = sb("gate", [P, NT, NX])
        gt = sb("gt", [NX, 2, P])
        hT = sb("hT", [P, 2, 4, 512])
        hp = ps("h", [P, 4, 512])
        yp = ps("y", [P, 4, 512])

        w_loaded = sem("w_loaded")
        mv_ready = sem("mv_ready")
        std_ready = sem("std_ready")
        rstd_ready = sem("rstd_ready")
        eps_ready = sem("eps_ready")
        xn_ready = sem("xn_ready")
        xt_full = sem("xt_full")
        xnt_ready = sem("xnt_ready")
        lg_full = sem("lg_full")
        lg_ready = sem("lg_ready")
        prob_ready = sem("prob_ready")
        step = sem("step")
        nmx_ready = sem("nmx_ready")
        gate_ready = sem("gate_ready")
        gt_full = sem("gt_full")
        gt_ready = sem("gt_ready")
        acc_ready = sem("acc_ready")
        b2_full = sem("b2_full")
        w_in = [sem(f"w_in{i}") for i in range(2)]
        h_full = sem("h_full")
        h_ready = sem("h_ready")
        y_full = sem("y_full")
        y_used = sem("y_used")
        stored = sem("stored")
        NW = 5

        block = ctx.enter_context(nc.Block())

        @block.sync
        def _(sp):
            for dst, src in ((ident[:], d["ident"]), (ones[:], d["onesrow"]),
                             (gw[:], d["gW"].rearrange("(k p) e -> p k e", p=P)), (gb[:], d["gb"]),
                             (b2[:], d["b2"])):
                sp.dma_start(dst, src).then_inc(w_loaded, 16)

            def load(e, par):
                sp.dma_start(w1[:, par], d["W1"][bass.ds(e, 1)].rearrange("a (k p) f -> p (a k) f", p=P)) \
                    .then_inc(w_in[par], 16)
                sp.dma_start(w2[:, par], d["W2"][bass.ds(e, 1)].rearrange("a (k p) f -> p (a k) f", p=P)) \
                    .then_inc(w_in[par], 16)
                sp.dma_start(b1[:, par], d["b1"][bass.ds(e, 1)].rearrange("a p f -> p (a f)")).then_inc(w_in[par], 16)

            load(0, 0)
            load(1, 1)
            with sp.Fori(0, 7) as i:
                for par in range(2):
                    sp.wait_ge(y_full, (2 * i + par + 1) * (2 * NB) + 4)
                    load(2 * i + par + 2, par)
            sp.wait_ge(y_full, 15 * 2 * NB + 4)
            load(16, 0)
            sp.wait_ge(y_used, NX * 2 * NB + 4)
            sp.dma_start(out.rearrange("(n p) m -> p n m", p=P), xres[:]).then_inc(stored, 16)
            sp.wait_ge(stored, 16)

        def all_experts(eng, body):
            with eng.Fori(0, 8) as i:
                for par in range(2):
                    body(2 * i + par, par, i)
            body(16, 0, 8)

        @block.tensor
        def _(pe):
            pe.wait_ge(w_loaded, 16 * NW)
            for i in range(NT):
                pe.wait_ge(xn_ready, i + 1)
                if i >= 2:
                    pe.wait_ge(xnt_ready, i - 1)
                for k in range(2):
                    mm = pe.transpose(hp[:, i % 2, k * P:(k + 1) * P], xn[:, i % 2, k * P:(k + 1) * P], ident[:])
                mm.then_inc(xt_full, 1)
            for i in range(NT):
                pe.wait_ge(xnt_ready, i + 1)
                if i >= 2:
                    pe.wait_ge(lg_ready, i - 1)
                o = yp[:, i % 2, 0:NE]
                for k in range(2):
                    pe.matmul(o, xnt[:, k, i * P:(i + 1) * P], gw[:, k, :], start=(k == 0), stop=False)
                pe.matmul(o, ones[:], gb[:], start=False, stop=True).then_inc(lg_full, 1)
            for i in range(NT + 1):
                if i < NT:
                    pe.wait_ge(gate_ready, i + 1)
                    if i >= 2:
                        pe.wait_ge(gt_ready, i - 1)
                    pe.transpose(hp[0:NX, i % 2, 0:P], gate[:, i, :], ident[:]).then_inc(gt_full, 1)
                if i >= 1:
                    pe.wait_ge(gt_ready, i)
                    if i >= 3:
                        pe.wait_ge(acc_ready, i - 2)
                    pe.matmul(yp[:, 2 + (i - 1) % 2, 0:DM], gt[:, (i - 1) % 2, :], b2[:], start=True, stop=True) \
                        .then_inc(b2_full, 1)
            pe.wait_ge(acc_ready, NT)
            pe.sem_inc(y_full, 4)

            def expert(e, par, k_e):
                pe.wait_ge(w_in[par], 48 * k_e + 48)
                for nb in range(NB + 1):
                    if nb < NB:
                        for f in range(4):
                            pe.wait_ge(h_ready, (e * NB + nb) * 4 + f + 1)
                            for k in range(2):
                                mm = pe.matmul(hp[:, f, :], w1[:, par, k, f * P:(f + 1) * P],
                                               xnt[:, k, nb * 512:(nb + 1) * 512], start=(k == 0), stop=(k == 1))
                            mm.then_inc(h_full, 1)
                    if nb >= 1:
                        q = nb - 1
                        pe.wait_ge(h_ready, (e * NB + q) * 4 + 8)
                        for a in range(4):
                            if a % 2 == 0:
                                pe.wait_ge(y_used, (e * NB + q) * 2 + a // 2 + 1)
                            for f in range(4):
                                mm = pe.matmul(yp[:, 2 * (q % 2) + a // 2, (a % 2) * DM:(a % 2 + 1) * DM],
                                               hT[:, q % 2, f, a * P:(a + 1) * P], w2[:, par, f, :],
                                               start=(f == 0), stop=(f == 3))
                            if a % 2 == 1:
                                mm.then_inc(y_full, 1)

            all_experts(pe, expert)

        @block.scalar
        def _(act):
            act.wait_ge(mv_ready, 1)
            nc.scalar.activation(std[:], mv[:, :, 1], ACT.Sqrt, bias=epsln[:, 0:1]).then_inc(std_ready, 1)
            act.wait_ge(w_loaded, 16 * NW)
            for i in range(NT):
                act.wait_ge(xt_full, i + 1)
                nc.scalar.copy(xnt[:, :, i * P:(i + 1) * P], hp[:, i % 2, 0:2 * P].rearrange("p (k t) -> p k t", k=2)) \
                    .then_inc(xnt_ready, 1)
            for i in range(NT):
                act.wait_ge(lg_full, i + 1)
                nc.scalar.copy(lg[:, i, :], yp[:, i % 2, 0:NE]).then_inc(lg_ready, 1)
            act.wait_ge(nmx_ready, 1)

            def gates_out(i):
                act.wait_ge(gt_full, i + 1)
                if i >= 2:
                    act.wait_ge(b2_full, i - 1)
                nc.scalar.copy(gt[:, i % 2, :], hp[0:NX, i % 2, 0:P]).then_inc(gt_ready, 1)

            for i in range(NT):
                if i >= 2:
                    act.wait_ge(gate_ready, i - 1)
                nc.scalar.activation(pr[:, i % 2, 0:NE], lg[:, i, :], ACT.Exp, bias=nmx[:, i:i + 1],
                                     accum_out=sm[:, i:i + 1]).then_inc(prob_ready, 1)
                if i >= 1:
                    gates_out(i - 1)
            gates_out(NT - 1)
            act.sem_inc(h_ready, 4)

            def expert(e, par, k_e):
                for nb in range(NB):
                    act.wait_ge(y_full, (e * NB + nb) * 2 + 2)
                    for f in range(4):
                        act.wait_ge(h_full, (e * NB + nb) * 4 + f + 1)
                        nc.scalar.activation(hT[:, nb % 2, f, :], hp[:, f, :], ACT.Gelu,
                                             bias=b1[:, par, f:f + 1]).then_inc(h_ready, 1)

            all_experts(act, expert)

        @block.vector
        def _(dve):
            V = nc.vector
            chain = [0]

            def link(ins):
                chain[0] += 1
                ins.then_inc(step, 1)
                dve.wait_ge(step, chain[0])

            V.memset(pr[:], -1.0)
            V.memset(gate[:], 1.0)
            link(V.memset(epsln[:], EPS_LN))
            for i in range(NT):
                ins = V.bn_stats(bst[:, i, :], xres[:, i, :])
            link(ins)
            for i in range(NT):
                ins = V.bn_aggr(mv[:, i, :], bst[:, i, :])
            ins.then_inc(mv_ready, 1)
            dve.wait_ge(std_ready, 1)
            link(V.reciprocal(rstd[:], std[:]))
            for i in range(NT):
                if i >= 2:
                    dve.wait_ge(xt_full, i - 1)
                V.tensor_scalar(xn[:, i % 2, :], xres[:, i, :], mv[:, i, 0:1], rstd[:, i:i + 1],
                                ALU.subtract, ALU.mult).then_inc(xn_ready, 1)
                dve.wait_ge(xn_ready, i + 1)
                ins = V.tensor_tensor(xres[:, i, :], xres[:, i, :], xn[:, i % 2, :], ALU.add)
            link(ins)
            dve.wait_ge(lg_ready, NT)
            link(V.tensor_reduce(nmx[:], lg[:], AX.X, ALU.max))
            V.tensor_scalar(nmx[:], nmx[:], -1.0, None, ALU.mult).then_inc(nmx_ready, 1)
            for i in range(NT + 1):
                if i < NT:
                    dve.wait_ge(prob_ready, i + 1)
                    link(V.reciprocal(sm[:, i:i + 1], sm[:, i:i + 1]))
                    link(V.tensor_scalar(pr[:, i % 2, 0:NE], pr[:, i % 2, 0:NE], sm[:, i:i + 1], None, ALU.mult))
                    link(V.max(top[:], pr[:, i % 2, :]))
                    link(V.memset(top[:, 3:8], -1.0))
                    link(V.match_replace(rest[:], top[:], pr[:, i % 2, :], 0.0))
                    V.tensor_tensor(gate[:, i, 0:NE], pr[:, i % 2, 0:NE], rest[:, 0:NE], ALU.subtract) \
                        .then_inc(gate_ready, 1)
                if i >= 1:
                    dve.wait_ge(b2_full, i)
                    V.tensor_tensor(xres[:, i - 1, :], yp[:, 2 + (i - 1) % 2, 0:DM], xres[:, i - 1, :], ALU.add) \
                        .then_inc(acc_ready, 1)
            dve.wait_ge(gate_ready, NT)
            dve.sem_inc(y_used, 4)

            def expert(e, par, k_e):
                for nb in range(NB):
                    for half in range(2):
                        n2 = (e * NB + nb) * 2 + half
                        dve.wait_ge(y_full, n2 + 5)
                        dve.wait_ge(y_used, n2 + 1)
                        for a in range(2):
                            i = nb * 4 + half * 2 + a
                            ins = V.scalar_tensor_tensor(
                                xres[:, i, :], yp[:, 2 * (nb % 2) + half, a * DM:(a + 1) * DM],
                                gate[:, i, bass.ds(e, 1)], xres[:, i, :], ALU.mult, ALU.add)
                        ins.then_inc(y_used, 1)

            all_experts(dve, expert)


def program(nc, d, out, stage=3):
    x1 = nc.dram_tensor("x1_scratch", (NTOK, DM), F32).ap() if stage > 1 else out
    attention(nc, d, d["x"].rearrange("b t m -> (b t) m"), x1)
    if stage > 1:
        with nc.sbuf_tensor("xres", [P, NT, DM], F32) as xres:
            cross_attention(nc, d, x1, xres)
            experts(nc, d, xres, out)


def layouts(inputs):
    r = {"x": inputs["x"]}
    w = np.asarray(inputs["L0_attn_W_in"])
    order = np.concatenate([np.arange(2 * DI), 2 * DI + 2 * np.arange(H), 2 * DI + 2 * np.arange(H) + 1])
    r["W_in"] = w[order].T
    w = np.asarray(inputs["L0_attn_W_bc"]).reshape(G, J, 4, N, DI)
    r["W_bc"] = w.transpose(0, 2, 1, 3, 4).reshape(H * 4 * N, DI).T
    r["W_out"] = np.asarray(inputs["L0_attn_W_out"]).T
    r["conv_bias"] = np.asarray(inputs["L0_attn_dw_bias"]).reshape(4, P).T
    r["A_states"] = np.asarray(inputs["L0_attn_A_log"]).reshape(G, J * N).T
    for k in ("dw_weight", "skip", "A_log", "dt_bias"):
        r[k] = inputs["L0_attn_" + k]
    r["ctxT"] = np.asarray(inputs["ctx_768"]).transpose(0, 2, 1)
    heads = np.array([8 * (q // 2) + 2 * row + q % 2 for row in range(4) for q in range(4)])
    cols = (heads[:, None] * DQ + np.arange(DQ)[None]).reshape(-1)
    for k in ("wq", "wk"):
        r[k] = inputs["L0_xattn_" + k]
    r["wv"] = np.asarray(inputs["L0_xattn_wv"])[:, cols]
    r["bv"] = np.asarray(inputs["L0_xattn_bv"])[cols][None]
    r["wo"] = np.asarray(inputs["L0_xattn_wo"])[cols]
    r["bo"] = np.asarray(inputs["L0_xattn_bo"])[None]
    for k in ("bq", "bk"):
        r[k] = np.asarray(inputs["L0_xattn_" + k]).reshape(2, P).T
    ffn = {k[7:]: np.asarray(v) for k, v in inputs.items() if k.startswith("L0_ffn_")}
    r["gW"], r["gb"] = ffn["gW"], ffn["gb"][None]
    sw1 = ffn["sW1"][0].reshape(DM, 2, FF).transpose(1, 0, 2)
    r["W1"] = np.concatenate([ffn["rW1"], sw1])
    r["W2"] = np.concatenate([ffn["rW2"], ffn["sW2"][0].reshape(2, FF, DM)])
    r["b1"] = np.concatenate([ffn["rb1"], ffn["sb1"][0].reshape(2, FF)]).reshape(NX, 4, P).transpose(0, 2, 1)
    r["b2"] = np.concatenate([ffn["rb2"], ffn["sb2"], np.zeros((1, DM), np.float32)])
    r.update(constants())
    return {k: np.ascontiguousarray(v) for k, v in r.items()}


def kernel(**inputs):
    import numpy as _np
    import concourse.bacc as _bacc
    from concourse import mybir as _mybir
    from concourse.bass_utils import run_bass_kernel_spmd as _run

    nc = _bacc.Bacc("TRN2", target_bir_lowering=False, num_devices=1)
    arrays, args = {}, {}
    for name, a in layouts(inputs).items():
        arrays[f"in_{name}_dram"] = a
        args[name] = nc.dram_tensor(f"in_{name}_dram", a.shape, _mybir.dt.from_np(a.dtype), kind="ExternalInput").ap()
    out = nc.dram_tensor("out_0_dram", (B, T, DM), F32, kind="ExternalOutput").ap()
    program(nc, args, out.rearrange("b t m -> (b t) m"))
    r = _run(nc, [arrays], core_ids=[0])
    return r.results[0]["out_0_dram"]
```

```python
from contextlib import ExitStack

import numpy as np

import concourse.bass as bass
from concourse import mybir

F32 = mybir.dt.float32
F16 = mybir.dt.float16
ALU = mybir.AluOpType
ACT = mybir.ActivationFunctionType
AX = mybir.AxisListType

P = 128
B, T, DM = 4, 1024, 256
NTOK = B * T
DI, H, N, DH = 512, 32, 32, 16
KCONV = 4
L = 64
CH = 4
UT = CH * L
NU = NTOK // UT
TT = UT // P
NT = NTOK // P
UPB = T // UT
G, J = 8, 4
LANES = G * CH
EPS_LN, EPS_BC = 1e-5, 1e-8
DT_MIN, DT_MAX, Y_MAX = 1e-4, 0.1, 0.106


class Signal:

    def __init__(self, sem, per):
        self.sem, self.per = sem, per

    def wait(self, eng, u, k):
        eng.wait_ge(self.sem, k if u is None else u * self.per + k)


def constants():
    c = {}
    c["ident"] = np.eye(P, dtype=np.float32)
    jn = np.arange(P) // N
    c["sel4"] = (jn[:, None] == np.arange(J)[None]).astype(np.float32)
    c["blockd"] = (jn[:, None] == (np.arange(J * DH) // DH)[None]).astype(np.float32)
    h = np.arange(64) % H
    c["selh"] = (h[:, None, None] == (np.arange(G)[:, None] * J + jn[None])[None]).astype(np.float32)
    c["causal"] = (np.arange(L)[None] >= (np.arange(P) % L)[:, None]).astype(np.float32)
    r = np.ones((P, 2 * CH * L), np.float32)
    r[:, ::L] = 0
    c["resetm"] = r
    c["contm"] = np.tile((np.arange(NU) % UPB != 0).astype(np.float32)[None], (P, 1))
    par = (np.arange(P) // 16) % 2
    c["parity"] = np.stack([par == 0, par == 1], 1).astype(np.float32)
    c["onesrow"] = np.ones((1, P), np.float32)
    return c


PT = 512
NPASS = NTOK // PT
PA = PT // P
PBANKS = 5
SV, SW = 16.0, 64.0

PRING = [("xT", 0), ("xT", 1)] + [("val", m) for m in range(4)] + [("par",)]
PRING += [("gate", a) for a in range(PA)] + [("vt", a) for a in range(PA)]
PIDX = {k: i for i, k in enumerate(PRING)}
assert len(PRING) % PBANKS == 0


def projections(nc, d, x, st):
    with ExitStack() as ctx:
        def sb(name, shape, dt=F32):
            return ctx.enter_context(nc.sbuf_tensor("p_" + name, shape, dt))

        def ps(name, shape):
            return ctx.enter_context(nc.psum_tensor("pp_" + name, shape, F32))

        def sem(name):
            return ctx.enter_context(nc.semaphore("p_" + name))

        ident = sb("ident", [P, P])
        win = sb("win", [P, 2, 2 * DI + 2 * H])
        convw = sb("convw", [P, 4, KCONV])
        convb = sb("convb", [P, 4])
        epsln = sb("epsln", [P, 1])
        xt = sb("xt", [P, NT, DM])
        bst = sb("bst", [P, NT, 6])
        mv = sb("mv", [P, NT, 2])
        std = sb("std", [P, NT])
        rstd = sb("rstd", [P, NT])
        xn = sb("xn", [P, 2, PA, DM])
        xnt = sb("xnt", [P, 2, PT])
        vraw = sb("vraw", [P, 2, 4, PT + KCONV - 1])
        cv = sb("cv", [P, 4, PT])
        valt = sb("valt", [P, 4, PT])
        vhl = sb("vhl", [P, 2, 2, 4, PT], F16)
        vtok = sb("vtok", [P, 2, PA, DI])
        sg = sb("sg", [P, 2, PA, DI])
        rawp = sb("rawp", [2 * H, PT])
        wf = sb("wf", [P, H * 4 * N])
        whl = sb("whl", [P, 2, H * 4 * N], F16)
        ring = ps("ring", [P, PBANKS, 512])

        w_loaded = sem("w_loaded")
        NW = 4
        init_ready = sem("init_ready")
        x_in = sem("x_in")
        stats_ready = sem("stats_ready")
        std_ready = sem("std_ready")
        ring_full = Signal(sem("ring_full"), len(PRING))
        xn_ready = Signal(sem("xn_ready"), 1)
        xnt_ready = Signal(sem("xnt_ready"), 2)
        vraw_ready = Signal(sem("vraw_ready"), 4)
        raw_ready = Signal(sem("raw_ready"), 1)
        raw_out = Signal(sem("raw_out"), 32)
        sg_ready = Signal(sem("sg_ready"), PA)
        conv_ready = Signal(sem("conv_ready"), 4)
        valt_ready = Signal(sem("valt_ready"), 4)
        vhi_ready = Signal(sem("vhi_ready"), 1)
        vlo_ready = Signal(sem("vlo_ready"), 1)
        vtok_ready = Signal(sem("vtok_ready"), PA)
        stored = [Signal(sem(f"stored{i}"), 16 * 4) for i in range(2)]
        w_in = sem("w_in")
        whi_ready = sem("whi_ready")
        wlo_ready = sem("wlo_ready")
        w_out = sem("w_out")
        step = sem("step")

        emptied = {("par",): (raw_ready, 1)}
        for i in range(4):
            emptied |= {("xT", i): (xnt_ready, i + 1), ("val", i): (vraw_ready, i + 1),
                        ("gate", i): (sg_ready, i + 1)}

        def passes(eng, body):
            with eng.Fori(0, NPASS // 2) as i:
                for par in range(2):
                    body(2 * i + par, par, i)

        wv = d["W_bc"].rearrange("(k p) o -> k p o", p=P)
        wov = st["whl"].rearrange("p v k o -> k p v o")
        block = ctx.enter_context(nc.Block())

        @block.sync
        def _(sp):
            sp.dma_start(xt[:], x.rearrange("(n p) m -> p n m", p=P)).then_inc(x_in, 16)
            for dst, src in ((ident[:], d["ident"]), (win[:], d["W_in"].rearrange("(k p) o -> p k o", p=P)),
                             (convw[:], d["dw_weight"].rearrange("(k p) c -> p k c", p=P)),
                             (convb[:], d["conv_bias"])):
                sp.dma_start(dst, src).then_inc(w_loaded, 16)

            def body(u, par, i):
                raw_ready.wait(sp, u, 1)
                for q in range(2):
                    sp.dma_start(st["raw"][q, bass.ds(i, 1), :, par * PT:(par + 1) * PT].rearrange("a h t -> h (a t)"),
                                 rawp[q * H:(q + 1) * H, :]).then_inc(raw_out.sem, 16)
                sg_ready.wait(sp, u, PA)
                sp.dma_start(st["sg"].rearrange("(u a p) m -> u p a m", a=PA, p=P)[u], sg[:, par]) \
                    .then_inc(stored[par].sem, 16)
                vtok_ready.wait(sp, u, 2 * PA)
                sp.dma_start(st["vtok"].rearrange("(u a p) m -> u p a m", a=PA, p=P)[u], vtok[:, par]) \
                    .then_inc(stored[par].sem, 16)
                vlo_ready.wait(sp, u, 1)
                for v in range(2):
                    sp.dma_start(st["vhl"][2 * u + v], vhl[:, par, :, :, v * UT:(v + 1) * UT]) \
                        .then_inc(stored[par].sem, 16)

            passes(sp, body)
            for s in stored:
                sp.wait_ge(s.sem, 64 * (NPASS // 2) + 64)
            sp.wait_ge(raw_out.sem, 32 * NPASS + 32)

        @block.tensor
        def _(pe):
            pe.wait_ge(w_loaded, 16 * NW)

            def body(u, par, i):
                def put(key):
                    n = PIDX[key]
                    if n >= PBANKS:
                        sig, k = emptied[PRING[n - PBANKS]]
                        sig.wait(pe, u, k)
                    return ring[:, n % PBANKS, :]

                def full(ins):
                    ins.then_inc(ring_full.sem, 1)

                xn_ready.wait(pe, u, 1)
                vtok_ready.wait(pe, u, PA)
                for k in range(2):
                    o = put(("xT", k))
                    for a in range(PA):
                        mm = pe.transpose(o[:, a * P:(a + 1) * P], xn[:, par, a, k * P:(k + 1) * P], ident[:])
                    full(mm)
                xnt_ready.wait(pe, u, 2)
                for m in range(4):
                    o = put(("val", m))
                    for k in range(2):
                        mm = pe.matmul(o, win[:, k, DI + m * P:DI + (m + 1) * P], xnt[:, k, :],
                                       start=(k == 0), stop=(k == 1))
                    full(mm)
                o = put(("par",))
                for k in range(2):
                    mm = pe.matmul(o[0:2 * H, :], win[:, k, 2 * DI:2 * DI + 2 * H], xnt[:, k, :],
                                   start=(k == 0), stop=(k == 1))
                full(mm)
                for a in range(PA):
                    o = put(("gate", a))
                    for k in range(2):
                        mm = pe.matmul(o, xnt[:, k, a * P:(a + 1) * P], win[:, k, 0:DI],
                                       start=(k == 0), stop=(k == 1))
                    full(mm)
                valt_ready.wait(pe, u, 4)
                for a in range(PA):
                    o = put(("vt", a))
                    for k in range(4):
                        mm = pe.transpose(o[:, k * P:(k + 1) * P], valt[:, k, a * P:(a + 1) * P], ident[:])
                    full(mm)

            passes(pe, body)

        @block.scalar
        def _(act):
            act.wait_ge(stats_ready, 1)
            nc.scalar.activation(std[:], mv[:, :, 1], ACT.Sqrt, bias=epsln[:, 0:1]).then_inc(std_ready, 1)
            act.wait_ge(w_loaded, 16 * NW)
            act.wait_ge(init_ready, 1)
            act.sem_inc(vtok_ready.sem, PA)
            act.sem_inc(raw_out.sem, 32)
            for s in stored:
                act.sem_inc(s.sem, 64)

            def body(u, par, i):
                def take(key):
                    n = PIDX[key]
                    ring_full.wait(act, u, n + 1)
                    return ring[:, n % PBANKS, :]

                for k in range(2):
                    o = take(("xT", k))
                    nc.scalar.copy(xnt[:, k, :], o).then_inc(xnt_ready.sem, 1)
                for m in range(4):
                    o = take(("val", m))
                    nc.scalar.copy(vraw[:, par, m, KCONV - 1:], o).then_inc(vraw_ready.sem, 1)
                o = take(("par",))
                raw_out.wait(act, u, 32)
                nc.scalar.copy(rawp[:], o[0:2 * H, :]).then_inc(raw_ready.sem, 1)
                stored[par].wait(act, i, 64)
                for a in range(PA):
                    o = take(("gate", a))
                    nc.scalar.activation(sg[:, par, a, :], o, ACT.Silu).then_inc(sg_ready.sem, 1)
                for m in range(4):
                    conv_ready.wait(act, u, m + 1)
                    nc.scalar.activation(valt[:, m, :], cv[:, m, :], ACT.Silu).then_inc(valt_ready.sem, 1)
                for a in range(PA):
                    o = take(("vt", a))
                    nc.scalar.copy(vtok[:, par, a, :], o).then_inc(vtok_ready.sem, 1)

            passes(act, body)

        @block.gpsimd
        def _(pool):
            for i in range(DI // P):
                pool.dma_start(wf[:], wv[i]).then_inc(w_in, 16)
                pool.wait_ge(w_in, 16 * i + 16)
                nc.gpsimd.tensor_scalar(whl[:, 0], wf[:], SW, None, ALU.mult).then_inc(whi_ready, 1)
                pool.wait_ge(whi_ready, 2 * i + 1)
                nc.gpsimd.tensor_scalar(wf[:], wf[:], SW, None, ALU.mult).then_inc(whi_ready, 1)
                pool.wait_ge(whi_ready, 2 * i + 2)
                nc.gpsimd.tensor_tensor(whl[:, 1], wf[:], whl[:, 0], ALU.subtract).then_inc(wlo_ready, 1)
                pool.wait_ge(wlo_ready, i + 1)
                pool.dma_start(wov[i], whl[:]).then_inc(w_out, 16)
                pool.wait_ge(w_out, 16 * i + 16)

        @block.vector
        def _(dve):
            V = nc.vector
            V.memset(epsln[:], EPS_LN)
            V.memset(vraw[:, :, :, 0:KCONV - 1], 0.0).then_inc(init_ready, 1)
            dve.wait_ge(x_in, 16)
            for n in range(NT):
                ins = V.bn_stats(bst[:, n, :], xt[:, n, :])
            ins.then_inc(step, 1)
            dve.wait_ge(step, 1)
            for n in range(NT):
                ins = V.bn_aggr(mv[:, n, :], bst[:, n, :])
            ins.then_inc(stats_ready, 1)
            dve.wait_ge(std_ready, 1)
            V.reciprocal(rstd[:], std[:]).then_inc(step, 1)
            dve.wait_ge(step, 2)
            dve.wait_ge(w_loaded, 16 * NW)
            dve.wait_ge(init_ready, 1)

            def body(u, par, i):
                dve.sem_clear(step)
                chain = [0]

                def link(ins):
                    chain[0] += 1
                    ins.then_inc(step, 1)
                    dve.wait_ge(step, chain[0])

                for a in range(PA):
                    n = bass.ds(u * PA + a, 1)
                    ins = V.tensor_scalar(xn[:, par, a, :], xt[:, n, :].rearrange("p a m -> p (a m)"),
                                          mv[:, n, 0:1].rearrange("p a m -> p (a m)"), rstd[:, n],
                                          ALU.subtract, ALU.mult)
                ins.then_inc(xn_ready.sem, 1)
                for k in range(4):
                    vraw_ready.wait(dve, u, k + 1)
                    if par == 1:
                        link(V.tensor_copy(vraw[:, 1, k, 0:KCONV - 1], vraw[:, 0, k, PT:PT + KCONV - 1]))
                    link(V.tensor_scalar(cv[:, k, :], vraw[:, par, k, 3:], convw[:, k, 3:4], convb[:, k:k + 1],
                                         ALU.mult, ALU.add))
                    for q in range(3):
                        ins = V.scalar_tensor_tensor(cv[:, k, :], vraw[:, par, k, q:q + PT], convw[:, k, q:q + 1],
                                                     cv[:, k, :], ALU.mult, ALU.add)
                        if q == 2:
                            ins.then_inc(conv_ready.sem, 1)
                        else:
                            link(ins)
                valt_ready.wait(dve, u, 4)
                V.tensor_scalar(vhl[:, par, 0], valt[:], SV, None, ALU.mult).then_inc(vhi_ready.sem, 1)
                vhi_ready.wait(dve, u, 1)
                V.scalar_tensor_tensor(vhl[:, par, 1], valt[:], SV, vhl[:, par, 0], ALU.mult, ALU.subtract) \
                    .then_inc(vlo_ready.sem, 1)

            passes(dve, body)


def parameters(nc, d, st):
    with ExitStack() as ctx:
        def sb(name, shape):
            return ctx.enter_context(nc.sbuf_tensor("q_" + name, shape, F32))

        def sem(name):
            return ctx.enter_context(nc.semaphore("q_" + name))

        NC = T // L
        ident = sb("ident", [P, P])
        dtb = sb("dtb", [P, 1])
        raw = sb("raw", [P, 2, T])
        yv = sb("yv", [P, T])
        ones = sb("ones", [P, T])
        q4 = sb("q4", [P, 4, T])
        qb = sb("qb", [P, NC, L + 1])
        qx = sb("qx", [P, NC])
        qd = sb("qd", [P, 3, T])
        pts = sb("pts", [P, B, UPB, 3, TT, H])
        tp = ctx.enter_context(nc.psum_tensor("qp_t", [P, 6, 4, P], F32))

        loaded = sem("loaded")
        act_ready = sem("act_ready")
        q_ready = sem("q_ready")
        t_full = sem("t_full")
        pts_ready = sem("pts_ready")
        stored = sem("stored")
        step = sem("step")
        block = ctx.enter_context(nc.Block())

        @block.sync
        def _(sp):
            sp.dma_start(ident[:], d["ident"]).then_inc(loaded, 16)
            sp.dma_start(dtb[:], d["dt_bias_b"]).then_inc(loaded, 16)
            for q in range(2):
                sp.dma_start(raw[:, q, :], st["raw"][q].rearrange("b h t -> (b h) t")).then_inc(loaded, 16)
            sp.wait_ge(q_ready, 1)
            for b in range(B):
                r = slice(b * H, (b + 1) * H)
                us = slice(b * UPB, (b + 1) * UPB)
                for q in range(4):
                    sp.dma_start(st["q4"][us, q].rearrange("c h t -> h c t"),
                                 q4[r, q].rearrange("h (c t) -> h c t", c=UPB)).then_inc(stored, 16)
                sp.dma_start(st["qend"][us].rearrange("u h c -> h u c"),
                             qx[r].rearrange("h (u c) -> h u c", u=UPB)).then_inc(stored, 16)
            sp.wait_ge(pts_ready, 6)
            sp.dma_start(st["ptok"].rearrange("(b c) p q a h -> p (b c) (q a h)", b=B),
                         pts[:].rearrange("p b c q a h -> p (b c) (q a h)")).then_inc(stored, 16)
            sp.wait_ge(stored, 16 * (5 * B + 1))

        @block.tensor
        def _(pe):
            pe.wait_ge(loaded, 64)
            pe.wait_ge(q_ready, 1)
            for q in range(3):
                for n in range(8):
                    mm = pe.transpose(tp[:, 2 * q + n // 4, n % 4, :], qd[:, q, n * P:(n + 1) * P], ident[:])
                    if n % 4 == 3:
                        mm.then_inc(t_full, 1)

        @block.scalar
        def _(act):
            act.wait_ge(loaded, 64)
            nc.scalar.activation(raw[:, 0, :], raw[:, 0, :], ACT.Exp, bias=dtb[:, 0:1]).then_inc(act_ready, 1)
            nc.scalar.activation(raw[:, 1, :], raw[:, 1, :], ACT.Tanh, scale=0.5).then_inc(act_ready, 1)
            for q in range(3):
                for half in range(2):
                    act.wait_ge(t_full, 2 * q + half + 1)
                    for a in range(TT):
                        ins = nc.scalar.copy(
                            pts[:, :, 2 * half:2 * half + 2, q, a, :],
                            tp[:, 2 * q + half, a::TT, :].rearrange("p c (b h) -> p b c h", b=B))
                    ins.then_inc(pts_ready, 1)

        @block.vector
        def _(dve):
            V = nc.vector
            chain = [0]

            def link(ins):
                chain[0] += 1
                ins.then_inc(step, 1)
                dve.wait_ge(step, chain[0])

            V.memset(qb[:], 1.0)
            link(V.memset(ones[:], 1.0))
            ey, th, dt = raw[:, 0, :], raw[:, 1, :], qd[:, 2, :]
            dve.wait_ge(act_ready, 2)
            link(V.tensor_scalar(ey, ey, Y_MAX, None, ALU.min))
            link(V.tensor_scalar(yv[:], ey, 1.0 / 7, None, ALU.mult))
            for cst in (-1.0 / 6, 1.0 / 5, -1.0 / 4, 1.0 / 3, -1.0 / 2, 1.0):
                link(V.scalar_tensor_tensor(yv[:], yv[:], cst, ey, ALU.add, ALU.mult))
            link(V.tensor_scalar(dt, yv[:], DT_MIN, DT_MAX, ALU.max, ALU.min))
            link(V.tensor_scalar(th, th, 0.25, 0.25, ALU.mult, ALU.add))
            link(V.tensor_tensor(yv[:], dt, th, ALU.mult))
            link(V.tensor_scalar(q4[:, 2, :], yv[:], 1.0, None, ALU.add))
            V.tensor_tensor(q4[:, 3, :], dt, dt, ALU.mult)
            for c in range(NC):
                ins = V.tensor_tensor_scan(qb[:, c, 1:], q4[:, 2, c * L:(c + 1) * L], ones[:, 0:L], 1.0,
                                           ALU.mult, ALU.mult)
            link(ins)
            cview = "p (c t) -> p c t"
            V.tensor_copy(qx[:], qb[:, :, L])
            V.tensor_copy(qd[:, 0, :].rearrange(cview, c=NC), qb[:, :, 0:L])
            link(V.tensor_copy(qd[:, 1, :].rearrange(cview, c=NC), qb[:, :, 1:]))
            link(V.reciprocal(yv[:], qd[:, 1, :]))
            link(V.tensor_tensor(q4[:, 0, :], dt, qd[:, 0, :], ALU.mult))
            V.tensor_tensor(q4[:, 1, :], dt, yv[:], ALU.mult).then_inc(q_ready, 1)


def ring_tiles():
    tiles = [("bcB", g) for g in range(G)]
    for s in range(G + 2):
        if s < G:
            tiles += [("FB", s), ("D", s)]
        if s >= 2:
            tiles += [("BT", s - 2), ("G", s - 2, 0), ("G", s - 2, 1)]
    for s in range(G + 1):
        if s < G:
            tiles += [("bcC", s), ("w", s)]
        if s >= 1:
            tiles.append(("FC", s - 1))
    tiles += [("yT", 0), ("yT", 1)]
    return tiles


RING = ring_tiles()
RIDX = {k: i for i, k in enumerate(RING)}
assert len(RING) % 2 == 0


def mixer(nc, d, st, x, x1):
    with ExitStack() as ctx:
        def sb(name, shape, dt=F32):
            return ctx.enter_context(nc.sbuf_tensor(name, shape, dt))

        def ps(name, shape):
            return ctx.enter_context(nc.psum_tensor(name, shape, F32))

        def sem(name):
            return ctx.enter_context(nc.semaphore(name))

        ident = sb("ident", [P, P])
        sel4 = sb("sel4", [P, J])
        blockd = sb("blockd", [P, J * DH])
        seld = sb("seld", [64, G, P])
        causal = sb("causal", [P, L])
        resetm = sb("resetm", [P, 2 * UT])
        contm = sb("contm", [P, NU])
        whl = sb("whl", [P, 2, 4, G, 4, P], F16)
        wout = sb("wout", [P, 4, DM])
        arow = sb("arow", [2 * H, N])
        nega = sb("nega", [P, G])
        skipb = sb("skipb", [P, DI])
        hst = sb("hst", [P, CH + 1, 2, G, DH])
        cmask = sb("cmask", [P, 1])
        coef = sb("coef", [P, L, 2, LANES])
        wrow = sb("wrow", [H, 2, UT])
        dr = sb("dr", [2 * H, UT])
        qend = sb("qend", [H, CH])
        vhl = sb("vhl", [P, 2, 4, UT], F16)
        vtok = sb("vtok", [P, TT, DI])
        sg = sb("sg", [P, TT, DI])
        ptok = sb("ptok", [P, 3, TT, H])
        x1s = sb("x1s", [P, TT, DM])
        phi = sb("phi", [P, L + 1, 2, 2, LANES])
        pinv = sb("pinv", [P, G, UT])
        qe = sb("qe", [P, LANES])
        em = sb("em", [P, 2, 2, LANES])
        pend = sb("pend", [P, 2, LANES])
        du = sb("du", [P, TT, DI])
        bt = sb("bt", [P, G, 2, UT])
        bcs = sb("bcs", [P, 2, 2, UT])
        sq = sb("sq", [P, 2, UT])
        fbs = sb("fbs", [P, 2, UT])
        m2 = sb("m2", [P, 2, UT])
        ct = sb("ct", [P, 3, 2, UT])
        km = sb("km", [P, 2, J, TT, L])
        hbd = sb("hbd", [P, 2, CH, 2, J * DH])
        uu = sb("uu", [P, 2, 2, LANES])
        nr = sb("nr", [P, G, TT, 2, J])
        nre = sb("nre", [P, G, TT, 2, J])
        rn = sb("rn", [P, G, TT, 2, J])
        fc4 = sb("fc4", [P, G, TT, J])
        dus = sb("dus", [P, TT, G, J])
        fct = sb("fct", [P, 2, TT, J, N])
        ysc = sb("ysc", [P, 2, TT, J * DH])
        ysk = sb("ysk", [P, TT, J * DH])

        def over(mem, at, shape, names):
            n = int(np.prod(shape))
            return mem[:, at:at + n].rearrange(f"p ({names}) -> p {names}", **dict(zip(names.split(), shape)))

        bcs_flat = bcs[:].rearrange("p i v t -> p (i v t)")
        hbd_flat = hbd[:].rearrange("p i c v e -> p (i c v e)")
        m1 = ct[:, 0]
        btt = over(bcs_flat, 0, (2, TT, P), "v a m")
        ygt = over(bcs_flat, 0, (TT, 4, P), "a k t")
        gs = over(km[:].rearrange("p i j a t -> p (i j a t)"), 0, (CH, 2, G, DH), "c v g e")
        hu = over(hbd_flat, 0, (2, 2, G, DH), "r v g e")
        ht = over(hbd_flat, 4 * G * DH, (2, G, DH), "v g e")

        ring = ps("ring", [P, 2, 512])
        ssp_bank = ps("ssp", [P, 512])
        yp_bank = ps("yp", [P, 512])
        ssp = ssp_bank[:, 0:G * TT * 2 * J].rearrange("p (g a v j) -> p g a v j", g=G, a=TT, v=2)
        yp = yp_bank[:, 0:TT * J * DH].rearrange("p (a e) -> p a e", a=TT)
        kp = ps("kp", [P, 4, 512])

        w_loaded = sem("w_loaded")
        NW = 12
        exps_ready = sem("exps_ready")
        init_ready = sem("init_ready")
        first_full = sem("first_full")
        wrow_in = Signal(sem("wrow_in"), 16)
        dr_in = Signal(sem("dr_in"), 32)
        vhl_in = Signal(sem("vhl_in"), 16)
        vtok_in = Signal(sem("vtok_in"), 16)
        ptok_in = Signal(sem("ptok_in"), 16)
        sg_in = Signal(sem("sg_in"), 16)
        x_in = Signal(sem("x_in"), 16)
        x_out = Signal(sem("x_out"), 16)
        ring_full = Signal(sem("ring_full"), len(RING))
        coef_ready = Signal(sem("coef_ready"), G)
        ln_ready = Signal(sem("ln_ready"), G)
        scan_ready = Signal(sem("scan_ready"), G // 2)
        pinv_ready = Signal(sem("pinv_ready"), 1)
        evolved = Signal(sem("evolved"), 1)
        em_ready = Signal(sem("em_ready"), 1)
        bcs_ready = Signal(sem("bcs_ready"), 2 * G)
        sq_ready = Signal(sem("sq_ready"), 2 * G)
        ss_ready = Signal(sem("ss_ready"), 2 * G)
        nr_ready = Signal(sem("nr_ready"), 1 + G)
        fct_ready = Signal(sem("fct_ready"), 2 * G)
        fbs_ready = Signal(sem("fbs_ready"), 2 * G)
        bt_ready = Signal(sem("bt_ready"), G)
        du_ready = Signal(sem("du_ready"), 1)
        btt_ready = Signal(sem("btt_ready"), G)
        gs_ready = Signal(sem("gs_ready"), 2 * G)
        h_ready = Signal(sem("h_ready"), 4 * CH + 1)
        hbd_ready = Signal(sem("hbd_ready"), G)
        ct_ready = Signal(sem("ct_ready"), G)
        k_ready = Signal(sem("k_ready"), G)
        km_ready = Signal(sem("km_ready"), G)
        y_ready = Signal(sem("y_ready"), G)
        ysc_ready = Signal(sem("ysc_ready"), G)
        yg_ready = Signal(sem("yg_ready"), 3 * G)
        ygt_ready = Signal(sem("ygt_ready"), TT)
        o_ready = Signal(sem("o_ready"), TT)
        x1_ready = Signal(sem("x1_ready"), 1)
        step = sem("dve_step")

        emptied = {("yT", a): (ygt_ready, a + 1) for a in range(TT)}
        for g in range(G):
            emptied |= {("w", g): (coef_ready, G + g + 1), ("D", g): (ln_ready, g + 1),
                        ("bcB", g): (sq_ready, g + 1), ("bcC", g): (sq_ready, G + g + 1),
                        ("FB", g): (fbs_ready, g + 1), ("FC", g): (fbs_ready, G + g + 1),
                        ("BT", g): (btt_ready, g + 1), ("G", g, 0): (gs_ready, 2 * g + 1),
                        ("G", g, 1): (gs_ready, 2 * g + 2)}

        def tokens(v):
            return v.rearrange("(u a p) m -> u p a m", a=TT, p=P)

        def lead(v, k):
            return v.unsqueeze(1).broadcast_to([v.shape[0], k, *v.shape[1:]])

        def spread(v, k):
            n = len(v.shape)
            return v.unsqueeze(n).broadcast_to([*v.shape, k])

        block = ctx.enter_context(nc.Block())

        @block.sync
        def _(sp):
            def load_wrow(u):
                sp.dma_start(wrow[:], st["q4"][u][0:2].rearrange("q h t -> h q t")).then_inc(wrow_in.sem, 16)

            def load_dr(u):
                sp.dma_start(dr[:], st["q4"][u][2:4].rearrange("q h t -> (q h) t")).then_inc(dr_in.sem, 16)
                sp.dma_start(qend[:], st["qend"][u]).then_inc(dr_in.sem, 16)

            def load_vhl(u):
                sp.dma_start(vhl[:], st["vhl"][u]).then_inc(vhl_in.sem, 16)

            def load_ptok(u):
                sp.dma_start(ptok[:], st["ptok"][u]).then_inc(ptok_in.sem, 16)

            def load_vtok(u):
                sp.dma_start(vtok[:], tokens(st["vtok"])[u]).then_inc(vtok_in.sem, 16)

            def load_sg(u):
                sp.dma_start(sg[:], tokens(st["sg"])[u]).then_inc(sg_in.sem, 16)

            def load_x(u):
                sp.dma_start(x1s[:], tokens(x)[u]).then_inc(x_in.sem, 16)

            def store(u):
                x1_ready.wait(sp, u, 1)
                sp.dma_start(tokens(x1)[u], x1s[:]).then_inc(x_out.sem, 16)

            for dst, src in (
                    (seld[:], d["selh"]), (nega[:], d["A_states"]), (arow[H:2 * H, :], d["A_log"])):
                sp.dma_start(dst, src).then_inc(w_loaded, 16)
            load_wrow(0)
            load_vhl(0)
            for dst, src in (
                    (whl[:], st["whl"].rearrange("p v k (g c o) -> p v k g c o", g=G, c=4)),
                    (ident[:], d["ident"]), (sel4[:], d["sel4"]), (blockd[:], d["blockd"]),
                    (causal[:], d["causal"]), (resetm[:], d["resetm"]), (contm[:], d["contm"]),
                    (wout[:], d["W_out"].rearrange("(k p) o -> p k o", p=P)),
                    ):
                sp.dma_start(dst, src).then_inc(w_loaded, 16)
            sp.dma_start(skipb[:], d["skip"].partition_broadcast(P)).then_inc(w_loaded, 16)
            load_ptok(0)
            load_vtok(0)
            load_dr(0)
            load_sg(0)
            load_x(0)
            with sp.Fori(0, NU - 1) as u:
                coef_ready.wait(sp, u, G)
                load_wrow(u + 1)
                ring_full.wait(sp, u, RIDX[("D", G - 1)] + 1)
                load_dr(u + 1)
                ring_full.wait(sp, u, RIDX[("bcC", G - 1)] + 1)
                load_vhl(u + 1)
                fct_ready.wait(sp, u, 2 * G)
                load_ptok(u + 1)
                yg_ready.wait(sp, u, 3 * G)
                load_vtok(u + 1)
                ring_full.wait(sp, u, RIDX[("yT", TT - 1)] + 1)
                load_sg(u + 1)
                store(u)
                x_out.wait(sp, u, 16)
                load_x(u + 1)
            sp.wait_ge(coef_ready.sem, NU * G)
            load_wrow(0)
            sp.wait_ge(x1_ready.sem, NU)
            sp.dma_start(tokens(x1)[NU - 1], x1s[:]).then_inc(x_out.sem, 16)
            sp.wait_ge(x_out.sem, 16 * NU)

        @block.tensor
        def _(pe):
            def spread_coefs(o, g):
                for q in range(2):
                    mm = pe.matmul(o[:, q * UT:(q + 1) * UT], seld[0:H, g, :], wrow[:, q, :], start=True, stop=True)
                return mm

            pe.wait_ge(w_loaded, 16 * NW)
            pe.wait_ge(init_ready, 2)
            pe.wait_ge(wrow_in.sem, 16)
            for g in range(G):
                if g >= 2:
                    pe.wait_ge(coef_ready.sem, g - 1)
                spread_coefs(ring[:, g % 2, :], g).then_inc(first_full, 1)
            pe.wait_ge(coef_ready.sem, G)
            with pe.Fori(0, NU) as u:
                def put(key):
                    i = RIDX[key]
                    if i >= 2:
                        sig, k = emptied[RING[i - 2]]
                        sig.wait(pe, u, k)
                    return ring[:, i % 2, :]

                def full(ins):
                    ins.then_inc(ring_full.sem, 1)

                def bc(name, g, first):
                    o = put((name, g))
                    for v in range(2):
                        n = 0
                        for k in range(4):
                            for wh, vh in ((0, 0), (0, 1), (1, 0)):
                                mm = pe.matmul(o[:, v * UT:(v + 1) * UT], whl[:, wh, k, g, first + v, :],
                                               vhl[:, vh, k, :], start=(n == 0), stop=(n == 11))
                                n += 1
                    full(mm)

                def sums(n, g):
                    sq_ready.wait(pe, u, n + 1)
                    if n >= G:
                        nr_ready.wait(pe, u, n - G + 1)
                    for a in range(TT):
                        for v in range(2):
                            mm = pe.matmul(ssp[:, g, a, v, :], sq[:, v, a * P:(a + 1) * P], sel4[:],
                                           start=True, stop=True)
                    mm.then_inc(ss_ready.sem, 1)

                def factors(name, n, g):
                    fct_ready.wait(pe, u, n + 1)
                    o = put((name, g))
                    for a in range(TT):
                        mm = pe.transpose(o[:, a * P:(a + 1) * P], fct[:, g % 2, a].rearrange("p j n -> p (j n)"), ident[:])
                    full(mm)

                vhl_in.wait(pe, u, 16)
                for s in range(G + 1):
                    if s < G:
                        bc("bcB", s, 0)
                    if s >= 1:
                        sums(s - 1, s - 1)
                for s in range(G + 2):
                    if s < G:
                        factors("FB", s, s)
                        if s == 0:
                            dr_in.wait(pe, u, 32)
                        o = put(("D", s))
                        mm = pe.matmul(o[:, 0:UT], seld[:, s, :], dr[:], start=True, stop=True)
                        if s == 0:
                            for g in range(G):
                                mm = pe.matmul(o[:, UT + g * CH:UT + (g + 1) * CH], seld[0:H, g, :], qend[:],
                                               start=True, stop=True)
                        full(mm)
                    if s >= 2:
                        g = s - 2
                        bt_ready.wait(pe, u, g + 1)
                        o = put(("BT", g))
                        for v in range(2):
                            for a in range(TT):
                                c0 = (v * TT + a) * P
                                mm = pe.transpose(o[:, c0:c0 + P], bt[:, g, v, a * P:(a + 1) * P], ident[:])
                        full(mm)
                        btt_ready.wait(pe, u, g + 1)
                        if g == 0:
                            du_ready.wait(pe, u, 1)
                        for odd in range(2):
                            o = put(("G", g, odd))
                            r = slice(L * odd, L * odd + L)
                            for a in range(TT):
                                for v in range(2):
                                    c0 = (a * 2 + v) * J * DH
                                    mm = pe.matmul(o[:, c0:c0 + J * DH], btt[r, v, a, :],
                                                   du[r, a, g * J * DH:(g + 1) * J * DH], start=True, stop=True)
                            full(mm)
                for s in range(G + 3):
                    if s < G:
                        bc("bcC", s, 2)
                        if s == 0:
                            wrow_in.wait(pe, u, 32)
                        full(spread_coefs(put(("w", s)), s))
                    if 1 <= s <= G:
                        factors("FC", G + s - 1, s - 1)
                    if 2 <= s <= G + 1:
                        g = s - 2
                        ct_ready.wait(pe, u, g + 1)
                        if g > 0:
                            km_ready.wait(pe, u, g)
                        for c in range(CH):
                            r0 = L * (c % 2)
                            for v in range(2):
                                for j in range(J):
                                    mm = pe.matmul(kp[r0:r0 + L, j, (c // 2) * L:(c // 2 + 1) * L],
                                                   bt[N * j:N * j + N, g, v, c * L:(c + 1) * L],
                                                   ct[N * j:N * j + N, g % 3, v, c * L:(c + 1) * L],
                                                   start=(v == 0), stop=(v == 1), skip_group_check=True)
                        mm.then_inc(k_ready.sem, 1)
                    if s < G:
                        sums(G + s, s)
                    if s >= 3:
                        g = s - 3
                        km_ready.wait(pe, u, g + 1)
                        hbd_ready.wait(pe, u, g + 1)
                        if g > 0:
                            ysc_ready.wait(pe, u, g)
                        for c in range(CH):
                            r0 = L * (c % 2)
                            o = yp[r0:r0 + L, c // 2, :]
                            for v in range(2):
                                pe.matmul(o, ct[:, g % 3, v, c * L:(c + 1) * L], hbd[:, g % 2, c, v, :],
                                          start=(v == 0), stop=False, skip_group_check=True)
                            for j in range(J):
                                q0 = (g * J + j) * DH
                                mm = pe.matmul(o[:, j * DH:(j + 1) * DH], km[r0:r0 + L, g % 2, j, c // 2, :],
                                               du[r0:r0 + L, c // 2, q0:q0 + DH],
                                               start=False, stop=(j == J - 1), skip_group_check=True)
                        mm.then_inc(y_ready.sem, 1)
                yg_ready.wait(pe, u, 3 * G)
                for a in range(TT):
                    o = put(("yT", a))
                    for k in range(4):
                        mm = pe.transpose(o[:, k * P:(k + 1) * P], sg[:, a, k * P:(k + 1) * P], ident[:])
                    full(mm)
                for a in range(TT):
                    ygt_ready.wait(pe, u, a + 1)
                    for k in range(4):
                        mm = pe.matmul(kp[:, a, 0:DM], ygt[:, a, k, :], wout[:, k, :], start=(k == 0), stop=(k == 3))
                    mm.then_inc(o_ready.sem, 1)

        @block.scalar
        def _(act):
            act.wait_ge(w_loaded, 16 * NW)
            nc.scalar.activation(nega[:], nega[:], ACT.Exp).then_inc(exps_ready, 1)
            nc.scalar.activation(arow[H:2 * H, :], arow[H:2 * H, :], ACT.Exp).then_inc(exps_ready, 1)
            act.wait_ge(init_ready, 2)

            def coefs(o, g):
                for q in range(2):
                    src = o[:, q * UT:(q + 1) * UT].rearrange("p (c t) -> p c t", c=CH)
                    dst = coef[:, :, q, g * CH:(g + 1) * CH].rearrange("p t c -> p c t")
                    if q == 0:
                        nc.scalar.activation(dst, src, ACT.Copy, scale=nega[:, g:g + 1])
                    else:
                        nc.scalar.copy(dst, src).then_inc(coef_ready.sem, 1)

            for g in range(G):
                act.wait_ge(first_full, g + 1)
                coefs(ring[:, g % 2, :], g)
            with act.Fori(0, NU) as u:
                def take(key):
                    i = RIDX[key]
                    ring_full.wait(act, u, i + 1)
                    return ring[:, i % 2, :]

                def factors(name, n, g):
                    o = take((name, g))
                    if n >= 2:
                        (bt_ready if n - 2 < G else ct_ready).wait(act, u, (n - 2) % G + 1)
                    nc.scalar.copy(fbs[:, g % 2, :], o[:, 0:UT]).then_inc(fbs_ready.sem, 1)

                for g in range(G):
                    o = take(("bcB", g)).rearrange("p (v t) -> p v t", v=2)
                    nc.scalar.copy(bt[:, g], o).then_inc(bcs_ready.sem, 1)
                    if g >= 1:
                        ss_ready.wait(act, u, g)
                    nc.scalar.activation(sq[:], o, ACT.Square).then_inc(sq_ready.sem, 1)
                ss_ready.wait(act, u, G)
                nc.scalar.activation(nr[:], ssp[:], ACT.Sqrt).then_inc(nr_ready.sem, 1)
                for s in range(G + 2):
                    if s < G:
                        factors("FB", s, s)
                        o = take(("D", s))
                        if s == 0:
                            nc.scalar.copy(qe[:], o[:, UT:UT + LANES])
                        nc.scalar.activation(pinv[:, s, :], o[:, 0:UT], ACT.Ln).then_inc(ln_ready.sem, 1)
                    if s >= 2:
                        g = s - 2
                        o = take(("BT", g))
                        nc.scalar.copy(btt[:], o.rearrange("p (v a m) -> p v a m", v=2, a=TT)) \
                            .then_inc(btt_ready.sem, 1)
                        for odd in range(2):
                            o = take(("G", g, odd))
                            for j in range(J):
                                r = slice(N * j, N * j + N)
                                src = o[r, 0:TT * 2 * J * DH].rearrange("p (a v e) -> p a v e", a=TT, v=2)
                                ins = nc.scalar.copy(gs[r, odd::2, :, g, :], src[:, :, :, DH * j:DH * (j + 1)])
                            ins.then_inc(gs_ready.sem, 1)
                    if s == G:
                        scan_ready.wait(act, u, G // 2)
                        nc.scalar.activation(pinv[:], pinv[:], ACT.Exp, scale=-1.0).then_inc(pinv_ready.sem, 1)
                for s in range(G + 1):
                    if s < G:
                        o = take(("bcC", s)).rearrange("p (v t) -> p v t", v=2)
                        if s >= 2:
                            ct_ready.wait(act, u, s - 1)
                        nc.scalar.copy(bcs[:, s % 2, :, :], o).then_inc(bcs_ready.sem, 1)
                        if s >= 1:
                            ss_ready.wait(act, u, G + s)
                        nc.scalar.activation(sq[:], o, ACT.Square).then_inc(sq_ready.sem, 1)
                        coefs(take(("w", s)), s)
                    if s >= 1:
                        factors("FC", G + s - 1, s - 1)
                    if s < G:
                        ss_ready.wait(act, u, G + s + 1)
                        if s == 0:
                            fct_ready.wait(act, u, G)
                        nc.scalar.activation(nr[:, s], ssp[:, s], ACT.Sqrt).then_inc(nr_ready.sem, 1)
                for a in range(TT):
                    o = take(("yT", a))
                    if a == 0:
                        ct_ready.wait(act, u, G)
                    nc.scalar.copy(ygt[:, a], o.rearrange("p (k t) -> p k t", k=4)).then_inc(ygt_ready.sem, 1)

        @block.gpsimd
        def _(pool):
            nc.gpsimd.memset(hst[:, CH], 0.0).then_inc(init_ready, 1)
            with pool.Fori(0, NU) as u:
                em_ready.wait(pool, u, 1)
                nc.gpsimd.tensor_tensor(hst[:, 0].rearrange("p v g e -> p (v g e)"),
                                        hst[:, CH].rearrange("p v g e -> p (v g e)"),
                                        cmask[:].broadcast_to([P, 2 * G * DH]), ALU.mult).then_inc(h_ready.sem, 1)
                n = 1
                h_ready.wait(pool, u, n)
                gs_ready.wait(pool, u, 2 * G)
                for c in range(CH):
                    nc.gpsimd.tensor_tensor(ht[:], hst[:, c], gs[:, c], ALU.add).then_inc(h_ready.sem, 1)
                    n += 1
                    h_ready.wait(pool, u, n)
                    for r in range(2):
                        nc.gpsimd.tensor_tensor(
                            hu[:, r], ht[:], spread(em[:, r].rearrange("p k (g c) -> p k g c", g=G)[:, :, :, c], DH),
                            ALU.mult).then_inc(h_ready.sem, 1)
                        n += 1
                    h_ready.wait(pool, u, n)
                    nc.gpsimd.tensor_tensor(hst[:, c + 1], hu[:, :, 0], hu[:, :, 1], ALU.add).then_inc(h_ready.sem, 1)
                    n += 1
                    h_ready.wait(pool, u, n)
                assert n == h_ready.per
                vtok_in.wait(pool, u, 16)
                sg_in.wait(pool, u, 16)

                def expand(g):
                    if g >= 2:
                        y_ready.wait(pool, u, g - 1)
                    hv = hst[:, 0:CH, :, g, :].rearrange("p c v e -> p (c v) e")
                    nc.gpsimd.tensor_tensor(
                        hbd[:, g % 2].rearrange("p c v (j e) -> p (c v) j e", j=J),
                        hv.unsqueeze(2).broadcast_to([P, CH * 2, J, DH]),
                        blockd[:].rearrange("p (j e) -> p j e", j=J).unsqueeze(1).broadcast_to([P, CH * 2, J, DH]),
                        ALU.mult).then_inc(hbd_ready.sem, 1)

                def gated(g):
                    cs = slice(g * J * DH, (g + 1) * J * DH)
                    nc.gpsimd.tensor_tensor(ysk[:], vtok[:, :, cs], lead(skipb[:, cs], TT), ALU.mult) \
                        .then_inc(yg_ready.sem, 1)
                    ysc_ready.wait(pool, u, g + 1)
                    yg_ready.wait(pool, u, 3 * g + 1)
                    nc.gpsimd.tensor_tensor(ysk[:], ysk[:], ysc[:, g % 2], ALU.add).then_inc(yg_ready.sem, 1)
                    yg_ready.wait(pool, u, 3 * g + 2)
                    nc.gpsimd.tensor_tensor(sg[:, :, cs], ysk[:], sg[:, :, cs], ALU.mult).then_inc(yg_ready.sem, 1)
                    yg_ready.wait(pool, u, 3 * g + 3)

                expand(0)
                expand(1)
                for g in range(G):
                    gated(g)
                    if g + 2 < G:
                        expand(g + 2)

        @block.vector
        def _(dve):
            chain = [0]

            def link(ins):
                chain[0] += 1
                ins.then_inc(step, 1)
                dve.wait_ge(step, chain[0])

            V = nc.vector
            for row in range(2):
                for col in range(2):
                    V.memset(phi[:, 0, row, col, :], 1.0 if row == col else 0.0)
            dve.wait_ge(w_loaded, 16 * NW)
            dve.wait_ge(exps_ready, 2)
            for g in range(G):
                sg_ = seld[32:64, g, :].rearrange("p (j n) -> p j n", j=J)
                V.tensor_tensor(sg_, sg_, lead(arow[H:2 * H, :], J), ALU.mult)
            V.tensor_scalar(nega[:], nega[:], -1.0, None, ALU.mult).then_inc(init_ready, 1)
            dve.wait_ge(init_ready, 2)
            with dve.Fori(0, NU) as u:
                dve.sem_clear(step)
                chain[0] = 0
                V.tensor_copy(cmask[:], contm[:, bass.ds(u, 1)])
                coef_ready.wait(dve, u, G)
                for t in range(L):
                    cf = coef[:, t].unsqueeze(2).broadcast_to([P, 2, 2, LANES])
                    link(V.tensor_tensor(uu[:], phi[:, t, ::-1], cf, ALU.mult))
                    ins = V.tensor_tensor(phi[:, t + 1], phi[:, t], uu[:], ALU.add)
                    if t < L - 1:
                        link(ins)
                ins.then_inc(evolved.sem, 1)
                evolved.wait(dve, u, 1)

                def rows(row, t0, g):
                    return phi[:, t0:t0 + L, row, :, g * CH:(g + 1) * CH].rearrange("p t k c -> p k c t")

                def cols(v):
                    return lead(v.rearrange("p (c t) -> p c t", c=CH), 2)

                def both(v):
                    return v.rearrange("p k (c t) -> p k c t", c=CH)

                nr_ready.wait(dve, u, 1)
                ptok_in.wait(dve, u, 16)
                link(V.tensor_scalar(nre[:], nr[:], EPS_BC * SV * SW, None, ALU.add))
                link(V.reciprocal(rn[:], nre[:]))
                V.tensor_tensor(fc4[:], nre[:, :, :, 1], rn[:, :, :, 0], ALU.mult)
                link(V.tensor_tensor(dus[:], ptok[:, 2].rearrange("p a (g j) -> p a g j", g=G),
                                     rn[:, :, :, 1].rearrange("p g a j -> p a g j"), ALU.mult))

                def input_factors(g):
                    hs = slice(J * g, J * g + J)
                    if g >= 2:
                        fbs_ready.wait(dve, u, g - 1)
                    V.tensor_tensor(fct[:, g % 2], spread(fc4[:, g], N), spread(ptok[:, 0, :, hs], N), ALU.mult) \
                        .then_inc(fct_ready.sem, 1)

                def input_side(g):
                    bcs_ready.wait(dve, u, g + 1)
                    fbs_ready.wait(dve, u, g + 1)
                    link(V.tensor_tensor(fbs[:, g % 2, :], bt[:, g, 0, :], fbs[:, g % 2, :], ALU.mult))
                    V.tensor_tensor(both(m1), rows(1, 0, g), cols(fbs[:, g % 2, :]), ALU.mult)
                    link(V.tensor_tensor(both(m2), rows(0, 1, g), cols(bt[:, g, 1, :]), ALU.mult))
                    V.tensor_tensor(bt[:, g, 0, :], m1[:, 1, :], m2[:, 1, :], ALU.subtract)
                    V.tensor_tensor(bt[:, g, 1, :], m2[:, 0, :], m1[:, 0, :], ALU.subtract).then_inc(bt_ready.sem, 1)
                    bt_ready.wait(dve, u, g + 1)

                for s in range(G + 1):
                    if s < G:
                        input_factors(s)
                    if s == 0:
                        vtok_in.wait(dve, u, 16)
                        V.tensor_tensor(du[:].rearrange("p a (h e) -> p a h e", h=H),
                                        vtok[:].rearrange("p a (h e) -> p a h e", h=H),
                                        spread(dus[:].rearrange("p a g j -> p a (g j)"), DH), ALU.mult) \
                            .then_inc(du_ready.sem, 1)
                    if s >= 1:
                        input_side(s - 1)
                    if s % 2 == 1:
                        i = s // 2
                        ln_ready.wait(dve, u, 2 * i + 2)
                        pi = pinv[:, 2 * i:2 * i + 2, :].rearrange("p g t -> p (g t)")
                        V.tensor_tensor_scan(pi, resetm[:], pi, 0.0, ALU.mult, ALU.add).then_inc(scan_ready.sem, 1)
                pinv_ready.wait(dve, u, 1)
                pe_ = pinv[:].rearrange("p g (c t) -> p (g c) t", c=CH)[:, :, L - 1]
                link(V.tensor_copy(pend[:, 0], pe_))
                link(V.tensor_tensor(pend[:, 1], pend[:, 0], qe[:], ALU.mult))
                V.tensor_tensor(em[:, 0], phi[:, L, 0], lead(pend[:, 0], 2), ALU.mult)
                V.tensor_tensor(em[:, 1], phi[:, L, 1], lead(pend[:, 1], 2), ALU.mult).then_inc(em_ready.sem, 1)

                def output_factors(g):
                    nr_ready.wait(dve, u, g + 2)
                    link(V.tensor_scalar(nre[:, g], nr[:, g], EPS_BC * SV * SW, None, ALU.add))
                    link(V.reciprocal(rn[:, g], nre[:, g]))
                    hs = slice(J * g, J * g + J)
                    link(V.tensor_tensor(fc4[:, g], nre[:, g, :, 0], rn[:, g, :, 1], ALU.mult))
                    if g >= 2:
                        fbs_ready.wait(dve, u, G + g - 1)
                    V.tensor_tensor(fct[:, g % 2], spread(fc4[:, g], N), spread(ptok[:, 1, :, hs], N), ALU.mult) \
                        .then_inc(fct_ready.sem, 1)

                def output_side(g):
                    bcs_ready.wait(dve, u, G + g + 1)
                    fbs_ready.wait(dve, u, G + g + 1)
                    V.tensor_tensor(bcs[:, g % 2, 0, :], bcs[:, g % 2, 0, :], pinv[:, g, :], ALU.mult)
                    link(V.tensor_tensor(fbs[:, g % 2, :], pinv[:, g, :], fbs[:, g % 2, :], ALU.mult))
                    link(V.tensor_tensor(bcs[:, g % 2, 1, :], bcs[:, g % 2, 1, :], fbs[:, g % 2, :], ALU.mult))
                    if g >= 3:
                        y_ready.wait(dve, u, g - 2)
                    V.tensor_tensor(both(ct[:, g % 3]), rows(0, 1, g), cols(bcs[:, g % 2, 0, :]), ALU.mult)
                    link(V.tensor_tensor(both(m2), rows(1, 1, g), cols(bcs[:, g % 2, 1, :]), ALU.mult))
                    V.tensor_tensor(ct[:, g % 3], ct[:, g % 3], m2[:], ALU.add).then_inc(ct_ready.sem, 1)
                    ct_ready.wait(dve, u, g + 1)

                def mask(g):
                    k_ready.wait(dve, u, g + 1)
                    if g == 0:
                        h_ready.wait(dve, u, h_ready.per)
                    if g >= 2:
                        y_ready.wait(dve, u, g - 1)
                    V.tensor_tensor(km[:, g % 2], kp[:, :, 0:TT * L].rearrange("p j (a t) -> p j a t", a=TT),
                                    lead(causal[:], TT).unsqueeze(1).broadcast_to([P, J, TT, L]), ALU.mult) \
                        .then_inc(km_ready.sem, 1)

                def scale_out(g):
                    y_ready.wait(dve, u, g + 1)
                    if g >= 2:
                        yg_ready.wait(dve, u, 3 * (g - 1))
                    V.tensor_tensor(ysc[:, g % 2].rearrange("p a (j e) -> p a j e", j=J),
                                    yp[:].rearrange("p a (j e) -> p a j e", j=J), spread(rn[:, g, :, 0], DH),
                                    ALU.mult).then_inc(ysc_ready.sem, 1)

                for s in range(G + 3):
                    if 1 <= s <= G:
                        output_side(s - 1)
                    if s < G:
                        output_factors(s)
                    if 2 <= s <= G + 1:
                        mask(s - 2)
                    if s >= 3:
                        scale_out(s - 3)
                x_in.wait(dve, u, 16)
                o_ready.wait(dve, u, TT)
                V.tensor_tensor(x1s[:], kp[:, 0:TT, 0:DM], x1s[:], ALU.add).then_inc(x1_ready.sem, 1)


def attention(nc, d, x, x1):
    st = {k: nc.dram_tensor(k + "_scratch", shape, dt).ap() for k, shape, dt in (
        ("raw", (2, B, H, T), F32), ("sg", (NTOK, DI), F32), ("vtok", (NTOK, DI), F32),
        ("vhl", (NU, P, 2, 4, UT), F16), ("whl", (P, 2, 4, H * 4 * N), F16),
        ("q4", (NU, 4, H, UT), F32), ("qend", (NU, H, CH), F32), ("ptok", (NU, P, 3, TT, H), F32))}
    projections(nc, d, x, st)
    parameters(nc, d, st)
    mixer(nc, d, st, x, x1)


SK, DC = 77, 192
DQ = DM // 16
XT = T // P
NE, NX, FF = 15, 17, 512


def cross_ring():
    tiles = [("kT",), ("v",)] + [("xT", i) for i in range(XT // 2)]
    tiles += [("qT", m, i) for m in range(2) for i in range(T // 512)]
    for s in range(XT + 3):
        if 1 <= s <= XT:
            tiles.append(("O", s - 1))
        if 2 <= s <= XT + 1:
            tiles.append(("oT", s - 2))
        if s >= 3:
            tiles.append(("out", s - 3))
    return tiles


XRING = cross_ring()
XIDX = {k: i for i, k in enumerate(XRING)}
assert len(XRING) % 2 == 0


def cross_attention(nc, d, x1, xres):
    with ExitStack() as ctx:
        def sb(name, shape):
            return ctx.enter_context(nc.sbuf_tensor("x_" + name, shape, F32))

        def ps(name, shape):
            return ctx.enter_context(nc.psum_tensor("xp_" + name, shape, F32))

        def sem(name):
            return ctx.enter_context(nc.semaphore("x_" + name))

        ident = sb("ident", [P, P])
        parity = sb("parity", [P, 2])
        ones = sb("ones", [1, P])
        wq = sb("wq", [P, 2, DM])
        wo = sb("wo", [P, 2, DM])
        wka = sb("wka", [P, DM])
        wkb = sb("wkb", [DC - P, DM])
        wva = sb("wva", [P, DM])
        wvb = sb("wvb", [DC - P, DM])
        bq = sb("bq", [P, 2])
        bk = sb("bk", [P, 2])
        bv = sb("bv", [1, DM])
        bo = sb("bo", [1, DM])
        ca = sb("ca", [P, SK])
        cb = sb("cb", [DC - P, SK])
        kraw = sb("kraw", [P, 2, SK])
        kz = sb("kz", [P, 2, 2, SK])
        va = sb("va", [SK, 16, DQ + 1])
        epsln = sb("epsln", [P, 1])
        bst = sb("bst", [P, XT, 6])
        mv = sb("mv", [P, XT, 2])
        std = sb("std", [P, XT])
        rstd = sb("rstd", [P, XT])
        xn = sb("xn", [P, XT, DM])
        xnt = sb("xnt", [P, 2, T])
        qt = sb("qt", [P, 2, T])
        mx = sb("mx", [P, 2, 4, 4])
        s_sb = sb("s", [P, 2, 16, SK])
        pt = sb("pt", [SK, 2, 16, P])
        rec = sb("rec", [P, 16])
        osb = sb("o", [P, 2, DM])
        ot = sb("ot", [P, 2, 2, P])

        ring = ps("ring", [P, 2, 512])
        sp_ = ps("scores", [P, 4, 512])
        ptp = ps("pt", [P, 2, 512])

        w_loaded = sem("w_loaded")
        NW = 13
        eps_ready = sem("eps_ready")
        x_in = Signal(sem("x_in"), 16)
        c_in = Signal(sem("c_in"), 32)
        ring_full = Signal(sem("ring_full"), len(XRING))
        mv_ready = Signal(sem("mv_ready"), 1)
        std_ready = Signal(sem("std_ready"), 1)
        bst_ready = sem("bst_ready")
        rstd_ready = Signal(sem("rstd_ready"), 1)
        xn_ready = Signal(sem("xn_ready"), XT)
        xnt_ready = Signal(sem("xnt_ready"), XT // 2)
        kraw_ready = Signal(sem("kraw_ready"), 2)
        kz_ready = Signal(sem("kz_ready"), 2)
        va_ready = Signal(sem("va_ready"), 1)
        qt_ready = Signal(sem("qt_ready"), 4)
        s_full = Signal(sem("s_full"), XT)
        mx_ready = Signal(sem("mx_ready"), XT)
        s_ready = Signal(sem("s_ready"), XT)
        pt_full = Signal(sem("pt_full"), 4 * XT)
        pt_ready = Signal(sem("pt_ready"), 4 * XT)
        rec_ready = Signal(sem("rec_ready"), XT)
        o_ready = Signal(sem("o_ready"), XT)
        ot_ready = Signal(sem("ot_ready"), XT)
        x2_ready = Signal(sem("x2_ready"), XT)
        kv_taken = Signal(sem("kv_taken"), 1)

        emptied = {("kT",): (kraw_ready, 2), ("v",): (va_ready, 1)}
        emptied |= {("xT", i): (xnt_ready, i + 1) for i in range(XT // 2)}
        emptied |= {("qT", m, i): (qt_ready, 2 * m + i + 1) for m in range(2) for i in range(2)}
        for i in range(XT):
            emptied |= {("O", i): (o_ready, i + 1), ("oT", i): (ot_ready, i + 1), ("out", i): (x2_ready, i + 1)}

        x1v = x1.rearrange("(n p) m -> p n m", p=P)
        block = ctx.enter_context(nc.Block())

        @block.sync
        def _(sp):
            for dst, src in (
                    (ident[:], d["ident"]), (parity[:], d["parity"]), (ones[:], d["onesrow"]),
                    (wq[:], d["wq"].rearrange("(k p) o -> p k o", p=P)),
                    (wo[:], d["wo"].rearrange("(k p) o -> p k o", p=P)),
                    (wka[:], d["wk"][0:P]), (wkb[:], d["wk"][P:DC]), (wva[:], d["wv"][0:P]), (wvb[:], d["wv"][P:DC]),
                    (bq[:], d["bq"]), (bk[:], d["bk"]), (bv[:], d["bv"]), (bo[:], d["bo"])):
                sp.dma_start(dst, src).then_inc(w_loaded, 16)
            sp.sem_inc(kv_taken.sem, 1)
            with sp.Fori(0, B) as b:
                kv_taken.wait(sp, b, 1)
                sp.dma_start(xres[:, bass.ds(b * XT, XT), :], x1v[:, bass.ds(b * XT, XT), :]).then_inc(x_in.sem, 16)
                sp.dma_start(ca[:], d["ctxT"][bass.ds(b, 1), 0:P].rearrange("a p s -> p (a s)")).then_inc(c_in.sem, 16)
                sp.dma_start(cb[:], d["ctxT"][bass.ds(b, 1), P:DC].rearrange("a p s -> p (a s)")) \
                    .then_inc(c_in.sem, 16)

        @block.tensor
        def _(pe):
            pe.wait_ge(w_loaded, 16 * NW)
            pe.wait_ge(eps_ready, 2)
            with pe.Fori(0, B) as b:
                def put(key):
                    i = XIDX[key]
                    if i >= 2:
                        sig, k = emptied[XRING[i - 2]]
                        sig.wait(pe, b, k)
                    return ring[:, i % 2, :]

                c_in.wait(pe, b, 32)
                o = put(("kT",))
                for m in range(2):
                    for k, (w, c) in enumerate(((wka, ca), (wkb, cb))):
                        mm = pe.matmul(o[:, m * SK:(m + 1) * SK], w[:, m * P:(m + 1) * P], c[:],
                                       start=(k == 0), stop=(k == 1))
                mm.then_inc(ring_full.sem, 1)
                o = put(("v",))
                pe.matmul(o[0:SK, 0:DM], ca[:], wva[:], start=True, stop=False)
                pe.matmul(o[0:SK, 0:DM], cb[:], wvb[:], start=False, stop=False)
                pe.matmul(o[0:SK, 0:DM], ones[:, 0:SK], bv[:], start=False, stop=True).then_inc(ring_full.sem, 1)
                for i in range(XT // 2):
                    xn_ready.wait(pe, b, 2 * i + 2)
                    o = put(("xT", i))
                    for k in range(2):
                        for a in range(2):
                            mm = pe.transpose(o[:, (2 * k + a) * P:(2 * k + a + 1) * P],
                                              xn[:, 2 * i + a, k * P:(k + 1) * P], ident[:])
                    mm.then_inc(ring_full.sem, 1)
                for m in range(2):
                    for i in range(2):
                        xnt_ready.wait(pe, b, 2 * i + 2)
                        o = put(("qT", m, i))
                        for k in range(2):
                            mm = pe.matmul(o, wq[:, k, m * P:(m + 1) * P], xnt[:, k, 512 * i:512 * (i + 1)],
                                           start=(k == 0), stop=(k == 1))
                        mm.then_inc(ring_full.sem, 1)
                qt_ready.wait(pe, b, 4)
                kz_ready.wait(pe, b, 2)
                va_ready.wait(pe, b, 1)
                for s in range(XT + 3):
                    if s < XT:
                        if s > 0:
                            s_ready.wait(pe, b, s)
                        for q in range(4):
                            for r in range(4):
                                m, par = q // 2, q % 2
                                rr = slice(32 * r, 32 * r + 32)
                                mm = pe.matmul(sp_[:, r, q * SK:(q + 1) * SK], qt[rr, m, s * P:(s + 1) * P],
                                               kz[rr, m, par, :], start=True, stop=True)
                        mm.then_inc(s_full.sem, 1)
                    if 1 <= s <= XT:
                        i = s - 1
                        s_ready.wait(pe, b, i + 1)
                        for q in range(4):
                            n = 4 * i + q
                            if q >= 2:
                                pt_ready.wait(pe, b, n - 1)
                            for h in range(4):
                                mm = pe.transpose(ptp[0:SK, q % 2, h * P:(h + 1) * P], s_sb[:, i % 2, 4 * q + h, :],
                                                  ident[:])
                            mm.then_inc(pt_full.sem, 1)
                        o = put(("O", i))
                        for q in range(4):
                            pt_ready.wait(pe, b, 4 * i + q + 1)
                            for h in range(4 * q, 4 * q + 4):
                                mm = pe.matmul(o[:, h * (DQ + 1):(h + 1) * (DQ + 1)], pt[:, i % 2, h, :], va[:, h, :],
                                               start=True, stop=True)
                        mm.then_inc(ring_full.sem, 1)
                    if 2 <= s <= XT + 1:
                        i = s - 2
                        o_ready.wait(pe, b, i + 1)
                        o = put(("oT", i))
                        for k in range(2):
                            mm = pe.transpose(o[:, k * P:(k + 1) * P], osb[:, i % 2, k * P:(k + 1) * P], ident[:])
                        mm.then_inc(ring_full.sem, 1)
                    if s >= 3:
                        i = s - 3
                        ot_ready.wait(pe, b, i + 1)
                        o = put(("out", i))
                        for k in range(2):
                            pe.matmul(o[:, 0:DM], ot[:, i % 2, k, :], wo[:, k, :], start=(k == 0), stop=False)
                        pe.matmul(o[:, 0:DM], ones[:], bo[:], start=False, stop=True).then_inc(ring_full.sem, 1)
                x2_ready.wait(pe, b, XT)

        @block.scalar
        def _(act):
            act.wait_ge(w_loaded, 16 * NW)
            act.wait_ge(eps_ready, 2)
            with act.Fori(0, B) as b:
                def take(key):
                    i = XIDX[key]
                    ring_full.wait(act, b, i + 1)
                    return ring[:, i % 2, :]

                o = take(("kT",))
                for m in range(2):
                    nc.scalar.activation(kraw[:, m, :], o[:, m * SK:(m + 1) * SK], ACT.Identity,
                                         bias=bk[:, m:m + 1]).then_inc(kraw_ready.sem, 1)
                o = take(("v",))
                nc.scalar.copy(va[:, :, 0:DQ], o[0:SK, 0:DM].rearrange("p (h e) -> p h e", h=16)) \
                    .then_inc(va_ready.sem, 1)
                mv_ready.wait(act, b, 1)
                nc.scalar.activation(std[:], mv[:, :, 1], ACT.Sqrt, bias=epsln[:, 0:1]).then_inc(std_ready.sem, 1)
                for i in range(XT // 2):
                    o = take(("xT", i))
                    nc.scalar.copy(xnt[:, :, 256 * i:256 * (i + 1)], o.rearrange("p (k t) -> p k t", k=2)) \
                        .then_inc(xnt_ready.sem, 1)
                for m in range(2):
                    for i in range(2):
                        o = take(("qT", m, i))
                        nc.scalar.activation(qt[:, m, 512 * i:512 * (i + 1)], o, ACT.Identity, bias=bq[:, m:m + 1]) \
                            .then_inc(qt_ready.sem, 1)
                for s in range(XT + 2):
                    if 1 <= s <= XT:
                        i = s - 1
                        for q in range(4):
                            pt_full.wait(act, b, 4 * i + q + 1)
                            if q == 0 and i >= 2:
                                ring_full.wait(act, b, XIDX[("O", i - 2)] + 1)
                            nc.scalar.activation(pt[:, i % 2, 4 * q:4 * q + 4, :],
                                                 ptp[0:SK, q % 2, :].rearrange("p (h t) -> p h t", h=4),
                                                 ACT.Exp, scale=DQ ** -0.5).then_inc(pt_ready.sem, 1)
                    if s >= 2:
                        i = s - 2
                        o = take(("oT", i))
                        nc.scalar.copy(ot[:, i % 2], o[:, 0:2 * P].rearrange("p (k t) -> p k t", k=2)) \
                            .then_inc(ot_ready.sem, 1)

        @block.vector
        def _(dve):
            V = nc.vector
            V.memset(epsln[:], EPS_LN).then_inc(eps_ready, 1)
            V.memset(va[:], 1.0).then_inc(eps_ready, 1)
            dve.wait_ge(w_loaded, 16 * NW)
            with dve.Fori(0, B) as b:
                dve.sem_clear(bst_ready)
                x_in.wait(dve, b, 16)
                for i in range(XT):
                    ins = V.bn_stats(bst[:, i, :], xres[:, bass.ds(b * XT + i, 1), :].rearrange("p a m -> p (a m)"))
                ins.then_inc(bst_ready, 1)
                dve.wait_ge(bst_ready, 1)
                for i in range(XT):
                    ins = V.bn_aggr(mv[:, i, :], bst[:, i, :])
                ins.then_inc(mv_ready.sem, 1)
                std_ready.wait(dve, b, 1)
                V.reciprocal(rstd[:], std[:]).then_inc(rstd_ready.sem, 1)
                rstd_ready.wait(dve, b, 1)
                for i in range(XT):
                    V.tensor_scalar(xn[:, i, :], xres[:, bass.ds(b * XT + i, 1), :].rearrange("p a m -> p (a m)"),
                                    mv[:, i, 0:1], rstd[:, i:i + 1], ALU.subtract, ALU.mult).then_inc(xn_ready.sem, 1)
                kraw_ready.wait(dve, b, 2)
                for par in range(2):
                    V.tensor_scalar(kz[:, :, par, :], kraw[:], parity[:, par:par + 1], None, ALU.mult) \
                        .then_inc(kz_ready.sem, 1)
                for s in range(XT + 3):
                    if s < XT:
                        s_full.wait(dve, b, s + 1)
                        sc = sp_[:, :, 0:4 * SK].rearrange("p r (q k) -> p r q k", q=4)
                        V.tensor_reduce(mx[:, s % 2], sc, AX.X, ALU.max).then_inc(mx_ready.sem, 1)
                        mx_ready.wait(dve, b, s + 1)
                        V.tensor_tensor(s_sb[:, s % 2].rearrange("p (r q) k -> p r q k", r=4), sc,
                                        mx[:, s % 2].unsqueeze(3).broadcast_to([P, 4, 4, SK]), ALU.subtract) \
                            .then_inc(s_ready.sem, 1)
                    if 1 <= s <= XT:
                        i = s - 1
                        ring_full.wait(dve, b, XIDX[("O", i)] + 1)
                        o = ring[:, XIDX[("O", i)] % 2, 0:16 * (DQ + 1)].rearrange("p (h e) -> p h e", h=16)
                        V.reciprocal(rec[:], o[:, :, DQ]).then_inc(rec_ready.sem, 1)
                        rec_ready.wait(dve, b, i + 1)
                        V.tensor_tensor(osb[:, i % 2].rearrange("p (h e) -> p h e", h=16), o[:, :, 0:DQ],
                                        rec[:].unsqueeze(2).broadcast_to([P, 16, DQ]), ALU.mult) \
                            .then_inc(o_ready.sem, 1)
                    if s >= 3:
                        i = s - 3
                        ring_full.wait(dve, b, XIDX[("out", i)] + 1)
                        xr = xres[:, bass.ds(b * XT + i, 1), :].rearrange("p a m -> p (a m)")
                        V.tensor_tensor(xr, ring[:, XIDX[("out", i)] % 2, 0:DM], xr, ALU.add).then_inc(x2_ready.sem, 1)

        @block.gpsimd
        def _(pool):
            with pool.Fori(0, B) as b:
                ring_full.wait(pool, b, 2)
                pool.sem_inc(kv_taken.sem, 1)


def experts(nc, d, xres, out):
    with ExitStack() as ctx:
        def sb(name, shape):
            return ctx.enter_context(nc.sbuf_tensor("f_" + name, shape, F32))

        def ps(name, shape):
            return ctx.enter_context(nc.psum_tensor("fp_" + name, shape, F32))

        def sem(name):
            return ctx.enter_context(nc.semaphore("f_" + name))

        NB = NTOK // 512
        ident = sb("ident", [P, P])
        ones = sb("ones", [1, P])
        gw = sb("gw", [P, 2, NE])
        gb = sb("gb", [1, NE])
        b1 = sb("b1", [P, 2, 4])
        b2 = sb("b2", [NX, DM])
        w1 = sb("w1", [P, 2, 2, FF])
        w2 = sb("w2", [P, 2, 4, DM])
        epsln = sb("epsln", [P, 1])
        bst = sb("bst", [P, NT, 6])
        mv = sb("mv", [P, NT, 2])
        std = sb("std", [P, NT])
        rstd = sb("rstd", [P, NT])
        xn = sb("xn", [P, 2, DM])
        xnt = sb("xnt", [P, 2, NTOK])
        lg = sb("lg", [P, NT, NE])
        nmx = sb("nmx", [P, NT])
        sm = sb("sm", [P, NT])
        pr = sb("pr", [P, 2, 24])
        top = sb("top", [P, 8])
        rest = sb("rest", [P, 24])
        gate = sb("gate", [P, NT, NX])
        gt = sb("gt", [NX, 2, P])
        hT = sb("hT", [P, 2, 4, 512])
        hp = ps("h", [P, 4, 512])
        yp = ps("y", [P, 4, 512])

        w_loaded = sem("w_loaded")
        mv_ready = sem("mv_ready")
        std_ready = sem("std_ready")
        rstd_ready = sem("rstd_ready")
        eps_ready = sem("eps_ready")
        xn_ready = sem("xn_ready")
        xt_full = sem("xt_full")
        xnt_ready = sem("xnt_ready")
        lg_full = sem("lg_full")
        lg_ready = sem("lg_ready")
        prob_ready = sem("prob_ready")
        step = sem("step")
        nmx_ready = sem("nmx_ready")
        gate_ready = sem("gate_ready")
        gt_full = sem("gt_full")
        gt_ready = sem("gt_ready")
        acc_ready = sem("acc_ready")
        b2_full = sem("b2_full")
        w_in = [sem(f"w_in{i}") for i in range(2)]
        h_full = sem("h_full")
        h_ready = sem("h_ready")
        y_full = sem("y_full")
        y_used = sem("y_used")
        stored = sem("stored")
        NW = 5

        block = ctx.enter_context(nc.Block())

        @block.sync
        def _(sp):
            for dst, src in ((ident[:], d["ident"]), (ones[:], d["onesrow"]),
                             (gw[:], d["gW"].rearrange("(k p) e -> p k e", p=P)), (gb[:], d["gb"]),
                             (b2[:], d["b2"])):
                sp.dma_start(dst, src).then_inc(w_loaded, 16)

            def load(e, par):
                sp.dma_start(w1[:, par], d["W1"][bass.ds(e, 1)].rearrange("a (k p) f -> p (a k) f", p=P)) \
                    .then_inc(w_in[par], 16)
                sp.dma_start(w2[:, par], d["W2"][bass.ds(e, 1)].rearrange("a (k p) f -> p (a k) f", p=P)) \
                    .then_inc(w_in[par], 16)
                sp.dma_start(b1[:, par], d["b1"][bass.ds(e, 1)].rearrange("a p f -> p (a f)")).then_inc(w_in[par], 16)

            load(0, 0)
            load(1, 1)
            with sp.Fori(0, 7) as i:
                for par in range(2):
                    sp.wait_ge(y_full, (2 * i + par + 1) * (2 * NB) + 4)
                    load(2 * i + par + 2, par)
            sp.wait_ge(y_full, 15 * 2 * NB + 4)
            load(16, 0)
            sp.wait_ge(y_used, NX * 2 * NB + 4)
            sp.dma_start(out.rearrange("(n p) m -> p n m", p=P), xres[:]).then_inc(stored, 16)
            sp.wait_ge(stored, 16)

        def all_experts(eng, body):
            with eng.Fori(0, 8) as i:
                for par in range(2):
                    body(2 * i + par, par, i)
            body(16, 0, 8)

        @block.tensor
        def _(pe):
            pe.wait_ge(w_loaded, 16 * NW)
            for i in range(NT):
                pe.wait_ge(xn_ready, i + 1)
                if i >= 2:
                    pe.wait_ge(xnt_ready, i - 1)
                for k in range(2):
                    mm = pe.transpose(hp[:, i % 2, k * P:(k + 1) * P], xn[:, i % 2, k * P:(k + 1) * P], ident[:])
                mm.then_inc(xt_full, 1)
            for i in range(NT):
                pe.wait_ge(xnt_ready, i + 1)
                if i >= 2:
                    pe.wait_ge(lg_ready, i - 1)
                o = yp[:, i % 2, 0:NE]
                for k in range(2):
                    pe.matmul(o, xnt[:, k, i * P:(i + 1) * P], gw[:, k, :], start=(k == 0), stop=False)
                pe.matmul(o, ones[:], gb[:], start=False, stop=True).then_inc(lg_full, 1)
            for i in range(NT + 1):
                if i < NT:
                    pe.wait_ge(gate_ready, i + 1)
                    if i >= 2:
                        pe.wait_ge(gt_ready, i - 1)
                    pe.transpose(hp[0:NX, i % 2, 0:P], gate[:, i, :], ident[:]).then_inc(gt_full, 1)
                if i >= 1:
                    pe.wait_ge(gt_ready, i)
                    if i >= 3:
                        pe.wait_ge(acc_ready, i - 2)
                    pe.matmul(yp[:, 2 + (i - 1) % 2, 0:DM], gt[:, (i - 1) % 2, :], b2[:], start=True, stop=True) \
                        .then_inc(b2_full, 1)
            pe.wait_ge(acc_ready, NT)
            pe.sem_inc(y_full, 4)

            def expert(e, par, k_e):
                pe.wait_ge(w_in[par], 48 * k_e + 48)
                for nb in range(NB + 1):
                    if nb < NB:
                        for f in range(4):
                            pe.wait_ge(h_ready, (e * NB + nb) * 4 + f + 1)
                            for k in range(2):
                                mm = pe.matmul(hp[:, f, :], w1[:, par, k, f * P:(f + 1) * P],
                                               xnt[:, k, nb * 512:(nb + 1) * 512], start=(k == 0), stop=(k == 1))
                            mm.then_inc(h_full, 1)
                    if nb >= 1:
                        q = nb - 1
                        pe.wait_ge(h_ready, (e * NB + q) * 4 + 8)
                        for a in range(4):
                            if a % 2 == 0:
                                pe.wait_ge(y_used, (e * NB + q) * 2 + a // 2 + 1)
                            for f in range(4):
                                mm = pe.matmul(yp[:, 2 * (q % 2) + a // 2, (a % 2) * DM:(a % 2 + 1) * DM],
                                               hT[:, q % 2, f, a * P:(a + 1) * P], w2[:, par, f, :],
                                               start=(f == 0), stop=(f == 3))
                            if a % 2 == 1:
                                mm.then_inc(y_full, 1)

            all_experts(pe, expert)

        @block.scalar
        def _(act):
            act.wait_ge(mv_ready, 1)
            nc.scalar.activation(std[:], mv[:, :, 1], ACT.Sqrt, bias=epsln[:, 0:1]).then_inc(std_ready, 1)
            act.wait_ge(w_loaded, 16 * NW)
            for i in range(NT):
                act.wait_ge(xt_full, i + 1)
                nc.scalar.copy(xnt[:, :, i * P:(i + 1) * P], hp[:, i % 2, 0:2 * P].rearrange("p (k t) -> p k t", k=2)) \
                    .then_inc(xnt_ready, 1)
            for i in range(NT):
                act.wait_ge(lg_full, i + 1)
                nc.scalar.copy(lg[:, i, :], yp[:, i % 2, 0:NE]).then_inc(lg_ready, 1)
            act.wait_ge(nmx_ready, 1)

            def gates_out(i):
                act.wait_ge(gt_full, i + 1)
                if i >= 2:
                    act.wait_ge(b2_full, i - 1)
                nc.scalar.copy(gt[:, i % 2, :], hp[0:NX, i % 2, 0:P]).then_inc(gt_ready, 1)

            for i in range(NT):
                if i >= 2:
                    act.wait_ge(gate_ready, i - 1)
                nc.scalar.activation(pr[:, i % 2, 0:NE], lg[:, i, :], ACT.Exp, bias=nmx[:, i:i + 1],
                                     accum_out=sm[:, i:i + 1]).then_inc(prob_ready, 1)
                if i >= 1:
                    gates_out(i - 1)
            gates_out(NT - 1)
            act.sem_inc(h_ready, 4)

            def expert(e, par, k_e):
                for nb in range(NB):
                    act.wait_ge(y_full, (e * NB + nb) * 2 + 2)
                    for f in range(4):
                        act.wait_ge(h_full, (e * NB + nb) * 4 + f + 1)
                        nc.scalar.activation(hT[:, nb % 2, f, :], hp[:, f, :], ACT.Gelu,
                                             bias=b1[:, par, f:f + 1]).then_inc(h_ready, 1)

            all_experts(act, expert)

        @block.vector
        def _(dve):
            V = nc.vector
            chain = [0]

            def link(ins):
                chain[0] += 1
                ins.then_inc(step, 1)
                dve.wait_ge(step, chain[0])

            V.memset(pr[:], -1.0)
            V.memset(gate[:], 1.0)
            link(V.memset(epsln[:], EPS_LN))
            for i in range(NT):
                ins = V.bn_stats(bst[:, i, :], xres[:, i, :])
            link(ins)
            for i in range(NT):
                ins = V.bn_aggr(mv[:, i, :], bst[:, i, :])
            ins.then_inc(mv_ready, 1)
            dve.wait_ge(std_ready, 1)
            link(V.reciprocal(rstd[:], std[:]))
            for i in range(NT):
                if i >= 2:
                    dve.wait_ge(xt_full, i - 1)
                V.tensor_scalar(xn[:, i % 2, :], xres[:, i, :], mv[:, i, 0:1], rstd[:, i:i + 1],
                                ALU.subtract, ALU.mult).then_inc(xn_ready, 1)
                dve.wait_ge(xn_ready, i + 1)
                ins = V.tensor_tensor(xres[:, i, :], xres[:, i, :], xn[:, i % 2, :], ALU.add)
            link(ins)
            dve.wait_ge(lg_ready, NT)
            link(V.tensor_reduce(nmx[:], lg[:], AX.X, ALU.max))
            V.tensor_scalar(nmx[:], nmx[:], -1.0, None, ALU.mult).then_inc(nmx_ready, 1)
            for i in range(NT + 1):
                if i < NT:
                    dve.wait_ge(prob_ready, i + 1)
                    link(V.reciprocal(sm[:, i:i + 1], sm[:, i:i + 1]))
                    link(V.tensor_scalar(pr[:, i % 2, 0:NE], pr[:, i % 2, 0:NE], sm[:, i:i + 1], None, ALU.mult))
                    link(V.max(top[:], pr[:, i % 2, :]))
                    link(V.memset(top[:, 3:8], -1.0))
                    link(V.match_replace(rest[:], top[:], pr[:, i % 2, :], 0.0))
                    V.tensor_tensor(gate[:, i, 0:NE], pr[:, i % 2, 0:NE], rest[:, 0:NE], ALU.subtract) \
                        .then_inc(gate_ready, 1)
                if i >= 1:
                    dve.wait_ge(b2_full, i)
                    V.tensor_tensor(xres[:, i - 1, :], yp[:, 2 + (i - 1) % 2, 0:DM], xres[:, i - 1, :], ALU.add) \
                        .then_inc(acc_ready, 1)
            dve.wait_ge(gate_ready, NT)
            dve.sem_inc(y_used, 4)

            def expert(e, par, k_e):
                for nb in range(NB):
                    for half in range(2):
                        n2 = (e * NB + nb) * 2 + half
                        dve.wait_ge(y_full, n2 + 5)
                        dve.wait_ge(y_used, n2 + 1)
                        for a in range(2):
                            i = nb * 4 + half * 2 + a
                            ins = V.scalar_tensor_tensor(
                                xres[:, i, :], yp[:, 2 * (nb % 2) + half, a * DM:(a + 1) * DM],
                                gate[:, i, bass.ds(e, 1)], xres[:, i, :], ALU.mult, ALU.add)
                        ins.then_inc(y_used, 1)

            all_experts(dve, expert)


def program(nc, d, out, stage=3):
    x1 = nc.dram_tensor("x1_scratch", (NTOK, DM), F32).ap() if stage > 1 else out
    attention(nc, d, d["x"].rearrange("b t m -> (b t) m"), x1)
    if stage > 1:
        with nc.sbuf_tensor("xres", [P, NT, DM], F32) as xres:
            cross_attention(nc, d, x1, xres)
            experts(nc, d, xres, out)


def layouts(inputs):
    r = {"x": inputs["x"]}
    w = np.asarray(inputs["L0_attn_W_in"])
    order = np.concatenate([np.arange(2 * DI), 2 * DI + 2 * np.arange(H), 2 * DI + 2 * np.arange(H) + 1])
    r["W_in"] = w[order].T
    w = np.asarray(inputs["L0_attn_W_bc"]).reshape(G, J, 4, N, DI)
    r["W_bc"] = w.transpose(0, 2, 1, 3, 4).reshape(H * 4 * N, DI).T
    r["W_out"] = np.asarray(inputs["L0_attn_W_out"]).T
    r["conv_bias"] = np.asarray(inputs["L0_attn_dw_bias"]).reshape(4, P).T
    r["A_states"] = np.asarray(inputs["L0_attn_A_log"]).reshape(G, J * N).T
    for k in ("dw_weight", "skip", "A_log", "dt_bias"):
        r[k] = inputs["L0_attn_" + k]
    r["dt_bias_b"] = np.tile(np.asarray(inputs["L0_attn_dt_bias"]), B)[:, None]
    r["ctxT"] = np.asarray(inputs["ctx_768"]).transpose(0, 2, 1)
    heads = np.array([8 * (q // 2) + 2 * row + q % 2 for row in range(4) for q in range(4)])
    cols = (heads[:, None] * DQ + np.arange(DQ)[None]).reshape(-1)
    for k in ("wq", "wk"):
        r[k] = inputs["L0_xattn_" + k]
    r["wv"] = np.asarray(inputs["L0_xattn_wv"])[:, cols]
    r["bv"] = np.asarray(inputs["L0_xattn_bv"])[cols][None]
    r["wo"] = np.asarray(inputs["L0_xattn_wo"])[cols]
    r["bo"] = np.asarray(inputs["L0_xattn_bo"])[None]
    for k in ("bq", "bk"):
        r[k] = np.asarray(inputs["L0_xattn_" + k]).reshape(2, P).T
    ffn = {k[7:]: np.asarray(v) for k, v in inputs.items() if k.startswith("L0_ffn_")}
    r["gW"], r["gb"] = ffn["gW"], ffn["gb"][None]
    sw1 = ffn["sW1"][0].reshape(DM, 2, FF).transpose(1, 0, 2)
    r["W1"] = np.concatenate([ffn["rW1"], sw1])
    r["W2"] = np.concatenate([ffn["rW2"], ffn["sW2"][0].reshape(2, FF, DM)])
    r["b1"] = np.concatenate([ffn["rb1"], ffn["sb1"][0].reshape(2, FF)]).reshape(NX, 4, P).transpose(0, 2, 1)
    r["b2"] = np.concatenate([ffn["rb2"], ffn["sb2"], np.zeros((1, DM), np.float32)])
    r.update(constants())
    return {k: np.ascontiguousarray(v) for k, v in r.items()}


def kernel(**inputs):
    import numpy as _np
    import concourse.bacc as _bacc
    from concourse import mybir as _mybir
    from concourse.bass_utils import run_bass_kernel_spmd as _run

    nc = _bacc.Bacc("TRN2", target_bir_lowering=False, num_devices=1)
    arrays, args = {}, {}
    for name, a in layouts(inputs).items():
        arrays[f"in_{name}_dram"] = a
        args[name] = nc.dram_tensor(f"in_{name}_dram", a.shape, _mybir.dt.from_np(a.dtype), kind="ExternalInput").ap()
    out = nc.dram_tensor("out_0_dram", (B, T, DM), F32, kind="ExternalOutput").ap()
    program(nc, args, out.rearrange("b t m -> (b t) m"))
    r = _run(nc, [arrays], core_ids=[0])
    return r.results[0]["out_0_dram"]
```

```python
from contextlib import ExitStack

import numpy as np

import concourse.bass as bass
from concourse import mybir

F32 = mybir.dt.float32
I32 = mybir.dt.int32
ALU = mybir.AluOpType
ACT = mybir.ActivationFunctionType
AX = mybir.AxisListType

P = 128
B, T, DM = 4, 1024, 256
NTOK = B * T
DI, H, N, DH = 512, 32, 32, 16
KCONV = 4
L = 64
CH = 4
UT = CH * L
NU = NTOK // UT
TT = UT // P
NT = NTOK // P
UPB = T // UT
G, J = 8, 4
LANES = G * CH
EPS_LN, EPS_BC = 1e-5, 1e-8
DT_MIN, DT_MAX, Y_MAX = 1e-4, 0.1, 0.106


class Signal:

    def __init__(self, sem, per):
        self.sem, self.per = sem, per

    def wait(self, eng, u, k):
        eng.wait_ge(self.sem, k if u is None else u * self.per + k)


def constants():
    c = {}
    c["ident"] = np.eye(P, dtype=np.float32)
    jn = np.arange(P) // N
    c["sel4"] = (jn[:, None] == np.arange(J)[None]).astype(np.float32)
    c["blockd"] = (jn[:, None] == (np.arange(J * DH) // DH)[None]).astype(np.float32)
    h = np.arange(64) % H
    c["selh"] = (h[:, None, None] == (np.arange(G)[:, None] * J + jn[None])[None]).astype(np.float32)
    c["causal"] = (np.arange(L)[None] >= (np.arange(P) % L)[:, None]).astype(np.float32)
    r = np.ones((P, 2 * CH * L), np.float32)
    r[:, ::L] = 0
    c["resetm"] = r
    c["contm"] = np.tile((np.arange(NU) % UPB != 0).astype(np.float32)[None], (P, 1))
    par = (np.arange(P) // 16) % 2
    c["parity"] = np.stack([par == 0, par == 1], 1).astype(np.float32)
    c["onesrow"] = np.ones((1, P), np.float32)
    c["allones"] = np.ones((P, P), np.float32)
    c["before"] = (np.arange(P)[:, None] < np.arange(P)[None]).astype(np.float32)
    c["thr"] = np.tile(np.arange(NTOK // RT, dtype=np.float32)[None] * RT, (P, 1))
    c["tids"] = np.arange(NRT + 2, dtype=np.float32)[None]
    return c


PT = 512
NPASS = NTOK // PT
PA = PT // P
PBANKS = 5

PRING = [("xT", 0), ("xT", 1)] + [("val", m) for m in range(4)] + [("par",)]
PRING += [("gate", a) for a in range(PA)] + [("vt", a) for a in range(PA)]
PIDX = {k: i for i, k in enumerate(PRING)}
assert len(PRING) % PBANKS == 0


def projections(nc, d, x, st, wbc):
    with ExitStack() as ctx:
        def sb(name, shape, dt=F32):
            return ctx.enter_context(nc.sbuf_tensor("p_" + name, shape, dt))

        def ps(name, shape):
            return ctx.enter_context(nc.psum_tensor("pp_" + name, shape, F32))

        def sem(name):
            return ctx.enter_context(nc.semaphore("p_" + name))

        ident = sb("ident", [P, P])
        win = sb("win", [P, 2, 2 * DI + 2 * H])
        convw = sb("convw", [P, 4, KCONV])
        convb = sb("convb", [P, 4])
        epsln = sb("epsln", [P, 1])
        xt = sb("xt", [P, NT, DM])
        bst = sb("bst", [P, NT, 6])
        mv = sb("mv", [P, NT, 2])
        std = sb("std", [P, NT])
        rstd = sb("rstd", [P, NT])
        xn = sb("xn", [P, 2, PA, DM])
        xnt = sb("xnt", [P, 2, PT])
        vraw = sb("vraw", [P, 2, 4, PT + KCONV - 1])
        cv = sb("cv", [P, 4, PT])
        valt = sb("valt", [P, 2, 4, PT])
        vtok = sb("vtok", [P, 2, PA, DI])
        sg = sb("sg", [P, 2, PA, DI])
        rawp = sb("rawp", [2 * H, PT])
        ring = ps("ring", [P, PBANKS, 512])

        w_loaded = sem("w_loaded")
        NW = 4
        init_ready = sem("init_ready")
        x_in = sem("x_in")
        wbc_in = sem("wbc_in")
        stats_ready = sem("stats_ready")
        std_ready = sem("std_ready")
        ring_full = Signal(sem("ring_full"), len(PRING))
        xn_ready = Signal(sem("xn_ready"), 1)
        xnt_ready = Signal(sem("xnt_ready"), 2)
        vraw_ready = Signal(sem("vraw_ready"), 4)
        raw_ready = Signal(sem("raw_ready"), 1)
        raw_out = Signal(sem("raw_out"), 32)
        sg_ready = Signal(sem("sg_ready"), PA)
        conv_ready = Signal(sem("conv_ready"), 4)
        valt_ready = Signal(sem("valt_ready"), 4)
        vtok_ready = Signal(sem("vtok_ready"), PA)
        stored = [Signal(sem(f"stored{i}"), 16 * 4) for i in range(2)]
        step = sem("step")

        emptied = {("par",): (raw_ready, 1)}
        for i in range(4):
            emptied |= {("xT", i): (xnt_ready, i + 1), ("val", i): (vraw_ready, i + 1),
                        ("gate", i): (sg_ready, i + 1)}

        def passes(eng, body):
            with eng.Fori(0, NPASS // 2) as i:
                for par in range(2):
                    body(2 * i + par, par, i)

        block = ctx.enter_context(nc.Block())

        @block.sync
        def _(sp):
            sp.dma_start(xt[:], x.rearrange("(n p) m -> p n m", p=P)).then_inc(x_in, 16)
            for dst, src in ((ident[:], d["ident"]), (win[:], d["W_in"].rearrange("(k p) o -> p k o", p=P)),
                             (convw[:], d["dw_weight"].rearrange("(k p) c -> p k c", p=P)),
                             (convb[:], d["conv_bias"])):
                sp.dma_start(dst, src).then_inc(w_loaded, 16)
            sp.dma_start(wbc[:], d["W_bc"].rearrange("(k p) (g c o) -> p k g c o", p=P, g=G, c=4)).then_inc(wbc_in, 16)

            def body(u, par, i):
                raw_ready.wait(sp, u, 1)
                for q in range(2):
                    sp.dma_start(st["raw"][q, bass.ds(i, 1), :, par * PT:(par + 1) * PT].rearrange("a h t -> h (a t)"),
                                 rawp[q * H:(q + 1) * H, :]).then_inc(raw_out.sem, 16)
                sg_ready.wait(sp, u, PA)
                sp.dma_start(st["sg"].rearrange("(u a p) m -> u p a m", a=PA, p=P)[u], sg[:, par]) \
                    .then_inc(stored[par].sem, 16)
                vtok_ready.wait(sp, u, 2 * PA)
                sp.dma_start(st["vtok"].rearrange("(u a p) m -> u p a m", a=PA, p=P)[u], vtok[:, par]) \
                    .then_inc(stored[par].sem, 16)
                valt_ready.wait(sp, u, 4)
                for v in range(2):
                    sp.dma_start(st["valt"][2 * u + v], valt[:, par, :, v * UT:(v + 1) * UT]) \
                        .then_inc(stored[par].sem, 16)

            passes(sp, body)
            for s in stored:
                sp.wait_ge(s.sem, 64 * (NPASS // 2) + 64)
            sp.wait_ge(raw_out.sem, 32 * NPASS + 32)
            sp.wait_ge(wbc_in, 16)

        @block.tensor
        def _(pe):
            pe.wait_ge(w_loaded, 16 * NW)

            def body(u, par, i):
                def put(key):
                    n = PIDX[key]
                    if n >= PBANKS:
                        sig, k = emptied[PRING[n - PBANKS]]
                        sig.wait(pe, u, k)
                    return ring[:, n % PBANKS, :]

                def full(ins):
                    ins.then_inc(ring_full.sem, 1)

                xn_ready.wait(pe, u, 1)
                vtok_ready.wait(pe, u, PA)
                for k in range(2):
                    o = put(("xT", k))
                    for a in range(PA):
                        mm = pe.transpose(o[:, a * P:(a + 1) * P], xn[:, par, a, k * P:(k + 1) * P], ident[:])
                    full(mm)
                xnt_ready.wait(pe, u, 2)
                for m in range(4):
                    o = put(("val", m))
                    for k in range(2):
                        mm = pe.matmul(o, win[:, k, DI + m * P:DI + (m + 1) * P], xnt[:, k, :],
                                       start=(k == 0), stop=(k == 1))
                    full(mm)
                o = put(("par",))
                for k in range(2):
                    mm = pe.matmul(o[0:2 * H, :], win[:, k, 2 * DI:2 * DI + 2 * H], xnt[:, k, :],
                                   start=(k == 0), stop=(k == 1))
                full(mm)
                for a in range(PA):
                    o = put(("gate", a))
                    for k in range(2):
                        mm = pe.matmul(o, xnt[:, k, a * P:(a + 1) * P], win[:, k, 0:DI],
                                       start=(k == 0), stop=(k == 1))
                    full(mm)
                valt_ready.wait(pe, u, 4)
                for a in range(PA):
                    o = put(("vt", a))
                    for k in range(4):
                        mm = pe.transpose(o[:, k * P:(k + 1) * P], valt[:, par, k, a * P:(a + 1) * P], ident[:])
                    full(mm)

            passes(pe, body)

        @block.scalar
        def _(act):
            act.wait_ge(stats_ready, 1)
            nc.scalar.activation(std[:], mv[:, :, 1], ACT.Sqrt, bias=epsln[:, 0:1]).then_inc(std_ready, 1)
            act.wait_ge(w_loaded, 16 * NW)
            act.wait_ge(init_ready, 1)
            act.sem_inc(vtok_ready.sem, PA)
            act.sem_inc(raw_out.sem, 32)
            for s in stored:
                act.sem_inc(s.sem, 64)

            def body(u, par, i):
                def take(key):
                    n = PIDX[key]
                    ring_full.wait(act, u, n + 1)
                    return ring[:, n % PBANKS, :]

                for k in range(2):
                    o = take(("xT", k))
                    nc.scalar.copy(xnt[:, k, :], o).then_inc(xnt_ready.sem, 1)
                for m in range(4):
                    o = take(("val", m))
                    nc.scalar.copy(vraw[:, par, m, KCONV - 1:], o).then_inc(vraw_ready.sem, 1)
                o = take(("par",))
                raw_out.wait(act, u, 32)
                nc.scalar.copy(rawp[:], o[0:2 * H, :]).then_inc(raw_ready.sem, 1)
                stored[par].wait(act, i, 64)
                for a in range(PA):
                    o = take(("gate", a))
                    nc.scalar.activation(sg[:, par, a, :], o, ACT.Silu).then_inc(sg_ready.sem, 1)
                for m in range(4):
                    conv_ready.wait(act, u, m + 1)
                    nc.scalar.activation(valt[:, par, m, :], cv[:, m, :], ACT.Silu).then_inc(valt_ready.sem, 1)
                for a in range(PA):
                    o = take(("vt", a))
                    nc.scalar.copy(vtok[:, par, a, :], o).then_inc(vtok_ready.sem, 1)

            passes(act, body)

        @block.vector
        def _(dve):
            V = nc.vector
            V.memset(epsln[:], EPS_LN)
            V.memset(vraw[:, :, :, 0:KCONV - 1], 0.0).then_inc(init_ready, 1)
            dve.wait_ge(x_in, 16)
            for n in range(NT):
                ins = V.bn_stats(bst[:, n, :], xt[:, n, :])
            ins.then_inc(step, 1)
            dve.wait_ge(step, 1)
            for n in range(NT):
                ins = V.bn_aggr(mv[:, n, :], bst[:, n, :])
            ins.then_inc(stats_ready, 1)
            dve.wait_ge(std_ready, 1)
            V.reciprocal(rstd[:], std[:]).then_inc(step, 1)
            dve.wait_ge(step, 2)
            dve.wait_ge(w_loaded, 16 * NW)
            dve.wait_ge(init_ready, 1)

            def body(u, par, i):
                dve.sem_clear(step)
                chain = [0]

                def link(ins):
                    chain[0] += 1
                    ins.then_inc(step, 1)
                    dve.wait_ge(step, chain[0])

                for a in range(PA):
                    n = bass.ds(u * PA + a, 1)
                    ins = V.tensor_scalar(xn[:, par, a, :], xt[:, n, :].rearrange("p a m -> p (a m)"),
                                          mv[:, n, 0:1].rearrange("p a m -> p (a m)"), rstd[:, n],
                                          ALU.subtract, ALU.mult)
                ins.then_inc(xn_ready.sem, 1)
                for k in range(4):
                    vraw_ready.wait(dve, u, k + 1)
                    if par == 1:
                        link(V.tensor_copy(vraw[:, 1, k, 0:KCONV - 1], vraw[:, 0, k, PT:PT + KCONV - 1]))
                    link(V.tensor_scalar(cv[:, k, :], vraw[:, par, k, 3:], convw[:, k, 3:4], convb[:, k:k + 1],
                                         ALU.mult, ALU.add))
                    for q in range(3):
                        ins = V.scalar_tensor_tensor(cv[:, k, :], vraw[:, par, k, q:q + PT], convw[:, k, q:q + 1],
                                                     cv[:, k, :], ALU.mult, ALU.add)
                        if q == 2:
                            ins.then_inc(conv_ready.sem, 1)
                        else:
                            link(ins)

            passes(dve, body)


def parameters(nc, d, st):
    with ExitStack() as ctx:
        def sb(name, shape):
            return ctx.enter_context(nc.sbuf_tensor("q_" + name, shape, F32))

        def sem(name):
            return ctx.enter_context(nc.semaphore("q_" + name))

        NC = T // L
        ident = sb("ident", [P, P])
        dtb = sb("dtb", [P, 1])
        raw = sb("raw", [P, 2, T])
        yv = sb("yv", [P, T])
        ones = sb("ones", [P, T])
        q4 = sb("q4", [P, 4, T])
        qb = sb("qb", [P, NC, L + 1])
        qx = sb("qx", [P, NC])
        qd = sb("qd", [P, 3, T])
        pts = sb("pts", [P, B, UPB, 3, TT, H])
        tp = ctx.enter_context(nc.psum_tensor("qp_t", [P, 6, 4, P], F32))

        loaded = sem("loaded")
        act_ready = sem("act_ready")
        q_ready = sem("q_ready")
        t_full = sem("t_full")
        pts_ready = sem("pts_ready")
        stored = sem("stored")
        step = sem("step")
        block = ctx.enter_context(nc.Block())

        @block.sync
        def _(sp):
            sp.dma_start(ident[:], d["ident"]).then_inc(loaded, 16)
            sp.dma_start(dtb[:], d["dt_bias_b"]).then_inc(loaded, 16)
            for q in range(2):
                sp.dma_start(raw[:, q, :], st["raw"][q].rearrange("b h t -> (b h) t")).then_inc(loaded, 16)
            sp.wait_ge(q_ready, 1)
            for b in range(B):
                r = slice(b * H, (b + 1) * H)
                us = slice(b * UPB, (b + 1) * UPB)
                for q in range(4):
                    sp.dma_start(st["q4"][us, q].rearrange("c h t -> h c t"),
                                 q4[r, q].rearrange("h (c t) -> h c t", c=UPB)).then_inc(stored, 16)
                sp.dma_start(st["qend"][us].rearrange("u h c -> h u c"),
                             qx[r].rearrange("h (u c) -> h u c", u=UPB)).then_inc(stored, 16)
            sp.wait_ge(pts_ready, 6)
            sp.dma_start(st["ptok"].rearrange("(b c) p q a h -> p (b c) (q a h)", b=B),
                         pts[:].rearrange("p b c q a h -> p (b c) (q a h)")).then_inc(stored, 16)
            sp.wait_ge(stored, 16 * (5 * B + 1))

        @block.tensor
        def _(pe):
            pe.wait_ge(loaded, 64)
            pe.wait_ge(q_ready, 1)
            for q in range(3):
                for n in range(8):
                    mm = pe.transpose(tp[:, 2 * q + n // 4, n % 4, :], qd[:, q, n * P:(n + 1) * P], ident[:])
                    if n % 4 == 3:
                        mm.then_inc(t_full, 1)

        @block.scalar
        def _(act):
            act.wait_ge(loaded, 64)
            nc.scalar.activation(raw[:, 0, :], raw[:, 0, :], ACT.Exp, bias=dtb[:, 0:1]).then_inc(act_ready, 1)
            nc.scalar.activation(raw[:, 1, :], raw[:, 1, :], ACT.Tanh, scale=0.5).then_inc(act_ready, 1)
            for q in range(3):
                for half in range(2):
                    act.wait_ge(t_full, 2 * q + half + 1)
                    for a in range(TT):
                        ins = nc.scalar.copy(
                            pts[:, :, 2 * half:2 * half + 2, q, a, :],
                            tp[:, 2 * q + half, a::TT, :].rearrange("p c (b h) -> p b c h", b=B))
                    ins.then_inc(pts_ready, 1)

        @block.vector
        def _(dve):
            V = nc.vector
            chain = [0]

            def link(ins):
                chain[0] += 1
                ins.then_inc(step, 1)
                dve.wait_ge(step, chain[0])

            V.memset(qb[:], 1.0)
            link(V.memset(ones[:], 1.0))
            ey, th, dt = raw[:, 0, :], raw[:, 1, :], qd[:, 2, :]
            dve.wait_ge(act_ready, 2)
            link(V.tensor_scalar(ey, ey, Y_MAX, None, ALU.min))
            link(V.tensor_scalar(yv[:], ey, 1.0 / 7, None, ALU.mult))
            for cst in (-1.0 / 6, 1.0 / 5, -1.0 / 4, 1.0 / 3, -1.0 / 2, 1.0):
                link(V.scalar_tensor_tensor(yv[:], yv[:], cst, ey, ALU.add, ALU.mult))
            link(V.tensor_scalar(dt, yv[:], DT_MIN, DT_MAX, ALU.max, ALU.min))
            link(V.tensor_scalar(th, th, 0.25, 0.25, ALU.mult, ALU.add))
            link(V.tensor_tensor(yv[:], dt, th, ALU.mult))
            link(V.tensor_scalar(q4[:, 2, :], yv[:], 1.0, None, ALU.add))
            V.tensor_tensor(q4[:, 3, :], dt, dt, ALU.mult)
            for c in range(NC):
                ins = V.tensor_tensor_scan(qb[:, c, 1:], q4[:, 2, c * L:(c + 1) * L], ones[:, 0:L], 1.0,
                                           ALU.mult, ALU.mult)
            link(ins)
            cview = "p (c t) -> p c t"
            V.tensor_copy(qx[:], qb[:, :, L])
            V.tensor_copy(qd[:, 0, :].rearrange(cview, c=NC), qb[:, :, 0:L])
            link(V.tensor_copy(qd[:, 1, :].rearrange(cview, c=NC), qb[:, :, 1:]))
            link(V.reciprocal(yv[:], qd[:, 1, :]))
            link(V.tensor_tensor(q4[:, 0, :], dt, qd[:, 0, :], ALU.mult))
            V.tensor_tensor(q4[:, 1, :], dt, yv[:], ALU.mult).then_inc(q_ready, 1)


def ring_tiles():
    tiles = [("bcB", g) for g in range(G)]
    for s in range(G + 2):
        if s < G:
            tiles += [("FB", s), ("w", s)]
        if s >= 2:
            tiles.append(("BT", s - 2))
    tiles.append(("bcC", 0))
    for s in range(1, G + 1):
        tiles.append(("FC", s - 1))
        if s < G:
            tiles.append(("bcC", s))
    tiles += [("yT", 0), ("yT", 1)]
    return tiles


RING = ring_tiles()
RIDX = {k: i for i, k in enumerate(RING)}
assert len(RING) % 2 == 0
GA = 6


def mixer(nc, d, st, wbc, x, x1):
    with ExitStack() as ctx:
        def sb(name, shape, dt=F32):
            return ctx.enter_context(nc.sbuf_tensor(name, shape, dt))

        def ps(name, shape):
            return ctx.enter_context(nc.psum_tensor(name, shape, F32))

        def sem(name):
            return ctx.enter_context(nc.semaphore(name))

        ident = sb("ident", [P, P])
        sel4 = sb("sel4", [P, J])
        blockd = sb("blockd", [P, J * DH])
        seld = sb("seld", [64, G, P])
        causal = sb("causal", [P, L])
        resetm = sb("resetm", [P, 2 * UT])
        contm = sb("contm", [P, NU])
        wout = sb("wout", [P, 4, DM])
        arow = sb("arow", [2 * H, N])
        nega = sb("nega", [P, G])
        skipb = sb("skipb", [P, DI])
        hst = sb("hst", [P, CH + 1, 2, G, DH])
        cmask = sb("cmask", [P, 1])
        coef = sb("coef", [P, L, 2, LANES])
        wrow = sb("wrow", [H, 2, UT])
        dr = sb("dr", [2 * H, UT])
        qend = sb("qend", [H, CH])
        valt = sb("valt", [P, 4, UT])
        vtok = sb("vtok", [P, TT, DI])
        sg = sb("sg", [P, TT, DI])
        ptok = sb("ptok", [P, 3, TT, H])
        x1s = sb("x1s", [P, TT, DM])
        phi = sb("phi", [P, L + 1, 2, 2, LANES])
        pinv = sb("pinv", [P, G, UT])
        qe = sb("qe", [P, LANES])
        em = sb("em", [P, 2, 2, LANES])
        pend = sb("pend", [P, 2, LANES])
        du = sb("du", [P, TT, DI])
        bt = sb("bt", [P, G, 2, UT])
        bcs = sb("bcs", [P, 2, 2, UT])
        sq = sb("sq", [P, 2, UT])
        fbs = sb("fbs", [P, 2, UT])
        m2 = sb("m2", [P, 2, UT])
        ct = sb("ct", [P, 3, 2, UT])
        km = sb("km", [P, 2, J, TT, L])
        hbd = sb("hbd", [P, 2, CH, 2, J * DH])
        uu = sb("uu", [P, 2, 2, LANES])
        nr = sb("nr", [P, G, TT, 2, J])
        nre = sb("nre", [P, G, TT, 2, J])
        rn = sb("rn", [P, G, TT, 2, J])
        fc4 = sb("fc4", [P, G, TT, J])
        dus = sb("dus", [P, TT, G, J])
        fct = sb("fct", [P, 2, TT, J, N])
        ysc = sb("ysc", [P, 2, TT, J * DH])
        ysk = sb("ysk", [P, TT, J * DH])

        def over(mem, at, shape, names):
            n = int(np.prod(shape))
            return mem[:, at:at + n].rearrange(f"p ({names}) -> p {names}", **dict(zip(names.split(), shape)))

        bcs_flat = bcs[:].rearrange("p i v t -> p (i v t)")
        hbd_flat = hbd[:].rearrange("p i c v e -> p (i c v e)")
        m1 = ct[:, 0]
        btt = over(bcs_flat, 0, (2, 2, TT, P), "i v a m")
        ygt = over(bcs_flat, 0, (TT, 4, P), "a k t")
        gs = over(km[:].rearrange("p i j a t -> p (i j a t)"), 0, (CH, 2, G, DH), "c v g e")
        hu = over(hbd_flat, 0, (2, 2, G, DH), "r v g e")
        ht = over(hbd_flat, 4 * G * DH, (2, G, DH), "v g e")

        ring = ps("ring", [P, 2, 512])
        ssp_bank = ps("ssp", [P, 512])
        yp_bank = ps("yp", [P, 512])
        ssp = ssp_bank[:, 0:G * TT * 2 * J].rearrange("p (g a v j) -> p g a v j", g=G, a=TT, v=2)
        yp = yp_bank[:, 0:TT * J * DH].rearrange("p (a e) -> p a e", a=TT)
        kp = ps("kp", [P, 4, 512])

        w_loaded = sem("w_loaded")
        NW = 11
        exps_ready = sem("exps_ready")
        init_ready = sem("init_ready")
        first_full = sem("first_full")
        wrow_in = Signal(sem("wrow_in"), 16)
        dr_in = Signal(sem("dr_in"), 32)
        valt_in = Signal(sem("valt_in"), 16)
        vtok_in = Signal(sem("vtok_in"), 16)
        ptok_in = Signal(sem("ptok_in"), 16)
        sg_in = Signal(sem("sg_in"), 16)
        x_in = Signal(sem("x_in"), 16)
        x_out = Signal(sem("x_out"), 16)
        ring_full = Signal(sem("ring_full"), len(RING))
        d_full = Signal(sem("d_full"), G)
        g_full = Signal(sem("g_full"), 2 * G)
        coef_ready = Signal(sem("coef_ready"), G)
        ln_ready = Signal(sem("ln_ready"), G)
        scan_ready = Signal(sem("scan_ready"), G // 2)
        pinv_ready = Signal(sem("pinv_ready"), 1)
        evolved = Signal(sem("evolved"), 1)
        em_ready = Signal(sem("em_ready"), 1)
        bcs_ready = Signal(sem("bcs_ready"), 2 * G)
        sq_ready = Signal(sem("sq_ready"), 2 * G)
        ss_ready = Signal(sem("ss_ready"), 2 * G)
        nr_ready = Signal(sem("nr_ready"), 2 + G)
        fct_ready = Signal(sem("fct_ready"), 2 * G)
        fbs_ready = Signal(sem("fbs_ready"), 2 * G)
        bt_ready = Signal(sem("bt_ready"), G)
        du_ready = Signal(sem("du_ready"), 2)
        btt_ready = Signal(sem("btt_ready"), G)
        gs_ready = Signal(sem("gs_ready"), 2 * G)
        h_ready = Signal(sem("h_ready"), 4 * CH + 1)
        hbd_ready = Signal(sem("hbd_ready"), G)
        ct_ready = Signal(sem("ct_ready"), G)
        k_ready = Signal(sem("k_ready"), G)
        km_ready = Signal(sem("km_ready"), G)
        y_ready = Signal(sem("y_ready"), G)
        ysc_ready = Signal(sem("ysc_ready"), G)
        yg_ready = Signal(sem("yg_ready"), 3 * G)
        ygt_ready = Signal(sem("ygt_ready"), TT)
        o_ready = Signal(sem("o_ready"), TT)
        x1_ready = Signal(sem("x1_ready"), 1)
        step = sem("dve_step")

        emptied = {("yT", a): (ygt_ready, a + 1) for a in range(TT)}
        for g in range(G):
            emptied |= {("w", g): (coef_ready, G + g + 1),
                        ("bcB", g): (sq_ready, g + 1), ("bcC", g): (bcs_ready, G + g + 1),
                        ("FB", g): (fbs_ready, g + 1), ("FC", g): (fbs_ready, G + g + 1),
                        ("BT", g): (btt_ready, g + 1)}

        def tokens(v):
            return v.rearrange("(u a p) m -> u p a m", a=TT, p=P)

        def lead(v, k):
            return v.unsqueeze(1).broadcast_to([v.shape[0], k, *v.shape[1:]])

        def spread(v, k):
            n = len(v.shape)
            return v.unsqueeze(n).broadcast_to([*v.shape, k])

        block = ctx.enter_context(nc.Block())

        @block.sync
        def _(sp):
            def load_wrow(u):
                sp.dma_start(wrow[:], st["q4"][u][0:2].rearrange("q h t -> h q t")).then_inc(wrow_in.sem, 16)

            def load_dr(u):
                sp.dma_start(dr[:], st["q4"][u][2:4].rearrange("q h t -> (q h) t")).then_inc(dr_in.sem, 16)
                sp.dma_start(qend[:], st["qend"][u]).then_inc(dr_in.sem, 16)

            def load_valt(u):
                sp.dma_start(valt[:], st["valt"][u]).then_inc(valt_in.sem, 16)

            def load_ptok(u):
                sp.dma_start(ptok[:], st["ptok"][u]).then_inc(ptok_in.sem, 16)

            def load_vtok(u):
                sp.dma_start(vtok[:], tokens(st["vtok"])[u]).then_inc(vtok_in.sem, 16)

            def load_sg(u):
                sp.dma_start(sg[:], tokens(st["sg"])[u]).then_inc(sg_in.sem, 16)

            def load_x(u):
                sp.dma_start(x1s[:], tokens(x)[u]).then_inc(x_in.sem, 16)

            def store(u):
                x1_ready.wait(sp, u, 2)
                sp.dma_start(tokens(x1)[u], x1s[:]).then_inc(x_out.sem, 16)

            for dst, src in (
                    (seld[:], d["selh"]), (nega[:], d["A_states"]), (arow[H:2 * H, :], d["A_log"])):
                sp.dma_start(dst, src).then_inc(w_loaded, 16)
            load_wrow(0)
            load_valt(0)
            for dst, src in (
                    (ident[:], d["ident"]), (sel4[:], d["sel4"]), (blockd[:], d["blockd"]),
                    (causal[:], d["causal"]), (resetm[:], d["resetm"]), (contm[:], d["contm"]),
                    (wout[:], d["W_out"].rearrange("(k p) o -> p k o", p=P))):
                sp.dma_start(dst, src).then_inc(w_loaded, 16)
            sp.dma_start(skipb[:], d["skip"].partition_broadcast(P)).then_inc(w_loaded, 16)
            load_ptok(0)
            load_vtok(0)
            load_dr(0)
            load_sg(0)
            load_x(0)
            with sp.Fori(0, NU - 1) as u:
                coef_ready.wait(sp, u, G)
                load_wrow(u + 1)
                d_full.wait(sp, u, G)
                load_dr(u + 1)
                ring_full.wait(sp, u, RIDX[("bcC", G - 1)] + 1)
                load_valt(u + 1)
                fct_ready.wait(sp, u, 2 * G)
                load_ptok(u + 1)
                yg_ready.wait(sp, u, 3 * G)
                load_vtok(u + 1)
                ring_full.wait(sp, u, RIDX[("yT", TT - 1)] + 1)
                load_sg(u + 1)
                store(u)
                x_out.wait(sp, u, 16)
                load_x(u + 1)
            sp.wait_ge(coef_ready.sem, NU * G)
            load_wrow(0)
            sp.wait_ge(x1_ready.sem, NU + 1)
            sp.dma_start(tokens(x1)[NU - 1], x1s[:]).then_inc(x_out.sem, 16)
            sp.wait_ge(x_out.sem, 16 * NU)

        @block.tensor
        def _(pe):
            def spread_coefs(o, g):
                for q in range(2):
                    mm = pe.matmul(o[:, q * UT:(q + 1) * UT], seld[0:H, g, :], wrow[:, q, :], start=True, stop=True)
                return mm

            pe.wait_ge(w_loaded, 16 * NW)
            pe.wait_ge(init_ready, 2)
            pe.wait_ge(wrow_in.sem, 16)
            for g in range(G):
                if g >= 2:
                    pe.wait_ge(coef_ready.sem, g - 1)
                spread_coefs(ring[:, g % 2, :], g).then_inc(first_full, 1)
            pe.wait_ge(coef_ready.sem, G)
            with pe.Fori(0, NU) as u:
                def put(key):
                    i = RIDX[key]
                    if i >= 2:
                        sig, k = emptied[RING[i - 2]]
                        sig.wait(pe, u, k)
                    return ring[:, i % 2, :]

                def full(ins):
                    ins.then_inc(ring_full.sem, 1)

                def bc(name, g, first):
                    o = put((name, g))
                    for v in range(2):
                        for k in range(4):
                            mm = pe.matmul(o[:, v * UT:(v + 1) * UT], wbc[:, k, g, first + v, :], valt[:, k, :],
                                           start=(k == 0), stop=(k == 3))
                    full(mm)

                def sums(n, g):
                    sq_ready.wait(pe, u, n + 1)
                    if n == GA:
                        nr_ready.wait(pe, u, 1)
                    if n >= G:
                        nr_ready.wait(pe, u, n - G + 2)
                    for a in range(TT):
                        for v in range(2):
                            mm = pe.matmul(ssp[:, g, a, v, :], sq[:, v, a * P:(a + 1) * P], sel4[:],
                                           start=True, stop=True)
                    mm.then_inc(ss_ready.sem, 1)

                def factors(name, n, g):
                    fct_ready.wait(pe, u, n + 1)
                    o = put((name, g))
                    for a in range(TT):
                        mm = pe.transpose(o[:, a * P:(a + 1) * P], fct[:, g % 2, a].rearrange("p j n -> p (j n)"), ident[:])
                    full(mm)

                def decays(g):
                    if g == 0:
                        dr_in.wait(pe, u, 32)
                        x1_ready.wait(pe, u, 1)
                    if g >= 4:
                        ln_ready.wait(pe, u, g - 3)
                    mm = pe.matmul(kp[:, g % 4, 0:UT], seld[:, g, :], dr[:], start=True, stop=True)
                    if g == 0:
                        for q in range(G):
                            mm = pe.matmul(kp[:, 0, UT + q * CH:UT + (q + 1) * CH], seld[0:H, q, :], qend[:],
                                           start=True, stop=True)
                    mm.then_inc(d_full.sem, 1)

                valt_in.wait(pe, u, 16)
                for s in range(G + 1):
                    if s < G:
                        bc("bcB", s, 0)
                        decays(s)
                    if s >= 1:
                        sums(s - 1, s - 1)
                for s in range(G + 3):
                    if s < G:
                        factors("FB", s, s)
                        if s == 0:
                            wrow_in.wait(pe, u, 32)
                        full(spread_coefs(put(("w", s)), s))
                    if 2 <= s <= G + 1:
                        g = s - 2
                        bt_ready.wait(pe, u, g + 1)
                        o = put(("BT", g))
                        for v in range(2):
                            for a in range(TT):
                                c0 = (v * TT + a) * P
                                mm = pe.transpose(o[:, c0:c0 + P], bt[:, g, v, a * P:(a + 1) * P], ident[:])
                        full(mm)
                    if s >= 3:
                        g = s - 3
                        btt_ready.wait(pe, u, g + 1)
                        if g == 0:
                            du_ready.wait(pe, u, 2)
                            ln_ready.wait(pe, u, G)
                        if g >= 2:
                            gs_ready.wait(pe, u, 2 * g - 2)
                        for odd in range(2):
                            r = slice(L * odd, L * odd + L)
                            for a in range(TT):
                                for v in range(2):
                                    c0 = (a * 2 + v) * J * DH
                                    mm = pe.matmul(kp[:, 2 * (g % 2) + odd, c0:c0 + J * DH], btt[r, g % 2, v, a, :],
                                                   du[r, a, g * J * DH:(g + 1) * J * DH], start=True, stop=True)
                            mm.then_inc(g_full.sem, 1)
                    if s == G + 1:
                        bc("bcC", 0, 2)
                sums(G, 0)

                def causal_products(g):
                    ct_ready.wait(pe, u, g + 1)
                    if g > 0:
                        km_ready.wait(pe, u, g)
                    else:
                        gs_ready.wait(pe, u, 2 * G)
                    for c in range(CH):
                        r0 = L * (c % 2)
                        for v in range(2):
                            for j in range(J):
                                mm = pe.matmul(kp[r0:r0 + L, j, (c // 2) * L:(c // 2 + 1) * L],
                                               bt[N * j:N * j + N, g, v, c * L:(c + 1) * L],
                                               ct[N * j:N * j + N, g % 3, v, c * L:(c + 1) * L],
                                               start=(v == 0), stop=(v == 1), skip_group_check=True)
                    mm.then_inc(k_ready.sem, 1)

                def outputs(g):
                    km_ready.wait(pe, u, g + 1)
                    hbd_ready.wait(pe, u, g + 1)
                    if g > 0:
                        ysc_ready.wait(pe, u, g)
                    for c in range(CH):
                        r0 = L * (c % 2)
                        o = yp[r0:r0 + L, c // 2, :]
                        for v in range(2):
                            pe.matmul(o, ct[:, g % 3, v, c * L:(c + 1) * L], hbd[:, g % 2, c, v, :],
                                      start=(v == 0), stop=False, skip_group_check=True)
                        for j in range(J):
                            q0 = (g * J + j) * DH
                            mm = pe.matmul(o[:, j * DH:(j + 1) * DH], km[r0:r0 + L, g % 2, j, c // 2, :],
                                           du[r0:r0 + L, c // 2, q0:q0 + DH],
                                           start=False, stop=(j == J - 1), skip_group_check=True)
                    mm.then_inc(y_ready.sem, 1)

                for s in range(1, G + 3):
                    if s <= G:
                        factors("FC", G + s - 1, s - 1)
                    if s < G:
                        bc("bcC", s, 2)
                    if 2 <= s <= G + 1:
                        causal_products(s - 2)
                    if s < G:
                        sums(G + s, s)
                    if s >= 3:
                        outputs(s - 3)
                yg_ready.wait(pe, u, 3 * G)
                for a in range(TT):
                    o = put(("yT", a))
                    for k in range(4):
                        mm = pe.transpose(o[:, k * P:(k + 1) * P], sg[:, a, k * P:(k + 1) * P], ident[:])
                    full(mm)
                x_in.wait(pe, u, 16)
                for a in range(TT):
                    pe.matmul(kp[:, a, 0:DM], ident[:], x1s[:, a, :], start=True, stop=False)
                    ygt_ready.wait(pe, u, a + 1)
                    for k in range(4):
                        mm = pe.matmul(kp[:, a, 0:DM], ygt[:, a, k, :], wout[:, k, :], start=False, stop=(k == 3))
                    mm.then_inc(o_ready.sem, 1)

        @block.scalar
        def _(act):
            act.wait_ge(w_loaded, 16 * NW)
            nc.scalar.activation(nega[:], nega[:], ACT.Exp).then_inc(exps_ready, 1)
            nc.scalar.activation(arow[H:2 * H, :], arow[H:2 * H, :], ACT.Exp).then_inc(exps_ready, 1)
            act.wait_ge(init_ready, 2)

            def coefs(o, g):
                for q in range(2):
                    src = o[:, q * UT:(q + 1) * UT].rearrange("p (c t) -> p c t", c=CH)
                    dst = coef[:, :, q, g * CH:(g + 1) * CH].rearrange("p t c -> p c t")
                    if q == 0:
                        nc.scalar.activation(dst, src, ACT.Copy, scale=nega[:, g:g + 1])
                    else:
                        nc.scalar.copy(dst, src).then_inc(coef_ready.sem, 1)

            act.sem_inc(x1_ready.sem, 1)
            for g in range(G):
                act.wait_ge(first_full, g + 1)
                coefs(ring[:, g % 2, :], g)
            with act.Fori(0, NU) as u:
                def take(key):
                    i = RIDX[key]
                    ring_full.wait(act, u, i + 1)
                    return ring[:, i % 2, :]

                def factors(name, n, g):
                    o = take((name, g))
                    if n >= 2:
                        (bt_ready if n - 2 < G else ct_ready).wait(act, u, (n - 2) % G + 1)
                    nc.scalar.copy(fbs[:, g % 2, :], o[:, 0:UT]).then_inc(fbs_ready.sem, 1)

                for g in range(G):
                    o = take(("bcB", g)).rearrange("p (v t) -> p v t", v=2)
                    nc.scalar.copy(bt[:, g], o).then_inc(bcs_ready.sem, 1)
                    if g >= 1:
                        ss_ready.wait(act, u, g)
                    nc.scalar.activation(sq[:], o, ACT.Square).then_inc(sq_ready.sem, 1)
                    d_full.wait(act, u, g + 1)
                    if g == 0:
                        nc.scalar.copy(qe[:], kp[:, 0, UT:UT + LANES])
                    nc.scalar.activation(pinv[:, g, :], kp[:, g % 4, 0:UT], ACT.Ln).then_inc(ln_ready.sem, 1)
                    if g == GA:
                        ss_ready.wait(act, u, GA)
                        nc.scalar.activation(nr[:, 0:GA], ssp[:, 0:GA], ACT.Sqrt).then_inc(nr_ready.sem, 1)
                ss_ready.wait(act, u, G)
                nc.scalar.activation(nr[:, GA:], ssp[:, GA:], ACT.Sqrt).then_inc(nr_ready.sem, 1)

                def output_products(g):
                    o = take(("bcC", g)).rearrange("p (v t) -> p v t", v=2)
                    if g >= 1:
                        ss_ready.wait(act, u, G + g)
                    nc.scalar.activation(sq[:], o, ACT.Square).then_inc(sq_ready.sem, 1)
                    if g >= 2:
                        ct_ready.wait(act, u, g - 1)
                    if g == 0:
                        g_full.wait(act, u, 2 * G - 2)
                    nc.scalar.copy(bcs[:, g % 2, :, :], o).then_inc(bcs_ready.sem, 1)

                def output_norms(g):
                    ss_ready.wait(act, u, G + g + 1)
                    if g == 0:
                        fct_ready.wait(act, u, G)
                    nc.scalar.activation(nr[:, g], ssp[:, g], ACT.Sqrt).then_inc(nr_ready.sem, 1)

                for s in range(G + 3):
                    if s < G:
                        factors("FB", s, s)
                        coefs(take(("w", s)), s)
                    if 2 <= s <= G + 1:
                        g = s - 2
                        o = take(("BT", g))
                        if g >= 2:
                            g_full.wait(act, u, 2 * g - 2)
                        nc.scalar.copy(btt[:, g % 2], o.rearrange("p (v a m) -> p v a m", v=2, a=TT)) \
                            .then_inc(btt_ready.sem, 1)
                    if s >= 3:
                        g = s - 3
                        for odd in range(2):
                            g_full.wait(act, u, 2 * g + odd + 1)
                            for j in range(J):
                                r = slice(N * j, N * j + N)
                                src = kp[r, 2 * (g % 2) + odd, 0:TT * 2 * J * DH].rearrange(
                                    "p (a v e) -> p a v e", a=TT, v=2)
                                ins = nc.scalar.copy(gs[r, odd::2, :, g, :], src[:, :, :, DH * j:DH * (j + 1)])
                            ins.then_inc(gs_ready.sem, 1)
                    if s == G:
                        scan_ready.wait(act, u, G // 2)
                        nc.scalar.activation(pinv[:], pinv[:], ACT.Exp, scale=-1.0).then_inc(pinv_ready.sem, 1)
                    if s == G + 1:
                        output_products(0)
                output_norms(0)
                for s in range(1, G + 1):
                    factors("FC", G + s - 1, s - 1)
                    if s < G:
                        output_products(s)
                        output_norms(s)
                for a in range(TT):
                    o = take(("yT", a))
                    if a == 0:
                        ct_ready.wait(act, u, G)
                    nc.scalar.copy(ygt[:, a], o.rearrange("p (k t) -> p k t", k=4)).then_inc(ygt_ready.sem, 1)
                o_ready.wait(act, u, TT)
                nc.scalar.copy(x1s[:], kp[:, 0:TT, 0:DM]).then_inc(x1_ready.sem, 1)

        @block.gpsimd
        def _(pool):
            nc.gpsimd.memset(hst[:, CH], 0.0).then_inc(init_ready, 1)
            with pool.Fori(0, NU) as u:
                em_ready.wait(pool, u, 1)
                nc.gpsimd.tensor_tensor(hst[:, 0].rearrange("p v g e -> p (v g e)"),
                                        hst[:, CH].rearrange("p v g e -> p (v g e)"),
                                        cmask[:].broadcast_to([P, 2 * G * DH]), ALU.mult).then_inc(h_ready.sem, 1)
                n = 1
                h_ready.wait(pool, u, n)
                gs_ready.wait(pool, u, 2 * G)
                for c in range(CH):
                    nc.gpsimd.tensor_tensor(ht[:], hst[:, c], gs[:, c], ALU.add).then_inc(h_ready.sem, 1)
                    n += 1
                    h_ready.wait(pool, u, n)
                    for r in range(2):
                        nc.gpsimd.tensor_tensor(
                            hu[:, r], ht[:], spread(em[:, r].rearrange("p k (g c) -> p k g c", g=G)[:, :, :, c], DH),
                            ALU.mult).then_inc(h_ready.sem, 1)
                        n += 1
                    h_ready.wait(pool, u, n)
                    nc.gpsimd.tensor_tensor(hst[:, c + 1], hu[:, :, 0], hu[:, :, 1], ALU.add).then_inc(h_ready.sem, 1)
                    n += 1
                    h_ready.wait(pool, u, n)
                assert n == h_ready.per
                vtok_in.wait(pool, u, 16)
                sg_in.wait(pool, u, 16)

                def expand(g):
                    if g >= 2:
                        y_ready.wait(pool, u, g - 1)
                    hv = hst[:, 0:CH, :, g, :].rearrange("p c v e -> p (c v) e")
                    nc.gpsimd.tensor_tensor(
                        hbd[:, g % 2].rearrange("p c v (j e) -> p (c v) j e", j=J),
                        hv.unsqueeze(2).broadcast_to([P, CH * 2, J, DH]),
                        blockd[:].rearrange("p (j e) -> p j e", j=J).unsqueeze(1).broadcast_to([P, CH * 2, J, DH]),
                        ALU.mult).then_inc(hbd_ready.sem, 1)

                def gated(g):
                    cs = slice(g * J * DH, (g + 1) * J * DH)
                    nc.gpsimd.tensor_tensor(ysk[:], vtok[:, :, cs], lead(skipb[:, cs], TT), ALU.mult) \
                        .then_inc(yg_ready.sem, 1)
                    ysc_ready.wait(pool, u, g + 1)
                    yg_ready.wait(pool, u, 3 * g + 1)
                    nc.gpsimd.tensor_tensor(ysk[:], ysk[:], ysc[:, g % 2], ALU.add).then_inc(yg_ready.sem, 1)
                    yg_ready.wait(pool, u, 3 * g + 2)
                    nc.gpsimd.tensor_tensor(sg[:, :, cs], ysk[:], sg[:, :, cs], ALU.mult).then_inc(yg_ready.sem, 1)
                    yg_ready.wait(pool, u, 3 * g + 3)

                expand(0)
                expand(1)
                for g in range(G):
                    gated(g)
                    if g + 2 < G:
                        expand(g + 2)

        @block.vector
        def _(dve):
            chain = [0]

            def link(ins):
                chain[0] += 1
                ins.then_inc(step, 1)
                dve.wait_ge(step, chain[0])

            V = nc.vector
            for row in range(2):
                for col in range(2):
                    V.memset(phi[:, 0, row, col, :], 1.0 if row == col else 0.0)
            dve.wait_ge(w_loaded, 16 * NW)
            dve.wait_ge(exps_ready, 2)
            for g in range(G):
                sg_ = seld[32:64, g, :].rearrange("p (j n) -> p j n", j=J)
                V.tensor_tensor(sg_, sg_, lead(arow[H:2 * H, :], J), ALU.mult)
            V.tensor_scalar(nega[:], nega[:], -1.0, None, ALU.mult).then_inc(init_ready, 1)
            dve.wait_ge(init_ready, 2)
            with dve.Fori(0, NU) as u:
                dve.sem_clear(step)
                chain[0] = 0
                V.tensor_copy(cmask[:], contm[:, bass.ds(u, 1)])
                coef_ready.wait(dve, u, G)
                HL = LANES // 2

                def turn(ins):
                    chain[0] += 1
                    ins.then_inc(step, 1)
                    if chain[0] > 1:
                        dve.wait_ge(step, chain[0] - 1)

                for t in range(L):
                    for h in range(2):
                        hl = slice(h * HL, (h + 1) * HL)
                        cf = coef[:, t, :, hl].unsqueeze(2).broadcast_to([P, 2, 2, HL])
                        turn(V.tensor_tensor(uu[:, :, :, hl], phi[:, t, ::-1, :, hl], cf, ALU.mult))
                    for h in range(2):
                        hl = slice(h * HL, (h + 1) * HL)
                        ins = V.tensor_tensor(phi[:, t + 1, :, :, hl], phi[:, t, :, :, hl], uu[:, :, :, hl], ALU.add)
                        if t < L - 1 or h == 0:
                            turn(ins)
                ins.then_inc(evolved.sem, 1)
                evolved.wait(dve, u, 1)
                dve.wait_ge(step, chain[0])
                def rows(row, t0, g):
                    return phi[:, t0:t0 + L, row, :, g * CH:(g + 1) * CH].rearrange("p t k c -> p k c t")

                def cols(v):
                    return lead(v.rearrange("p (c t) -> p c t", c=CH), 2)

                def both(v):
                    return v.rearrange("p k (c t) -> p k c t", c=CH)

                ptok_in.wait(dve, u, 16)

                def input_norms(part, g0, g1):
                    gr, k = slice(g0, g1), g1 - g0
                    nr_ready.wait(dve, u, part + 1)
                    link(V.tensor_scalar(nre[:, gr], nr[:, gr], EPS_BC, None, ALU.add))
                    link(V.reciprocal(rn[:, gr], nre[:, gr]))
                    link(V.tensor_tensor(fc4[:, gr], nre[:, gr, :, 1], rn[:, gr, :, 0], ALU.mult))
                    link(V.tensor_tensor(dus[:, :, gr],
                                         ptok[:, 2, :, g0 * J:g1 * J].rearrange("p a (g j) -> p a g j", g=k),
                                         rn[:, gr, :, 1].rearrange("p g a j -> p a g j"), ALU.mult))
                    if part == 0:
                        input_factors(0)
                        input_factors(1)
                        vtok_in.wait(dve, u, 16)
                    hs, cs = slice(g0 * J, g1 * J), slice(g0 * J * DH, g1 * J * DH)
                    V.tensor_tensor(du[:, :, cs].rearrange("p a (h e) -> p a h e", h=J * k),
                                    vtok[:, :, cs].rearrange("p a (h e) -> p a h e", h=J * k),
                                    spread(dus[:].rearrange("p a g j -> p a (g j)")[:, :, hs], DH), ALU.mult) \
                        .then_inc(du_ready.sem, 1)

                def input_factors(g):
                    hs = slice(J * g, J * g + J)
                    if g >= 2:
                        fbs_ready.wait(dve, u, g - 1)
                    V.tensor_tensor(fct[:, g % 2], spread(fc4[:, g], N), spread(ptok[:, 0, :, hs], N), ALU.mult) \
                        .then_inc(fct_ready.sem, 1)

                def input_side(g):
                    bcs_ready.wait(dve, u, g + 1)
                    fbs_ready.wait(dve, u, g + 1)
                    link(V.tensor_tensor(fbs[:, g % 2, :], bt[:, g, 0, :], fbs[:, g % 2, :], ALU.mult))
                    V.tensor_tensor(both(m1), rows(1, 0, g), cols(fbs[:, g % 2, :]), ALU.mult)
                    link(V.tensor_tensor(both(m2), rows(0, 1, g), cols(bt[:, g, 1, :]), ALU.mult))
                    V.tensor_tensor(bt[:, g, 0, :], m1[:, 1, :], m2[:, 1, :], ALU.subtract)
                    V.tensor_tensor(bt[:, g, 1, :], m2[:, 0, :], m1[:, 0, :], ALU.subtract).then_inc(bt_ready.sem, 1)
                    bt_ready.wait(dve, u, g + 1)

                input_norms(0, 0, GA)
                for s in range(1, G + 1):
                    input_side(s - 1)
                    if s + 1 < G:
                        input_factors(s + 1)
                    if s == 1:
                        input_norms(1, GA, G)
                    if s <= G // 2:
                        i = s - 1
                        ln_ready.wait(dve, u, 2 * i + 2)
                        pi = pinv[:, 2 * i:2 * i + 2, :].rearrange("p g t -> p (g t)")
                        V.tensor_tensor_scan(pi, resetm[:], pi, 0.0, ALU.mult, ALU.add).then_inc(scan_ready.sem, 1)
                pinv_ready.wait(dve, u, 1)
                pe_ = pinv[:].rearrange("p g (c t) -> p (g c) t", c=CH)[:, :, L - 1]
                link(V.tensor_copy(pend[:, 0], pe_))
                link(V.tensor_tensor(pend[:, 1], pend[:, 0], qe[:], ALU.mult))
                V.tensor_tensor(em[:, 0], phi[:, L, 0], lead(pend[:, 0], 2), ALU.mult)
                V.tensor_tensor(em[:, 1], phi[:, L, 1], lead(pend[:, 1], 2), ALU.mult).then_inc(em_ready.sem, 1)

                def output_factors(g):
                    nr_ready.wait(dve, u, g + 3)
                    link(V.tensor_scalar(nre[:, g], nr[:, g], EPS_BC, None, ALU.add))
                    link(V.reciprocal(rn[:, g], nre[:, g]))
                    hs = slice(J * g, J * g + J)
                    link(V.tensor_tensor(fc4[:, g], nre[:, g, :, 0], rn[:, g, :, 1], ALU.mult))
                    if g >= 2:
                        fbs_ready.wait(dve, u, G + g - 1)
                    V.tensor_tensor(fct[:, g % 2], spread(fc4[:, g], N), spread(ptok[:, 1, :, hs], N), ALU.mult) \
                        .then_inc(fct_ready.sem, 1)

                def output_side(g):
                    bcs_ready.wait(dve, u, G + g + 1)
                    fbs_ready.wait(dve, u, G + g + 1)
                    V.tensor_tensor(bcs[:, g % 2, 0, :], bcs[:, g % 2, 0, :], pinv[:, g, :], ALU.mult)
                    link(V.tensor_tensor(fbs[:, g % 2, :], pinv[:, g, :], fbs[:, g % 2, :], ALU.mult))
                    link(V.tensor_tensor(bcs[:, g % 2, 1, :], bcs[:, g % 2, 1, :], fbs[:, g % 2, :], ALU.mult))
                    if g >= 3:
                        y_ready.wait(dve, u, g - 2)
                    V.tensor_tensor(both(ct[:, g % 3]), rows(0, 1, g), cols(bcs[:, g % 2, 0, :]), ALU.mult)
                    link(V.tensor_tensor(both(m2), rows(1, 1, g), cols(bcs[:, g % 2, 1, :]), ALU.mult))
                    V.tensor_tensor(ct[:, g % 3], ct[:, g % 3], m2[:], ALU.add).then_inc(ct_ready.sem, 1)
                    ct_ready.wait(dve, u, g + 1)

                def mask(g):
                    k_ready.wait(dve, u, g + 1)
                    if g == 0:
                        h_ready.wait(dve, u, h_ready.per)
                    if g >= 2:
                        y_ready.wait(dve, u, g - 1)
                    V.tensor_tensor(km[:, g % 2], kp[:, :, 0:TT * L].rearrange("p j (a t) -> p j a t", a=TT),
                                    lead(causal[:], TT).unsqueeze(1).broadcast_to([P, J, TT, L]), ALU.mult) \
                        .then_inc(km_ready.sem, 1)

                def scale_out(g):
                    y_ready.wait(dve, u, g + 1)
                    if g >= 2:
                        yg_ready.wait(dve, u, 3 * (g - 1))
                    V.tensor_tensor(ysc[:, g % 2].rearrange("p a (j e) -> p a j e", j=J),
                                    yp[:].rearrange("p a (j e) -> p a j e", j=J), spread(rn[:, g, :, 0], DH),
                                    ALU.mult).then_inc(ysc_ready.sem, 1)

                for s in range(G + 3):
                    if 1 <= s <= G:
                        output_side(s - 1)
                    if 2 <= s <= G + 1:
                        mask(s - 2)
                    if s < G:
                        output_factors(s)
                    if s >= 3:
                        scale_out(s - 3)


def attention(nc, d, x, x1):
    st = {k: nc.dram_tensor(k + "_scratch", shape, dt).ap() for k, shape, dt in (
        ("raw", (2, B, H, T), F32), ("sg", (NTOK, DI), F32), ("vtok", (NTOK, DI), F32),
        ("valt", (NU, P, 4, UT), F32),
        ("q4", (NU, 4, H, UT), F32), ("qend", (NU, H, CH), F32), ("ptok", (NU, P, 3, TT, H), F32))}
    with nc.sbuf_tensor("wbc", [P, 4, G, 4, P], F32) as wbc:
        projections(nc, d, x, st, wbc)
        parameters(nc, d, st)
        mixer(nc, d, st, wbc, x, x1)


SK, DC = 77, 192
DQ = DM // 16
XT = T // P


def cross_ring():
    tiles = [("kT",), ("v",)] + [("xT", i) for i in range(XT // 2)]
    tiles += [("qT", m, i) for m in range(2) for i in range(T // 512)]
    for s in range(XT + 3):
        if 1 <= s <= XT:
            tiles.append(("O", s - 1))
        if 2 <= s <= XT + 1:
            tiles.append(("oT", s - 2))
        if s >= 3:
            tiles.append(("out", s - 3))
    return tiles


XRING = cross_ring()
XIDX = {k: i for i, k in enumerate(XRING)}
assert len(XRING) % 2 == 0


def cross_attention(nc, d, x1, xres):
    with ExitStack() as ctx:
        def sb(name, shape):
            return ctx.enter_context(nc.sbuf_tensor("x_" + name, shape, F32))

        def ps(name, shape):
            return ctx.enter_context(nc.psum_tensor("xp_" + name, shape, F32))

        def sem(name):
            return ctx.enter_context(nc.semaphore("x_" + name))

        ident = sb("ident", [P, P])
        parity = sb("parity", [P, 2])
        ones = sb("ones", [1, P])
        wq = sb("wq", [P, 2, DM])
        wo = sb("wo", [P, 2, DM])
        wka = sb("wka", [P, DM])
        wkb = sb("wkb", [DC - P, DM])
        wva = sb("wva", [P, DM])
        wvb = sb("wvb", [DC - P, DM])
        bq = sb("bq", [P, 2])
        bk = sb("bk", [P, 2])
        bv = sb("bv", [1, DM])
        bo = sb("bo", [1, DM])
        ca = sb("ca", [P, SK])
        cb = sb("cb", [DC - P, SK])
        kraw = sb("kraw", [P, 2, SK])
        kz = sb("kz", [P, 2, 2, SK])
        va = sb("va", [SK, 16, DQ + 1])
        epsln = sb("epsln", [P, 1])
        bst = sb("bst", [P, XT, 6])
        mv = sb("mv", [P, XT, 2])
        std = sb("std", [P, XT])
        rstd = sb("rstd", [P, XT])
        xn = sb("xn", [P, XT, DM])
        xnt = sb("xnt", [P, 2, T])
        qt = sb("qt", [P, 2, T])
        mx = sb("mx", [P, 2, 4, 4])
        s_sb = sb("s", [P, 2, 16, SK])
        pt = sb("pt", [SK, 2, 16, P])
        rec = sb("rec", [P, 16])
        osb = sb("o", [P, 2, DM])
        ot = sb("ot", [P, 2, 2, P])

        ring = ps("ring", [P, 2, 512])
        sp_ = ps("scores", [P, 4, 512])
        ptp = ps("pt", [P, 2, 512])

        w_loaded = sem("w_loaded")
        NW = 13
        eps_ready = sem("eps_ready")
        x_in = Signal(sem("x_in"), 16)
        c_in = Signal(sem("c_in"), 32)
        ring_full = Signal(sem("ring_full"), len(XRING))
        mv_ready = Signal(sem("mv_ready"), 1)
        std_ready = Signal(sem("std_ready"), 1)
        bst_ready = sem("bst_ready")
        rstd_ready = Signal(sem("rstd_ready"), 1)
        xn_ready = Signal(sem("xn_ready"), XT)
        xnt_ready = Signal(sem("xnt_ready"), XT // 2)
        kraw_ready = Signal(sem("kraw_ready"), 2)
        kz_ready = Signal(sem("kz_ready"), 2)
        va_ready = Signal(sem("va_ready"), 1)
        qt_ready = Signal(sem("qt_ready"), 4)
        s_full = Signal(sem("s_full"), XT)
        mx_ready = Signal(sem("mx_ready"), XT)
        s_ready = Signal(sem("s_ready"), XT)
        pt_full = Signal(sem("pt_full"), 4 * XT)
        pt_ready = Signal(sem("pt_ready"), 4 * XT)
        rec_ready = Signal(sem("rec_ready"), XT)
        o_ready = Signal(sem("o_ready"), XT)
        ot_ready = Signal(sem("ot_ready"), XT)
        x2_ready = Signal(sem("x2_ready"), XT)
        kv_taken = Signal(sem("kv_taken"), 1)

        emptied = {("kT",): (kraw_ready, 2), ("v",): (va_ready, 1)}
        emptied |= {("xT", i): (xnt_ready, i + 1) for i in range(XT // 2)}
        emptied |= {("qT", m, i): (qt_ready, 2 * m + i + 1) for m in range(2) for i in range(2)}
        for i in range(XT):
            emptied |= {("O", i): (o_ready, i + 1), ("oT", i): (ot_ready, i + 1), ("out", i): (x2_ready, i + 1)}

        x1v = x1.rearrange("(n p) m -> p n m", p=P)
        block = ctx.enter_context(nc.Block())

        @block.sync
        def _(sp):
            for dst, src in (
                    (ident[:], d["ident"]), (parity[:], d["parity"]), (ones[:], d["onesrow"]),
                    (wq[:], d["wq"].rearrange("(k p) o -> p k o", p=P)),
                    (wo[:], d["wo"].rearrange("(k p) o -> p k o", p=P)),
                    (wka[:], d["wk"][0:P]), (wkb[:], d["wk"][P:DC]), (wva[:], d["wv"][0:P]), (wvb[:], d["wv"][P:DC]),
                    (bq[:], d["bq"]), (bk[:], d["bk"]), (bv[:], d["bv"]), (bo[:], d["bo"])):
                sp.dma_start(dst, src).then_inc(w_loaded, 16)
            sp.sem_inc(kv_taken.sem, 1)
            with sp.Fori(0, B) as b:
                kv_taken.wait(sp, b, 1)
                sp.dma_start(xres[:, bass.ds(b * XT, XT), :], x1v[:, bass.ds(b * XT, XT), :]).then_inc(x_in.sem, 16)
                sp.dma_start(ca[:], d["ctxT"][bass.ds(b, 1), 0:P].rearrange("a p s -> p (a s)")).then_inc(c_in.sem, 16)
                sp.dma_start(cb[:], d["ctxT"][bass.ds(b, 1), P:DC].rearrange("a p s -> p (a s)")) \
                    .then_inc(c_in.sem, 16)

        @block.tensor
        def _(pe):
            pe.wait_ge(w_loaded, 16 * NW)
            pe.wait_ge(eps_ready, 2)
            with pe.Fori(0, B) as b:
                def put(key):
                    i = XIDX[key]
                    if i >= 2:
                        sig, k = emptied[XRING[i - 2]]
                        sig.wait(pe, b, k)
                    return ring[:, i % 2, :]

                c_in.wait(pe, b, 32)
                o = put(("kT",))
                for m in range(2):
                    for k, (w, c) in enumerate(((wka, ca), (wkb, cb))):
                        mm = pe.matmul(o[:, m * SK:(m + 1) * SK], w[:, m * P:(m + 1) * P], c[:],
                                       start=(k == 0), stop=(k == 1))
                mm.then_inc(ring_full.sem, 1)
                o = put(("v",))
                pe.matmul(o[0:SK, 0:DM], ca[:], wva[:], start=True, stop=False)
                pe.matmul(o[0:SK, 0:DM], cb[:], wvb[:], start=False, stop=False)
                pe.matmul(o[0:SK, 0:DM], ones[:, 0:SK], bv[:], start=False, stop=True).then_inc(ring_full.sem, 1)
                for i in range(XT // 2):
                    xn_ready.wait(pe, b, 2 * i + 2)
                    o = put(("xT", i))
                    for k in range(2):
                        for a in range(2):
                            mm = pe.transpose(o[:, (2 * k + a) * P:(2 * k + a + 1) * P],
                                              xn[:, 2 * i + a, k * P:(k + 1) * P], ident[:])
                    mm.then_inc(ring_full.sem, 1)
                for m in range(2):
                    for i in range(2):
                        xnt_ready.wait(pe, b, 2 * i + 2)
                        o = put(("qT", m, i))
                        for k in range(2):
                            mm = pe.matmul(o, wq[:, k, m * P:(m + 1) * P], xnt[:, k, 512 * i:512 * (i + 1)],
                                           start=(k == 0), stop=(k == 1))
                        mm.then_inc(ring_full.sem, 1)
                qt_ready.wait(pe, b, 4)
                kz_ready.wait(pe, b, 2)
                va_ready.wait(pe, b, 1)
                for s in range(XT + 3):
                    if s < XT:
                        if s > 0:
                            s_ready.wait(pe, b, s)
                        for q in range(4):
                            for r in range(4):
                                m, par = q // 2, q % 2
                                rr = slice(32 * r, 32 * r + 32)
                                mm = pe.matmul(sp_[:, r, q * SK:(q + 1) * SK], qt[rr, m, s * P:(s + 1) * P],
                                               kz[rr, m, par, :], start=True, stop=True)
                        mm.then_inc(s_full.sem, 1)
                    if 1 <= s <= XT:
                        i = s - 1
                        s_ready.wait(pe, b, i + 1)
                        for q in range(4):
                            n = 4 * i + q
                            if q >= 2:
                                pt_ready.wait(pe, b, n - 1)
                            for h in range(4):
                                mm = pe.transpose(ptp[0:SK, q % 2, h * P:(h + 1) * P], s_sb[:, i % 2, 4 * q + h, :],
                                                  ident[:])
                            mm.then_inc(pt_full.sem, 1)
                        o = put(("O", i))
                        for q in range(4):
                            pt_ready.wait(pe, b, 4 * i + q + 1)
                            for h in range(4 * q, 4 * q + 4):
                                mm = pe.matmul(o[:, h * (DQ + 1):(h + 1) * (DQ + 1)], pt[:, i % 2, h, :], va[:, h, :],
                                               start=True, stop=True)
                        mm.then_inc(ring_full.sem, 1)
                    if 2 <= s <= XT + 1:
                        i = s - 2
                        o_ready.wait(pe, b, i + 1)
                        o = put(("oT", i))
                        for k in range(2):
                            mm = pe.transpose(o[:, k * P:(k + 1) * P], osb[:, i % 2, k * P:(k + 1) * P], ident[:])
                        mm.then_inc(ring_full.sem, 1)
                    if s >= 3:
                        i = s - 3
                        ot_ready.wait(pe, b, i + 1)
                        o = put(("out", i))
                        for k in range(2):
                            pe.matmul(o[:, 0:DM], ot[:, i % 2, k, :], wo[:, k, :], start=(k == 0), stop=False)
                        pe.matmul(o[:, 0:DM], ones[:], bo[:], start=False, stop=True).then_inc(ring_full.sem, 1)
                x2_ready.wait(pe, b, XT)

        @block.scalar
        def _(act):
            act.wait_ge(w_loaded, 16 * NW)
            act.wait_ge(eps_ready, 2)
            with act.Fori(0, B) as b:
                def take(key):
                    i = XIDX[key]
                    ring_full.wait(act, b, i + 1)
                    return ring[:, i % 2, :]

                o = take(("kT",))
                for m in range(2):
                    nc.scalar.activation(kraw[:, m, :], o[:, m * SK:(m + 1) * SK], ACT.Identity,
                                         bias=bk[:, m:m + 1]).then_inc(kraw_ready.sem, 1)
                o = take(("v",))
                nc.scalar.copy(va[:, :, 0:DQ], o[0:SK, 0:DM].rearrange("p (h e) -> p h e", h=16)) \
                    .then_inc(va_ready.sem, 1)
                mv_ready.wait(act, b, 1)
                nc.scalar.activation(std[:], mv[:, :, 1], ACT.Sqrt, bias=epsln[:, 0:1]).then_inc(std_ready.sem, 1)
                for i in range(XT // 2):
                    o = take(("xT", i))
                    nc.scalar.copy(xnt[:, :, 256 * i:256 * (i + 1)], o.rearrange("p (k t) -> p k t", k=2)) \
                        .then_inc(xnt_ready.sem, 1)
                for m in range(2):
                    for i in range(2):
                        o = take(("qT", m, i))
                        nc.scalar.activation(qt[:, m, 512 * i:512 * (i + 1)], o, ACT.Identity, bias=bq[:, m:m + 1]) \
                            .then_inc(qt_ready.sem, 1)
                for s in range(XT + 2):
                    if 1 <= s <= XT:
                        i = s - 1
                        for q in range(4):
                            pt_full.wait(act, b, 4 * i + q + 1)
                            if q == 0 and i >= 2:
                                ring_full.wait(act, b, XIDX[("O", i - 2)] + 1)
                            nc.scalar.activation(pt[:, i % 2, 4 * q:4 * q + 4, :],
                                                 ptp[0:SK, q % 2, :].rearrange("p (h t) -> p h t", h=4),
                                                 ACT.Exp, scale=DQ ** -0.5).then_inc(pt_ready.sem, 1)
                    if s >= 2:
                        i = s - 2
                        o = take(("oT", i))
                        nc.scalar.copy(ot[:, i % 2], o[:, 0:2 * P].rearrange("p (k t) -> p k t", k=2)) \
                            .then_inc(ot_ready.sem, 1)

        @block.vector
        def _(dve):
            V = nc.vector
            V.memset(epsln[:], EPS_LN).then_inc(eps_ready, 1)
            V.memset(va[:], 1.0).then_inc(eps_ready, 1)
            dve.wait_ge(w_loaded, 16 * NW)
            with dve.Fori(0, B) as b:
                dve.sem_clear(bst_ready)
                x_in.wait(dve, b, 16)
                for i in range(XT):
                    ins = V.bn_stats(bst[:, i, :], xres[:, bass.ds(b * XT + i, 1), :].rearrange("p a m -> p (a m)"))
                ins.then_inc(bst_ready, 1)
                dve.wait_ge(bst_ready, 1)
                for i in range(XT):
                    ins = V.bn_aggr(mv[:, i, :], bst[:, i, :])
                ins.then_inc(mv_ready.sem, 1)
                std_ready.wait(dve, b, 1)
                V.reciprocal(rstd[:], std[:]).then_inc(rstd_ready.sem, 1)
                rstd_ready.wait(dve, b, 1)
                for i in range(XT):
                    V.tensor_scalar(xn[:, i, :], xres[:, bass.ds(b * XT + i, 1), :].rearrange("p a m -> p (a m)"),
                                    mv[:, i, 0:1], rstd[:, i:i + 1], ALU.subtract, ALU.mult).then_inc(xn_ready.sem, 1)
                kraw_ready.wait(dve, b, 2)
                for par in range(2):
                    V.tensor_scalar(kz[:, :, par, :], kraw[:], parity[:, par:par + 1], None, ALU.mult) \
                        .then_inc(kz_ready.sem, 1)
                for s in range(XT + 3):
                    if s < XT:
                        s_full.wait(dve, b, s + 1)
                        sc = sp_[:, :, 0:4 * SK].rearrange("p r (q k) -> p r q k", q=4)
                        V.tensor_reduce(mx[:, s % 2], sc, AX.X, ALU.max).then_inc(mx_ready.sem, 1)
                        mx_ready.wait(dve, b, s + 1)
                        V.tensor_tensor(s_sb[:, s % 2].rearrange("p (r q) k -> p r q k", r=4), sc,
                                        mx[:, s % 2].unsqueeze(3).broadcast_to([P, 4, 4, SK]), ALU.subtract) \
                            .then_inc(s_ready.sem, 1)
                    if 1 <= s <= XT:
                        i = s - 1
                        ring_full.wait(dve, b, XIDX[("O", i)] + 1)
                        o = ring[:, XIDX[("O", i)] % 2, 0:16 * (DQ + 1)].rearrange("p (h e) -> p h e", h=16)
                        V.reciprocal(rec[:], o[:, :, DQ]).then_inc(rec_ready.sem, 1)
                        rec_ready.wait(dve, b, i + 1)
                        V.tensor_tensor(osb[:, i % 2].rearrange("p (h e) -> p h e", h=16), o[:, :, 0:DQ],
                                        rec[:].unsqueeze(2).broadcast_to([P, 16, DQ]), ALU.mult) \
                            .then_inc(o_ready.sem, 1)
                    if s >= 3:
                        i = s - 3
                        ring_full.wait(dve, b, XIDX[("out", i)] + 1)
                        xr = xres[:, bass.ds(b * XT + i, 1), :].rearrange("p a m -> p (a m)")
                        V.tensor_tensor(xr, ring[:, XIDX[("out", i)] % 2, 0:DM], xr, ALU.add).then_inc(x2_ready.sem, 1)

        @block.gpsimd
        def _(pool):
            with pool.Fori(0, B) as b:
                ring_full.wait(pool, b, 2)
                pool.sem_inc(kv_taken.sem, 1)


NE, TOPK, FF = 15, 3, 512
RT = 256
NRT = (TOPK * NTOK + NE * (RT - 1)) // RT
NROW = (NRT + 2) * RT
XP = 24


def experts(nc, d, xres, out):
    with ExitStack() as ctx:
        def sb(name, shape, dt=F32):
            return ctx.enter_context(nc.sbuf_tensor("f_" + name, shape, dt))

        def ps(name, shape):
            return ctx.enter_context(nc.psum_tensor("fp_" + name, shape, F32))

        def sem(name):
            return ctx.enter_context(nc.semaphore("f_" + name))

        xg = nc.dram_tensor("xg_scratch", (NROW, DM), F32).ap()
        yg = nc.dram_tensor("yg_scratch", (NRT * RT, DM), F32).ap()

        NB = NTOK // 512
        ident = sb("ident", [P, P])
        ones = sb("ones", [1, P])
        before = sb("before", [P, P])
        allones = sb("allones", [P, P])
        thr = sb("thr", [P, NTOK // RT])
        tids = sb("tids", [1, NRT + 2])
        gw = sb("gw", [P, 2, NE])
        gb = sb("gb", [1, NE])
        b1 = sb("b1", [P, 2, 4])
        b2 = sb("b2", [NE + 1, DM])
        w1 = sb("w1", [P, 2, 2, FF])
        w2 = sb("w2", [P, 2, 4, DM])
        epsln = sb("epsln", [P, 1])
        zeros = sb("zeros", [P, NROW * DM // P // 8])
        bst = sb("bst", [P, NT, 6])
        mv = sb("mv", [P, NT, 2])
        std = sb("std", [P, NT])
        rstd = sb("rstd", [P, NT])
        xn = sb("xn", [P, NT, DM])
        xnt = sb("xnt", [P, 2, NTOK])
        lg = sb("lg", [P, NT, NE])
        mx = sb("mx", [P, NT])
        sm = sb("sm", [P, NT])
        pr = sb("pr", [P, NT, XP])
        top = sb("top", [P, NT, 8])
        rest = sb("rest", [P, NT, XP])
        mask = sb("mask", [P, NT, NE])
        gate = sb("gate", [P, NT, NE + 1])
        gt = sb("gt", [NE + 1, 2, P])
        off = sb("off", [P, NT + 1, NE])
        cmp_ = sb("cmp", [P, NE, NTOK // RT])
        incl = sb("incl", [P, NE + 1])
        ntl = sb("ntl", [P, NE])
        first = sb("first", [P, NE])
        sv = sb("sv", [P, NT, NE])
        s8 = sb("s8", [P, NT, 8])
        rowid = sb("rowid", [P, NT, TOPK], I32)
        eq = sb("eq", [P, NT, NE])
        gk = sb("gk", [P, TOPK, NT])
        tcmp = sb("tcmp", [1, NRT + 2, NE])
        tef = sb("tef", [1, NRT + 2])
        te = sb("te", [1, NRT + 2], I32)
        hT = sb("hT", [P, 2, 4, 512])
        xr = sb("xr", [P, 2, 2, DM])
        xrt = sb("xrt", [P, 2, 2, RT])
        yr = sb("yr", [P, 2, 2, DM])
        hp = ps("h", [P, 4, 512])
        yp = ps("y", [P, 4, 512])

        w_loaded = sem("w_loaded")
        NW = 9
        mv_ready = sem("mv_ready")
        std_ready = sem("std_ready")
        zeros_ready = sem("zeros_ready")
        zeroed = sem("zeroed")
        xn_ready = sem("xn_ready")
        xt_full = sem("xt_full")
        xnt_ready = sem("xnt_ready")
        lg_full = sem("lg_full")
        lg_ready = sem("lg_ready")
        cent_ready = sem("cent_ready")
        prob_ready = sem("prob_ready")
        step = sem("step")
        gate_ready = sem("gate_ready")
        cum_full = sem("cum_full")
        cum_used = sem("cum_used")
        te_ready = sem("te_ready")
        rowid_ready = sem("rowid_ready")
        scattered = sem("scattered")
        gt_full = sem("gt_full")
        gt_ready = sem("gt_ready")
        acc_ready = sem("acc_ready")
        b2_full = sem("b2_full")
        w_in = [sem(f"w_in{i}") for i in range(2)]
        h_full = sem("h_full")
        h_ready = sem("h_ready")
        y_full = sem("y_full")
        y_used = sem("y_used")
        xr_in = [sem(f"xr_in{i}") for i in range(2)]
        xrt_full = sem("xrt_full")
        xrt_ready = sem("xrt_ready")
        hr_full = sem("hr_full")
        hr_ready = sem("hr_ready")
        yr_full = sem("yr_full")
        yr_ready = sem("yr_ready")
        yr_out = [sem(f"yr_out{i}") for i in range(2)]
        gathered = [sem(f"gathered{c}") for c in range(8)]
        combined = sem("combined")
        stored = sem("stored")

        outv = out.rearrange("(n p) m -> p n m", p=P)
        xgv = xg.rearrange("(t a p) m -> t p a m", a=2, p=P)
        ygv = yg.rearrange("(t a p) m -> t p a m", a=2, p=P)
        zv = xg.rearrange("(q p a) m -> q p (a m)", q=8, p=P)
        block = ctx.enter_context(nc.Block())

        @block.sync
        def _(sp):
            for dst, src in ((ident[:], d["ident"]), (ones[:], d["onesrow"]), (before[:], d["before"]),
                             (allones[:], d["allones"]), (thr[:], d["thr"]), (tids[:], d["tids"]),
                             (gw[:], d["gW"].rearrange("(k p) e -> p k e", p=P)), (gb[:], d["gb"]),
                             (b2[:], d["b2"])):
                sp.dma_start(dst, src).then_inc(w_loaded, 16)

            def load(e, par):
                sp.dma_start(w1[:, par], d["W1"][bass.ds(e, 1)].rearrange("a (k p) f -> p (a k) f", p=P)) \
                    .then_inc(w_in[par], 16)
                sp.dma_start(w2[:, par], d["W2"][bass.ds(e, 1)].rearrange("a (k p) f -> p (a k) f", p=P)) \
                    .then_inc(w_in[par], 16)
                sp.dma_start(b1[:, par], d["b1"][bass.ds(e, 1)].rearrange("a p f -> p (a f)")).then_inc(w_in[par], 16)

            load(NE, 0)
            load(NE + 1, 1)
            sp.wait_ge(zeros_ready, 1)
            for q in range(8):
                sp.dma_start(zv[q], zeros[:]).then_inc(zeroed, 16)

            def load_weights(t, par):
                load(sp.value_load(te[0:1, bass.ds(t, 1)], min_val=0, max_val=NE - 1), par)

            def load_rows(t, par):
                sp.dma_start(xr[:, par], xgv[t]).then_inc(xr_in[par], 16)

            sp.wait_ge(te_ready, 1)
            sp.wait_ge(scattered, 16 * NT * TOPK)
            for par in range(2):
                load_rows(par, par)
            for par in range(2):
                sp.wait_ge(y_full, (par + 1) * 2 * NB + 4)
                load_weights(par, par)
            with sp.Fori(0, NRT // 2) as i:
                for par in range(2):
                    t = 2 * i + par
                    sp.wait_ge(xrt_full, t + 1)
                    load_rows(t + 2, par)
                    sp.wait_ge(yr_full, t + 3)
                    load_weights(t + 2, par)
                    sp.wait_ge(yr_ready, t + 3)
                    sp.dma_start(ygv[t], yr[:, par]).then_inc(yr_out[par], 16)
            for c in range(8):
                sp.wait_ge(combined, NT * (TOPK - 1) + 4 * c + 4)
                sp.dma_start(outv[:, 4 * c:4 * c + 4, :], xres[:, 4 * c:4 * c + 4, :]).then_inc(stored, 16)
            sp.wait_ge(stored, 16 * 8)

        @block.gpsimd
        def _(pool):
            pool.wait_ge(zeroed, 16 * 8)
            pool.wait_ge(xn_ready, NT)
            pool.wait_ge(rowid_ready, 1)
            for n in range(NT):
                for k in range(TOPK):
                    pool.indirect_dma_start(xg, bass.IndirectOffsetOnAxis(ap=rowid[:, n, k:k + 1], axis=0),
                                            xn[:, n, :], None).then_inc(scattered, 16)
            pool.wait_ge(scattered, 16 * NT * TOPK)
            for par in range(2):
                pool.wait_ge(yr_out[par], 16 * (NRT // 2) + 16)
            for k in range(TOPK):
                for n in range(NT):
                    if k > 0:
                        pool.wait_ge(combined, (k - 1) * NT + n + 1)
                    pool.indirect_dma_start(xn[:, n, :], None, yg,
                                            bass.IndirectOffsetOnAxis(ap=rowid[:, n, k:k + 1], axis=0)) \
                        .then_inc(gathered[n // 4], 16)

        @block.tensor
        def _(pe):
            pe.wait_ge(w_loaded, 16 * NW)
            for i in range(NT):
                pe.wait_ge(xn_ready, i + 1)
                if i >= 2:
                    pe.wait_ge(xnt_ready, i - 1)
                for k in range(2):
                    mm = pe.transpose(hp[:, i % 2, k * P:(k + 1) * P], xn[:, i, k * P:(k + 1) * P], ident[:])
                mm.then_inc(xt_full, 1)
            for i in range(NT):
                pe.wait_ge(xnt_ready, i + 1)
                o = yp[:, 0, i * NE:(i + 1) * NE]
                for k in range(2):
                    pe.matmul(o, xnt[:, k, i * P:(i + 1) * P], gw[:, k, :], start=(k == 0), stop=False)
                mm = pe.matmul(o, ones[:], gb[:], start=False, stop=True)
            mm.then_inc(lg_full, 1)
            pe.wait_ge(gate_ready, 1)
            pe.wait_ge(lg_ready, 1)
            flat = mask[:].rearrange("p n e -> p (n e)")
            pe.matmul(yp[:, 0, 0:NT * NE], before[:], flat, start=True, stop=True)
            pe.matmul(yp[:, 1, 0:NT * NE], allones[:], flat, start=True, stop=True).then_inc(cum_full, 1)
            for i in range(NT + 1):
                if i < NT:
                    if i >= 2:
                        pe.wait_ge(gt_ready, i - 1)
                    pe.transpose(hp[0:NE + 1, i % 2, 0:P], gate[:, i, :], ident[:]).then_inc(gt_full, 1)
                if i >= 1:
                    pe.wait_ge(gt_ready, i)
                    if i >= 3:
                        pe.wait_ge(acc_ready, i - 2)
                    pe.matmul(yp[:, 2 + (i - 1) % 2, 0:DM], gt[:, (i - 1) % 2, :], b2[:], start=True, stop=True) \
                        .then_inc(b2_full, 1)
            pe.wait_ge(acc_ready, NT)
            pe.wait_ge(cum_used, 1)
            pe.sem_inc(y_full, 4)

            for e in range(2):
                pe.wait_ge(w_in[e], 48)
                with pe.Fori(0, NB // 2) as ib:
                    for q in range(2):
                        nb = 2 * ib + q
                        for f in range(4):
                            pe.wait_ge(h_ready, nb * 4 + (e * NB * 4 + f + 1))
                            for k in range(2):
                                mm = pe.matmul(hp[:, f, :], w1[:, e, k, f * P:(f + 1) * P],
                                               xnt[:, k, bass.ds(nb * 512, 512)], start=(k == 0), stop=(k == 1))
                            mm.then_inc(h_full, 1)
                        pe.wait_ge(h_ready, nb * 4 + (e * NB * 4 + 8))
                        for a in range(4):
                            if a % 2 == 0:
                                pe.wait_ge(y_used, nb * 2 + (e * NB * 2 + a // 2 + 1))
                            for f in range(4):
                                mm = pe.matmul(yp[:, 2 * q + a // 2, (a % 2) * DM:(a % 2 + 1) * DM],
                                               hT[:, q, f, a * P:(a + 1) * P], w2[:, e, f, :],
                                               start=(f == 0), stop=(f == 3))
                            if a % 2 == 1:
                                mm.then_inc(y_full, 1)

            pe.wait_ge(h_ready, 2 * NB * 4 + 4)
            pe.wait_ge(y_used, 2 * NB * 2 + 4)
            pe.sem_inc(yr_full, 2)

            def turn(par):
                for k in range(2):
                    for a in range(2):
                        mm = pe.transpose(yp[:, 2 + par, k * RT + a * P:k * RT + (a + 1) * P],
                                          xr[:, par, a, k * P:(k + 1) * P], ident[:])
                mm.then_inc(xrt_full, 1)

            pe.wait_ge(xr_in[0], 16)
            turn(0)
            with pe.Fori(0, NRT // 2) as i:
                for par in range(2):
                    t = 2 * i + par
                    pe.wait_ge(xrt_ready, t + 1)
                    pe.wait_ge(w_in[par], i * 48 + 96)
                    for f in range(4):
                        pe.wait_ge(hr_ready, t * 4 + f + 1)
                        for k in range(2):
                            mm = pe.matmul(hp[:, f, 0:RT], w1[:, par, k, f * P:(f + 1) * P], xrt[:, par, k, :], start=(k == 0), stop=(k == 1))
                        mm.then_inc(hr_full, 1)
                    pe.wait_ge(xr_in[1 - par], i * 16 + (par * 16 + 16))
                    turn(1 - par)
                    pe.wait_ge(yr_ready, t + 1)
                    pe.wait_ge(hr_ready, t * 4 + 8)
                    for a in range(2):
                        for f in range(4):
                            mm = pe.matmul(yp[:, par, a * DM:(a + 1) * DM], hT[:, par, f, a * P:(a + 1) * P],
                                           w2[:, par, f, :], start=(f == 0), stop=(f == 3))
                    mm.then_inc(yr_full, 1)

        @block.scalar
        def _(act):
            act.wait_ge(mv_ready, 1)
            nc.scalar.activation(std[:], mv[:, :, 1], ACT.Sqrt, bias=epsln[:, 0:1]).then_inc(std_ready, 1)
            act.wait_ge(w_loaded, 16 * NW)
            for i in range(NT):
                act.wait_ge(xt_full, i + 1)
                nc.scalar.copy(xnt[:, :, i * P:(i + 1) * P], hp[:, i % 2, 0:2 * P].rearrange("p (k t) -> p k t", k=2)) \
                    .then_inc(xnt_ready, 1)
            act.wait_ge(lg_full, 1)
            nc.scalar.copy(lg[:], yp[:, 0, 0:NT * NE].rearrange("p (n e) -> p n e", n=NT)).then_inc(lg_ready, 1)
            act.wait_ge(cent_ready, 1)
            nc.scalar.activation(lg[:], lg[:], ACT.Exp).then_inc(prob_ready, 1)
            for i in range(NT):
                act.wait_ge(gt_full, i + 1)
                if i >= 2:
                    act.wait_ge(b2_full, i - 1)
                nc.scalar.copy(gt[:, i % 2, :], hp[0:NE + 1, i % 2, 0:P]).then_inc(gt_ready, 1)
            act.sem_inc(h_ready, 4)
            act.sem_inc(hr_ready, 4)

            for e in range(2):
                with act.Fori(0, NB // 2) as ib:
                    for q in range(2):
                        nb = 2 * ib + q
                        act.wait_ge(y_full, nb * 2 + (e * NB * 2 + 2))
                        for f in range(4):
                            act.wait_ge(h_full, nb * 4 + (e * NB * 4 + f + 1))
                            nc.scalar.activation(hT[:, q, f, :], hp[:, f, :], ACT.Gelu,
                                                 bias=b1[:, e, f:f + 1]).then_inc(h_ready, 1)
            act.wait_ge(y_full, 2 * NB * 2 + 4)

            def turned(par):
                nc.scalar.copy(xrt[:, par], yp[:, 2 + par, :].rearrange("p (k t) -> p k t", k=2)) \
                    .then_inc(xrt_ready, 1)

            act.wait_ge(xrt_full, 1)
            turned(0)
            with act.Fori(0, NRT // 2) as i:
                for par in range(2):
                    t = 2 * i + par
                    act.wait_ge(yr_full, t + 1)
                    for f in range(4):
                        act.wait_ge(hr_full, t * 4 + f + 1)
                        nc.scalar.activation(hT[:, par, f, 0:RT], hp[:, f, 0:RT], ACT.Gelu,
                                             bias=b1[:, par, f:f + 1]).then_inc(hr_ready, 1)
                    act.wait_ge(xrt_full, t + 2)
                    turned(1 - par)

        @block.vector
        def _(dve):
            V = nc.vector
            chain = [0]

            def link(ins):
                chain[0] += 1
                ins.then_inc(step, 1)
                dve.wait_ge(step, chain[0])

            V.memset(zeros[:], 0.0).then_inc(zeros_ready, 1)
            V.memset(pr[:], -1.0)
            V.memset(gate[:], 1.0)
            V.memset(off[:], 0.0)
            V.memset(incl[:], 0.0)
            link(V.memset(epsln[:], EPS_LN))
            for i in range(NT):
                ins = V.bn_stats(bst[:, i, :], xres[:, i, :])
            link(ins)
            for i in range(NT):
                ins = V.bn_aggr(mv[:, i, :], bst[:, i, :])
            ins.then_inc(mv_ready, 1)
            dve.wait_ge(std_ready, 1)
            link(V.reciprocal(rstd[:], std[:]))
            for i in range(NT):
                V.tensor_scalar(xn[:, i, :], xres[:, i, :], mv[:, i, 0:1], rstd[:, i:i + 1],
                                ALU.subtract, ALU.mult).then_inc(xn_ready, 1)
            dve.wait_ge(xn_ready, NT)
            for i in range(0, NT, 4):
                ins = V.tensor_tensor(xres[:, i:i + 4, :], xres[:, i:i + 4, :], xn[:, i:i + 4, :], ALU.add)
            link(ins)
            dve.wait_ge(w_loaded, 16 * NW)
            dve.wait_ge(lg_ready, 1)

            def per(v, k):
                return v.unsqueeze(2).broadcast_to([P, v.shape[1], k])

            def each(v, k):
                return v.unsqueeze(1).broadcast_to([v.shape[0], k, v.shape[1]])

            link(V.tensor_reduce(mx[:], lg[:], AX.X, ALU.max))
            V.tensor_tensor(lg[:], lg[:], per(mx[:], NE), ALU.subtract).then_inc(cent_ready, 1)
            dve.wait_ge(prob_ready, 1)
            link(V.tensor_reduce(sm[:], lg[:], AX.X, ALU.add))
            link(V.reciprocal(sm[:], sm[:]))
            link(V.tensor_tensor(pr[:, :, 0:NE], lg[:], per(sm[:], NE), ALU.mult))
            for i in range(NT):
                ins = V.max(top[:, i, :], pr[:, i, :])
            link(ins)
            link(V.memset(top[:, :, TOPK:8], -1.0))
            for i in range(NT):
                ins = V.match_replace(rest[:, i, :], top[:, i, :], pr[:, i, :], -1.0)
            link(ins)
            link(V.tensor_scalar(mask[:], rest[:, :, 0:NE], 0.0, None, ALU.is_lt))
            V.tensor_tensor(gate[:, :, 0:NE], pr[:, :, 0:NE], mask[:], ALU.mult).then_inc(gate_ready, 1)
            dve.wait_ge(cum_full, 1)
            cum = yp[:, 0, 0:NT * NE].rearrange("p (n e) -> p n e", n=NT)
            tot = yp[:, 1, 0:NT * NE].rearrange("p (n e) -> p n e", n=NT)
            for n in range(NT):
                link(V.tensor_tensor(off[:, n + 1, :], tot[:, n, :], off[:, n, :], ALU.add))
            link(V.tensor_tensor(cmp_[:], per(off[:, NT, :], NTOK // RT), each(thr[:], NE), ALU.is_gt))
            link(V.tensor_reduce(ntl[:], cmp_[:], AX.X, ALU.add))
            for e in range(NE):
                link(V.tensor_tensor(incl[:, e + 1:e + 2], incl[:, e:e + 1], ntl[:, e:e + 1], ALU.add))
            link(V.tensor_tensor(tcmp[:], tids[:].unsqueeze(2).broadcast_to([1, NRT + 2, NE]),
                                 each(incl[0:1, 1:], NRT + 2), ALU.is_ge))
            link(V.tensor_reduce(tef[:], tcmp[:], AX.X, ALU.add))
            V.tensor_scalar(te[:], tef[:], NE - 1.0, None, ALU.min).then_inc(te_ready, 1)
            link(V.tensor_scalar(first[:], incl[:, 0:NE], float(RT), 1.0, ALU.mult, ALU.add))
            V.tensor_tensor(sv[:], cum, off[:, 0:NT, :], ALU.add).then_inc(cum_used, 1)
            dve.wait_ge(cum_used, 1)
            link(V.tensor_tensor(sv[:], sv[:], each(first[:], NT), ALU.add))
            link(V.tensor_tensor(sv[:], sv[:], mask[:], ALU.mult))
            for n in range(NT):
                ins = V.max(s8[:, n, :], sv[:, n, :])
            link(ins)
            V.tensor_scalar(rowid[:], s8[:, :, 0:TOPK], 1.0, None, ALU.subtract).then_inc(rowid_ready, 1)
            for k in range(TOPK):
                link(V.tensor_tensor(eq[:], sv[:], per(s8[:, :, k], NE), ALU.is_equal))
                link(V.tensor_tensor(eq[:], eq[:], gate[:, :, 0:NE], ALU.mult))
                link(V.tensor_reduce(gk[:, k, :], eq[:], AX.X, ALU.add))
            for i in range(NT):
                dve.wait_ge(b2_full, i + 1)
                V.tensor_tensor(xres[:, i, :], yp[:, 2 + i % 2, 0:DM], xres[:, i, :], ALU.add).then_inc(acc_ready, 1)
            dve.wait_ge(acc_ready, NT)
            dve.sem_inc(y_used, 4)

            for e in range(2):
                with dve.Fori(0, NB // 2) as ib:
                    for q in range(2):
                        nb = 2 * ib + q
                        for half in range(2):
                            dve.wait_ge(y_full, nb * 2 + (e * NB * 2 + half + 5))
                            dve.wait_ge(y_used, nb * 2 + (e * NB * 2 + half + 1))
                            xr2 = xres[:, bass.ds(nb * 4 + half * 2, 2), :]
                            V.tensor_tensor(xr2, yp[:, 2 * q + half, :].rearrange("p (a m) -> p a m", a=2),
                                            xr2, ALU.add).then_inc(y_used, 1)
            for s in yr_out:
                dve.sem_inc(s, 16)
            dve.sem_inc(yr_ready, 2)
            with dve.Fori(0, NRT // 2) as i:
                for par in range(2):
                    t = 2 * i + par
                    dve.wait_ge(yr_full, t + 3)
                    dve.wait_ge(yr_out[par], i * 16 + 16)
                    V.tensor_copy(yr[:, par], yp[:, par, :].rearrange("p (a m) -> p a m", a=2)).then_inc(yr_ready, 1)
            dve.wait_ge(y_used, 2 * NB * 2 + 4)
            for k in range(TOPK):
                for n in range(NT):
                    dve.wait_ge(gathered[n // 4], 64 * k + 64)
                    if k > 0:
                        dve.wait_ge(combined, (k - 1) * NT + n + 1)
                    V.scalar_tensor_tensor(xres[:, n, :], xn[:, n, :], gk[:, k, n:n + 1], xres[:, n, :],
                                           ALU.mult, ALU.add).then_inc(combined, 1)


def program(nc, d, out):
    x1 = nc.dram_tensor("x1_scratch", (NTOK, DM), F32).ap()
    attention(nc, d, d["x"].rearrange("b t m -> (b t) m"), x1)
    with nc.sbuf_tensor("xres", [P, NT, DM], F32) as xres:
        cross_attention(nc, d, x1, xres)
        experts(nc, d, xres, out)


def layouts(inputs):
    r = {"x": inputs["x"]}
    w = np.asarray(inputs["L0_attn_W_in"])
    order = np.concatenate([np.arange(2 * DI), 2 * DI + 2 * np.arange(H), 2 * DI + 2 * np.arange(H) + 1])
    r["W_in"] = w[order].T
    w = np.asarray(inputs["L0_attn_W_bc"]).reshape(G, J, 4, N, DI)
    r["W_bc"] = w.transpose(0, 2, 1, 3, 4).reshape(H * 4 * N, DI).T
    r["W_out"] = np.asarray(inputs["L0_attn_W_out"]).T
    r["conv_bias"] = np.asarray(inputs["L0_attn_dw_bias"]).reshape(4, P).T
    r["A_states"] = np.asarray(inputs["L0_attn_A_log"]).reshape(G, J * N).T
    for k in ("dw_weight", "skip", "A_log"):
        r[k] = inputs["L0_attn_" + k]
    r["dt_bias_b"] = np.tile(np.asarray(inputs["L0_attn_dt_bias"]), B)[:, None]
    r["ctxT"] = np.asarray(inputs["ctx_768"]).transpose(0, 2, 1)
    heads = np.array([8 * (q // 2) + 2 * row + q % 2 for row in range(4) for q in range(4)])
    cols = (heads[:, None] * DQ + np.arange(DQ)[None]).reshape(-1)
    for k in ("wq", "wk"):
        r[k] = inputs["L0_xattn_" + k]
    r["wv"] = np.asarray(inputs["L0_xattn_wv"])[:, cols]
    r["bv"] = np.asarray(inputs["L0_xattn_bv"])[cols][None]
    r["wo"] = np.asarray(inputs["L0_xattn_wo"])[cols]
    r["bo"] = np.asarray(inputs["L0_xattn_bo"])[None]
    for k in ("bq", "bk"):
        r[k] = np.asarray(inputs["L0_xattn_" + k]).reshape(2, P).T
    ffn = {k[7:]: np.asarray(v) for k, v in inputs.items() if k.startswith("L0_ffn_")}
    r["gW"], r["gb"] = ffn["gW"], ffn["gb"][None]
    sw1 = ffn["sW1"][0].reshape(DM, 2, FF).transpose(1, 0, 2)
    r["W1"] = np.concatenate([ffn["rW1"], sw1])
    r["W2"] = np.concatenate([ffn["rW2"], ffn["sW2"][0].reshape(2, FF, DM)])
    r["b1"] = np.concatenate([ffn["rb1"], ffn["sb1"][0].reshape(2, FF)]).reshape(NE + 2, 4, P).transpose(0, 2, 1)
    r["b2"] = np.concatenate([ffn["rb2"], ffn["sb2"]])
    r.update(constants())
    return {k: np.ascontiguousarray(v) for k, v in r.items()}


def kernel(**inputs):
    import numpy as _np
    import concourse.bacc as _bacc
    from concourse import mybir as _mybir
    from concourse.bass_utils import run_bass_kernel_spmd as _run

    nc = _bacc.Bacc("TRN2", target_bir_lowering=False, num_devices=1)
    arrays, args = {}, {}
    for name, a in layouts(inputs).items():
        arrays[f"in_{name}_dram"] = a
        args[name] = nc.dram_tensor(f"in_{name}_dram", a.shape, _mybir.dt.from_np(a.dtype), kind="ExternalInput").ap()
    out = nc.dram_tensor("out_0_dram", (B, T, DM), F32, kind="ExternalOutput").ap()
    program(nc, args, out.rearrange("b t m -> (b t) m"))
    r = _run(nc, [arrays], core_ids=[0])
    return r.results[0]["out_0_dram"]
```
